# Optimizing a Trainium2 kernel written in Bass

```python
import numpy as np
import jax
import jax.numpy as jnp

def _softmax(x, axis=-1):
    return jax.nn.softmax(x, axis=axis)

def _gelu(x):
    return jax.nn.gelu(x, approximate=True)

def _silu(x):
    return jax.nn.silu(x)

def _sigmoid(x):
    return jax.nn.sigmoid(x)

def _layernorm(x, axis=-1, eps=1e-05):
    m = jnp.mean(x, axis=axis, keepdims=True)
    v = jnp.var(x, axis=axis, keepdims=True)
    return (x - m) / jnp.sqrt(v + eps)

def _scatter_add(tgt, idx, src, axis=0):
    return tgt.at[idx].add(src)

def _segment_sum(src, seg, n):
    return jax.ops.segment_sum(src, seg, n)
kernel_name = 'mk_hybrid_d1_jaxref_r8_fc5d6f'

def setup_inputs(seed: int=0):
    np.random.seed(seed)
    _w = jnp.asarray

    def _L0_attn_a_setup():
        import jax, jax.numpy as jnp
        import numpy as np
        H, HD, D = (16, 64, 128)
        SCALE = HD ** (-0.5)
        TEMP = 1.0
        EPS = 1e-05
        key = jax.random.key(seed)
        ks = jax.random.split(key, 10)
        B, N = (2, 256)
        lim = 1.0 / np.sqrt(D)

        def lin(k, out_d, in_d):
            k1, k2 = jax.random.split(k)
            W = jax.random.uniform(k1, (out_d, in_d), jnp.float32, -lim, lim)
            b = jax.random.uniform(k2, (out_d,), jnp.float32, -lim, lim)
            return (W, b)
        Wq, bq = lin(ks[0], H * HD, D)
        Wk, bk = lin(ks[1], H * HD, D)
        Wv, bv = lin(ks[2], H * HD, D)
        Wo, bo = lin(ks[3], D, H * HD)
        return {'x': jax.random.normal(ks[4], (B, N, D), jnp.float32), 'adaptive_scale': jnp.ones((H,), jnp.float32), 'Wq': Wq, 'bq': bq, 'Wk': Wk, 'bk': bk, 'Wv': Wv, 'bv': bv, 'Wo': Wo, 'bo': bo, 'gamma': jnp.ones((D,), jnp.float32), 'beta': jnp.zeros((D,), jnp.float32)}
    _L0_attn_a_in = _L0_attn_a_setup()

    def _L0_attn_b_setup():
        import jax, jax.numpy as jnp
        import numpy as np
        INF_APPROX = 1e+30
        ROTARY_BASE = 10000.0
        D_HEAD = 128

        def _rope(x, base=ROTARY_BASE):
            _, length, _, width = x.shape
            half = width // 2
            positions = jnp.arange(length, dtype=x.dtype)
            dims = jnp.arange(half, dtype=x.dtype)
            ang_freqs = jnp.power(base, -dims / half)
            radians = positions[:, None] * ang_freqs[None, :]
            cos = jnp.cos(radians)[None, :, None, :]
            sin = jnp.sin(radians)[None, :, None, :]
            even, odd = jnp.split(x, 2, axis=-1)
            return jnp.concatenate([even * cos - odd * sin, even * sin + odd * cos], axis=-1)
        key = jax.random.key(seed)
        k1, k2, k3, k4, k5 = jax.random.split(key, 5)
        B, T, M, H, D = (2, 512, 128, 8, 128)
        n_layer = 24
        x = jax.random.normal(k1, (B, T, M), dtype=jnp.float32)
        std_qkv = M ** (-0.5)
        std_o = (M * 2 * n_layer) ** (-0.5)
        w_aq = jnp.zeros((M, H, D), dtype=jnp.float32)
        w_ak = std_qkv * jax.random.normal(k3, (M, H, D), dtype=jnp.float32)
        w_av = std_qkv * jax.random.normal(k4, (M, H, D), dtype=jnp.float32)
        w_ao = std_o * jax.random.normal(k5, (H, D, M), dtype=jnp.float32)
        return {'x': x, 'w_aq': w_aq, 'w_ak': w_ak, 'w_av': w_av, 'w_ao': w_ao}
    _L0_attn_b_in = _L0_attn_b_setup()

    def _L0_ffn_setup():
        import jax, jax.numpy as jnp
        import numpy as np
        HIDDEN = 128
        INTER = 512
        key = jax.random.key(seed)
        k1, k2, k3, k4, k5 = jax.random.split(key, 5)
        hidden_states = jax.random.normal(k1, (4, 256, HIDDEN), dtype=jnp.float32)
        W1 = jax.random.normal(k2, (HIDDEN, INTER), dtype=jnp.float32) * (1.0 / np.sqrt(HIDDEN))
        b1 = jax.random.normal(k3, (INTER,), dtype=jnp.float32) * 0.02
        W2 = jax.random.normal(k4, (INTER, HIDDEN), dtype=jnp.float32) * (1.0 / np.sqrt(INTER))
        b2 = jax.random.normal(k5, (HIDDEN,), dtype=jnp.float32) * 0.02
        return {'hidden_states': hidden_states, 'W1': W1, 'b1': b1, 'W2': W2, 'b2': b2}
    _L0_ffn_in = _L0_ffn_setup()
    _d = {'L0_attn_a_x': _L0_attn_a_in['x'], 'L0_attn_a_adaptive_scale': _L0_attn_a_in['adaptive_scale'], 'L0_attn_a_Wq': _L0_attn_a_in['Wq'], 'L0_attn_a_bq': _L0_attn_a_in['bq'], 'L0_attn_a_Wk': _L0_attn_a_in['Wk'], 'L0_attn_a_bk': _L0_attn_a_in['bk'], 'L0_attn_a_Wv': _L0_attn_a_in['Wv'], 'L0_attn_a_bv': _L0_attn_a_in['bv'], 'L0_attn_a_Wo': _L0_attn_a_in['Wo'], 'L0_attn_a_bo': _L0_attn_a_in['bo'], 'L0_attn_a_gamma': _L0_attn_a_in['gamma'], 'L0_attn_a_beta': _L0_attn_a_in['beta'], 'L0_attn_b_w_aq': _L0_attn_b_in['w_aq'], 'L0_attn_b_w_ak': _L0_attn_b_in['w_ak'], 'L0_attn_b_w_av': _L0_attn_b_in['w_av'], 'L0_attn_b_w_ao': _L0_attn_b_in['w_ao'], 'L0_ffn_W1': _L0_ffn_in['W1'], 'L0_ffn_b1': _L0_ffn_in['b1'], 'L0_ffn_W2': _L0_ffn_in['W2'], 'L0_ffn_b2': _L0_ffn_in['b2']}
    _x0 = _d['L0_attn_a_x']
    _d['L0_attn_a_x'] = jax.random.normal(jax.random.fold_in(jax.random.key(seed), 1), (1, 2048, 128), dtype=_x0.dtype)
    del _x0
    return _d

def reference(L0_attn_a_x, L0_attn_a_adaptive_scale, L0_attn_a_Wq, L0_attn_a_bq, L0_attn_a_Wk, L0_attn_a_bk, L0_attn_a_Wv, L0_attn_a_bv, L0_attn_a_Wo, L0_attn_a_bo, L0_attn_a_gamma, L0_attn_a_beta, L0_attn_b_w_aq, L0_attn_b_w_ak, L0_attn_b_w_av, L0_attn_b_w_ao, L0_ffn_W1, L0_ffn_b1, L0_ffn_W2, L0_ffn_b2):

    def _L0_attn_a_ref(x, adaptive_scale, Wq, bq, Wk, bk, Wv, bv, Wo, bo, gamma, beta):
        import jax, jax.numpy as jnp
        import numpy as np
        H, HD, D = (16, 64, 128)
        SCALE = HD ** (-0.5)
        TEMP = 1.0
        EPS = 1e-05
        B, N, _ = x.shape
        Q = (x @ Wq.T + bq).reshape(B, N, H, HD)
        K = (x @ Wk.T + bk).reshape(B, N, H, HD)
        V = (x @ Wv.T + bv).reshape(B, N, H, HD)
        scores = jnp.einsum('bnhd,bmhd->bhnm', Q, K)
        scores = scores * (SCALE * adaptive_scale)[None, :, None, None] / TEMP
        w = jax.nn.softmax(scores, axis=-1)
        attn = jnp.einsum('bhnm,bmhd->bnhd', w, V).reshape(B, N, H * HD)
        y = x + (attn @ Wo.T + bo)
        mu = jnp.mean(y, axis=-1, keepdims=True)
        var = jnp.var(y, axis=-1, keepdims=True)
        return (y - mu) / jnp.sqrt(var + EPS) * gamma + beta

    def _L0_attn_b_ref(x, w_aq, w_ak, w_av, w_ao):
        import jax, jax.numpy as jnp
        import numpy as np
        INF_APPROX = 1e+30
        ROTARY_BASE = 10000.0
        D_HEAD = 128

        def _rope(x, base=ROTARY_BASE):
            _, length, _, width = x.shape
            half = width // 2
            positions = jnp.arange(length, dtype=x.dtype)
            dims = jnp.arange(half, dtype=x.dtype)
            ang_freqs = jnp.power(base, -dims / half)
            radians = positions[:, None] * ang_freqs[None, :]
            cos = jnp.cos(radians)[None, :, None, :]
            sin = jnp.sin(radians)[None, :, None, :]
            even, odd = jnp.split(x, 2, axis=-1)
            return jnp.concatenate([even * cos - odd * sin, even * sin + odd * cos], axis=-1)
        B, T, M = x.shape
        q = jnp.einsum('btm,mhd->bthd', x, w_aq)
        k = jnp.einsum('btm,mhd->bthd', x, w_ak)
        v = jnp.einsum('btm,mhd->bthd', x, w_av)
        q = _rope(q)
        k = _rope(k)
        s = jnp.einsum('bihd,bjhd->bhij', q, k) / D_HEAD
        i = jnp.arange(T)[:, None]
        j = jnp.arange(T)[None, :]
        mask = (i < j).astype(x.dtype)[None, None, :, :]
        s = s - jnp.asarray(INF_APPROX, x.dtype) * mask
        p = jax.nn.softmax(s, axis=-1)
        o = jnp.einsum('bhij,bjhd->bihd', p, v)
        r = jnp.einsum('bihd,hdm->bim', o, w_ao)
        return r

    def _L0_ffn_ref(hidden_states, W1, b1, W2, b2):
        import jax, jax.numpy as jnp
        import numpy as np
        HIDDEN = 128
        INTER = 512
        h = jax.nn.relu(jnp.einsum('bsh,hi->bsi', hidden_states, W1) + b1)
        return jnp.einsum('bsi,ih->bsh', h, W2) + b2
    x = L0_attn_a_x
    x = x + _L0_attn_a_ref(_layernorm(x, axis=-1), L0_attn_a_adaptive_scale, L0_attn_a_Wq, L0_attn_a_bq, L0_attn_a_Wk, L0_attn_a_bk, L0_attn_a_Wv, L0_attn_a_bv, L0_attn_a_Wo, L0_attn_a_bo, L0_attn_a_gamma, L0_attn_a_beta)
    x = x + _L0_ffn_ref(_layernorm(x, axis=-1), L0_ffn_W1, L0_ffn_b1, L0_ffn_W2, L0_ffn_b2)
    x = x + _L0_attn_b_ref(_layernorm(x, axis=-1), L0_attn_b_w_aq, L0_attn_b_w_ak, L0_attn_b_w_av, L0_attn_b_w_ao)
    x = x + _L0_ffn_ref(_layernorm(x, axis=-1), L0_ffn_W1, L0_ffn_b1, L0_ffn_W2, L0_ffn_b2)
    return x

_drawn_inputs = setup_inputs


def setup_inputs(seed=0):
    import zlib

    import numpy as np

    out = dict(_drawn_inputs(seed))
    spreads = {'L0_attn_a_adaptive_scale': (1.0, 0.6),
     'L0_attn_a_gamma': (1.0, 0.2),
     'L0_attn_a_beta': (0.0, 0.1),
     'L0_attn_b_w_aq': (0.0, 0.8)}
    factors = {'L0_attn_a_Wq': 3.882,
     'L0_attn_a_bq': 8.0,
     'L0_attn_a_Wk': 3.829,
     'L0_attn_a_bk': 64.0,
     'L0_attn_a_Wv': 3.165,
     'L0_attn_b_w_ak': 8.0,
     'L0_ffn_b1': 5.075,
     'L0_ffn_b2': 3.446,
     'L0_attn_a_bo': 3.263}
    for name, (base, spread) in spreads.items():
        noise = np.random.default_rng([zlib.crc32(name.encode()), seed]).standard_normal(out[name].shape)
        drawn = base * np.exp(spread * noise) if base else spread * noise
        out[name] = jnp.asarray(drawn.astype(out[name].dtype))
    for name, factor in factors.items():
        out[name] = (out[name] * factor).astype(out[name].dtype)
    return out
```

```python
from contextlib import ExitStack

import numpy as np

import concourse.bass as bass
from concourse import mybir

F32 = mybir.dt.float32
F32R = mybir.dt.float32r
ALU = mybir.AluOpType
ACT = mybir.ActivationFunctionType
X_AXIS = mybir.AxisListType.X

P = 128
T = 2048
D = 128
TILES = T // P
BLK = 512
BLOCKS = T // BLK
BT = BLK // P
EPS = 1e-5

HA, DA = 16, 64
VA = DA + 1
SCALE_A = DA ** -0.5
ITER_A = HA // 2
UNITS_A = 2 * BLOCKS
STEPS_A = TILES // 2
G_A = UNITS_A * STEPS_A
WCOL = 2 * DA + 2

HB, DB = 8, 128
VB = DB + 1
ITER_B = HB // 2
UNITS_B = 2 * BLOCKS
MASKED = -1e30
INTER = 512
CH = INTER // P

AUX = 2 * BT


def steps_b(qb):
    return BT * (qb + 1)


G_B = 2 * sum(steps_b(q) for q in range(BLOCKS))


def ring_items_a(ul, step, first, last):
    hs, qb = divmod(ul, BLOCKS)
    items = []
    has_next = not (last and ul == UNITS_A - 1)
    if has_next:
        at = [0, 3, 5, 7, 10, 12, 14, 16, 16]
        items += [("max", i) for i in range(at[step], at[step + 1])]
    if ((ul - 1) % UNITS_A) // BLOCKS == 1 and not (first and ul == 0):
        items += [("turned",)] if step == 2 else [("output",)] if step == 3 else []
    if not (last and hs == 1) and qb < 2 and step in (5, 6):
        items += [("project", 2 * qb + step - 5)]
    if has_next and step == STEPS_A - 1:
        items += [("rows",)]
    return items


def max_items_b(qb):
    return [(i, c) for i in range(BT) for c in range(qb + 1)]


PROJECT_B = {(1, 5): [0], (2, 3): [1], (2, 6): [2], (2, 9): [3], (3, 1): [4], (3, 3): [5], (3, 5): [6], (3, 7): [7]}


def ring_items_b(ul, step, first, last):
    hs, qb = divmod(ul, BLOCKS)
    n = steps_b(qb)
    has_next = not (last and ul == UNITS_B - 1)
    items = []
    if has_next:
        todo = max_items_b((qb + 1) % BLOCKS)
        begin = n - 3 if qb == BLOCKS - 1 else 0
        room = n - 1 - begin
        if begin <= step < n - 1:
            lo, hi = (len(todo) * (step - begin + d) // room for d in (0, 1))
            items += [("max", j) for j in range(lo, hi)]
    if not (first and ul == 0):
        items += [("turned",)] if step == 2 else [("output",)] if step == 3 else []
    if not (last and hs == 1):
        items += [("project", b) for b in PROJECT_B.get((qb, step), [])]
    if has_next and step == n - 1:
        items += [("rows",)]
    return items


def count_items(items_of, units, steps_of):
    return sum(len(items_of(ul, s, False, False)) for ul in range(units) for s in range(steps_of(ul)))


RING_A = count_items(ring_items_a, UNITS_A, lambda ul: STEPS_A)
RING_B = count_items(ring_items_b, UNITS_B, lambda ul: steps_b(ul % BLOCKS))
assert RING_A % 2 == 0 and RING_B % 2 == 0
LEAD_A = BLOCKS + 16 + 1
LEAD_B = 2 * BLOCKS + BT + 1
SKIP = 2


def build(nc, x, adaptive_scale, Wq, bq, Wk, bk, Wv, bv, Wo, bo, gamma, beta,
          w_aq, w_ak, w_av, w_ao, W1, b1, W2, b2, rope_cos, rope_sin, out):
    ctx = ExitStack()
    with ctx:
        def sb(name, shape, dt=F32):
            return ctx.enter_context(nc.sbuf_tensor(name, shape, dt))

        def pb(name, shape):
            return ctx.enter_context(nc.psum_tensor(name, shape, F32))

        def sem(name):
            return ctx.enter_context(nc.semaphore(name))

        X = sb("X", [P, TILES, D])
        XN = sb("XN", [P, TILES, D])
        XNT = sb("XNT", [P, T])
        V = sb("V", [P, TILES, HA * VA])
        PR = sb("PR", [P, 2, 2 * BLK])
        F = sb("F", [P, 2, BLK])
        WST = sb("WST", [P, 2, 2 * DB])
        AT = sb("AT", [P, BLK])
        AB = sb("AB", [P, BT, DB])
        SHARED = sb("SHARED", [P, max(HA * WCOL + 8 * D + T, 2 * T + HB * D)])
        W1s = sb("W1s", [P, INTER])
        W2s = sb("W2s", [P, CH, D])
        ident = sb("ident", [P, P])
        rowmask = sb("rowmask", [AUX, BT, P])
        bo_b = sb("bo_b", [P, D])
        gamma_b = sb("gamma_b", [P, D])
        beta_b = sb("beta_b", [P, D])
        b2_b = sb("b2_b", [P, D])
        b1c = sb("b1c", [P, CH])
        eps = sb("eps", [P, 1])
        stats = sb("stats", [P, BT, 6])
        meanvar = sb("meanvar", [P, BT, 2])
        std = sb("std", [P, BT])
        rstd = sb("rstd", [P, BT])
        maxes = sb("maxes", [P, BT, BLOCKS])
        negmax = sb("negmax", [P, BT])
        negparts = sb("negparts", [P, AUX])
        rden = sb("rden", [P, BT])
        KH = [sb(f"KH{i}", [P, T], F32R) for i in range(2)]
        KL = [sb(f"KL{i}", [P, T], F32R) for i in range(2)]
        QH = [sb(f"QH{i}", [P, T], F32R) for i in range(2)]
        QL = [sb(f"QL{i}", [P, T], F32R) for i in range(2)]
        ident_r = sb("ident_r", [P, P], F32R)
        later_keys = sb("later_keys", [P, P], F32R)
        later_keys_t = sb("later_keys_t", [P, P], F32R)
        ones_r = sb("ones_r", [AUX, P], F32R)
        MROW = sb("MROW", [AUX, 2, BLK], F32R)

        wqk_raw = V[:, 0:2, :].rearrange("p a b -> p (a b)")[:, 0:HA * P].rearrange("p (h c) -> p h c", c=P)
        wv_raw = V[:, 2, 0:HA * DA].rearrange("p (j c) -> p j c", c=P)
        wo_raw = V[:, 3, 0:HA * DA].rearrange("p (j c) -> p j c", c=P)
        braw = V[0:HA, 4, 0:P]
        sraw = V[0:DA, 5, 0:HA]
        bv_b = PR[:, 0, :]
        wvT = PR[:, 1, :]
        WQK = SHARED[:, 0:HA * WCOL].rearrange("p (h c) -> p h c", c=WCOL)
        WoT = SHARED[:, HA * WCOL:HA * WCOL + 8 * D].rearrange("p (j c) -> p j c", c=D)
        A2 = SHARED[:, HA * WCOL + 8 * D:HA * WCOL + 8 * D + T].rearrange("p (t c) -> p t c", c=D)
        COS = SHARED[:, 0:T]
        SIN = SHARED[:, T:2 * T]
        WAO = SHARED[:, 2 * T:2 * T + HB * D].rearrange("p (h c) -> p h c", c=D)
        WQKB = XN[:, :, :].rearrange("p (h a) c -> p h a c", a=2)
        wav = PR[:, 1, :]
        VAv = V[:, :, :].rearrange("p t (h c) -> p t h c", c=VA)
        VBv = V[:, :, 0:HB * VB].rearrange("p t (h c) -> p t h c", c=VB)
        PRB = PR[:, 0, :].rearrange("p (s q) -> p s q", s=2)
        SWAP = PR[:, 1, :].rearrange("p (s q) -> p s q", s=2)
        HID = PR[:, :, :].rearrange("p a (b q) -> p (a b) q", b=2)
        mask_raw = F[:, 0, 0:2 * P].rearrange("p (a c) -> p a c", a=2)

        ST = [pb(f"ST{i}", [P, 2 * BLK]) for i in range(2)]
        RING = [pb(f"RING{i}", [P, BLK]) for i in range(2)]
        O = [pb(f"O{i}", [P, BLK]) for i in range(2)]
        QUARTER = [ST[i // 2][:, (i % 2) * BLK:(i % 2 + 1) * BLK] for i in range(4)]
        SB = [QUARTER[0], QUARTER[1]]
        OB = [(O[0], QUARTER[2]), (O[1], QUARTER[3])]

        x_in = [sem(f"x_in{b}") for b in range(BLOCKS)]
        w_in = sem("w_in")
        vw_in = sem("vw_in")
        c_in = sem("c_in")
        fw_in = sem("fw_in")
        consts = sem("consts")
        const_r = sem("const_r")
        chain = sem("chain")
        pchain = sem("pchain")
        var_ready = sem("var_ready")
        std_ready = sem("std_ready")
        xn_ready = sem("xn_ready")
        xnt_put = sem("xnt_put")
        xnt_ready = sem("xnt_ready")
        wt_put = sem("wt_put")
        wt_act = sem("wt_act")
        wt_dve = sem("wt_dve")
        v_put = sem("v_put")
        v_act = sem("v_act")
        v_dve = sem("v_dve")
        ones_set = sem("ones_set")
        xbo = sem("xbo")
        bweights = sem("bweights")
        hid_put = sem("hid_put")
        hid_ready = sem("hid_ready")
        ffn_put = sem("ffn_put")
        x_ready = sem("x_ready")
        out_done = sem("out_done")

        class Phase:
            pass

        def phase(n):
            s = Phase()
            s.wst_ready = sem(f"wst_ready_{n}")
            s.ring_put = sem(f"ring_put_{n}")
            s.ring_taken = sem(f"ring_taken_{n}")
            s.rope_summed = sem(f"rope_summed_{n}")
            s.high_ready = sem(f"high_ready_{n}")
            s.operands_ready = sem(f"operands_ready_{n}")
            s.max_ready = sem(f"max_ready_{n}")
            s.scores = sem(f"scores_{n}")
            s.exps = sem(f"exps_{n}")
            s.pv = sem(f"pv_{n}")
            s.o_taken = sem(f"o_taken_{n}")
            return s

        sa, sbb = phase("a"), phase("b")

        def wait(eng, s, value):
            if not isinstance(value, int) or value > 0:
                eng.wait_ge(s, value)

        block = ctx.enter_context(nc.Block())

        @block.sync
        def _(sp):
            xin = x[0].rearrange("(t p) c -> p t c", p=P)
            for b in range(BLOCKS):
                sp.dma_start(X[:, b * BT:(b + 1) * BT, :], xin[:, b * BT:(b + 1) * BT, :]).then_inc(x_in[b], 16)
            sp.dma_start(wqk_raw[0:DA, :, :], Wq.rearrange("(h d) c -> d h c", d=DA)).then_inc(w_in, 16)
            sp.dma_start(wqk_raw[DA:P, :, :], Wk.rearrange("(h d) c -> d h c", d=DA)).then_inc(w_in, 16)
            sp.dma_start(braw[:, 0:DA], bq.rearrange("(h d) -> h d", d=DA)).then_inc(w_in, 16)
            sp.dma_start(braw[:, DA:P], bk.rearrange("(h d) -> h d", d=DA)).then_inc(w_in, 16)
            sp.dma_start(sraw, adaptive_scale.partition_broadcast(DA)).then_inc(w_in, 16)
            sp.dma_start(wv_raw, Wv.rearrange("(j p) c -> p j c", p=P)).then_inc(vw_in, 16)
            sp.dma_start(wo_raw, Wo.rearrange("p (j c) -> p j c", c=P)).then_inc(vw_in, 16)
            sp.dma_start(bv_b, bv.partition_broadcast(P)).then_inc(vw_in, 16)
            for dst, src in ((bo_b, bo), (gamma_b, gamma), (beta_b, beta), (b2_b, b2)):
                sp.dma_start(dst[:, :], src.partition_broadcast(P)).then_inc(c_in, 16)
            sp.dma_start(b1c[:, :], b1.rearrange("(j p) -> p j", p=P), allow_slow_non_contiguous=True).then_inc(fw_in, 16)
            sp.dma_start(W1s[:, :], W1).then_inc(fw_in, 16)
            sp.dma_start(W2s[:, :, :], W2.rearrange("(j p) n -> p j n", p=P)).then_inc(fw_in, 16)
            wait(sp, sa.ring_taken, LEAD_A - SKIP + ITER_A * RING_A - 17 - 4 + 2)
            sp.dma_start(COS, rope_cos).then_inc(bweights, 16)
            sp.dma_start(SIN, rope_sin).then_inc(bweights, 16)
            sp.dma_start(WAO, w_ao.rearrange("h d m -> d h m")).then_inc(bweights, 16)
            wait(sp, ffn_put, BLOCKS)
            sp.dma_start(wav, w_av.rearrange("m h d -> m (h d)")).then_inc(bweights, 16)
            wait(sp, xnt_put, 3 * BLOCKS)
            sp.dma_start(WQKB[:, :, 0, :], w_aq).then_inc(bweights, 16)
            sp.dma_start(WQKB[:, :, 1, :], w_ak).then_inc(bweights, 16)
            oout = out[0].rearrange("(t p) c -> p t c", p=P)
            for b in range(BLOCKS):
                wait(sp, x_ready, BLOCKS + b + 1)
                sp.dma_start(oout[:, b * BT:(b + 1) * BT, :], X[:, b * BT:(b + 1) * BT, :]).then_inc(out_done, 16)
            wait(sp, out_done, 16 * BLOCKS)

        @block.gpsimd
        def _(pool):
            tick = [0]

            def link(ins):
                tick[0] += 1
                ins.then_inc(pchain, 1)
                pool.wait_ge(pchain, tick[0])

            link(pool.memset(ident[:, :], 0.0))
            pool.affine_select(out=ident[:, :], in_=ident[:, :], compare_op=ALU.not_equal, fill=1.0, base=0,
                               pattern=[[-1, P]], channel_multiplier=1).then_inc(consts, 1)
            link(pool.memset(mask_raw, 0.0))
            pool.affine_select(out=mask_raw[:, 0, :], in_=mask_raw[:, 0, :], compare_op=ALU.is_ge, fill=MASKED,
                               base=0, pattern=[[-1, P]], channel_multiplier=1)
            pool.affine_select(out=mask_raw[:, 1, :], in_=mask_raw[:, 1, :], compare_op=ALU.is_ge, fill=MASKED,
                               base=0, pattern=[[1, P]], channel_multiplier=-1).then_inc(consts, 1)
            link(pool.memset(rowmask[:, :, :], 0.0))
            for half in range(2):
                ins = pool.affine_select(out=rowmask[:, :, :], in_=rowmask[:, :, :], compare_op=ALU.not_equal,
                                         fill=1.0, base=-half * BT, pattern=[[-1, BT], [0, P]],
                                         channel_multiplier=1)
                if half == 0:
                    link(ins)
            ins.then_inc(consts, 1)
            pool.wait_ge(wt_act, 5)
            pool.wait_ge(wt_dve, 5)
            pool.tensor_copy(WST[:, 0, 0:WCOL], WQK[:, 0, :]).then_inc(sa.wst_ready, 1)
            pool.wait_ge(wt_put, 9)
            pool.memset(VAv[:, :, :, DA:VA], 1.0).then_inc(ones_set, 1)
            pool.wait_ge(ones_set, 1)

            def low_parts_a(hs, blk, index):
                pool.wait_ge(sa.high_ready, index + 1)
                q = slice(blk * BLK, (blk + 1) * BLK)
                f = F[:, blk % 2, :]
                pool.tensor_tensor(QL[hs][0:DA, q], f[0:DA, :], QL[hs][0:DA, q].bitcast(F32), ALU.subtract)
                pool.tensor_tensor(KL[hs][DA:P, q], f[DA:P, :], KH[hs][DA:P, q].bitcast(F32),
                                   ALU.subtract).then_inc(sa.operands_ready, 1)

            for blk in range(BLOCKS):
                low_parts_a(0, blk, blk)
            pool.wait_ge(c_in, 64)
            pool.wait_ge(sa.operands_ready, BLOCKS)
            pool.wait_ge(xnt_put, BLOCKS)
            pool.tensor_tensor(XN[:, :, :], XN[:, :, :], bo_b[:, :].unsqueeze(1).broadcast_to((P, TILES, D)),
                               ALU.add).then_inc(xbo, 1)
            pool.tensor_tensor(X[:, :, :], X[:, :, :], beta_b[:, :].unsqueeze(1).broadcast_to((P, TILES, D)),
                               ALU.add).then_inc(xbo, 1)

            def heads_a(it, last=False):
                for hs in range(2):
                    if last and hs == 1:
                        continue
                    head = it * 2 + hs + 1
                    pool.wait_ge(sa.operands_ready, head * BLOCKS)
                    pool.tensor_copy(WST[:, 1 - hs, 0:WCOL], WQK[:, bass.ds(head, 1), :].rearrange("p a c -> p (a c)")
                                     ).then_inc(sa.wst_ready, 1)
                    pool.wait_ge(sa.wst_ready, head + 1)
                    for blk in range(BLOCKS):
                        low_parts_a(1 - hs, blk, head * BLOCKS + blk)

            heads_a(0)
            with pool.Fori(1, ITER_A - 1) as it:
                heads_a(it)
            heads_a(ITER_A - 1, last=True)

            pool.wait_ge(bweights, 16 * 6)
            pool.memset(VBv[:, :, :, DB:VB], 1.0).then_inc(ones_set, 1)
            pool.tensor_copy(WST[:, 0, :], WQKB[:, 0, :, :].rearrange("p a c -> p (a c)")
                             ).then_inc(sbb.wst_ready, 1)

            def rope_and_low_b(hs, j, index, item):
                pool.wait_ge(sbb.ring_taken, item + 1)
                s = j % 2
                q = slice(j // 2 * BLK, (j // 2 + 1) * BLK)
                high, low = ((QH, QL), (KH, KL))[j % 2]
                pool.tensor_tensor(F[:, s, :], F[:, s, :], SWAP[:, s, :], ALU.add).then_inc(sbb.rope_summed, 1)
                pool.wait_ge(sbb.high_ready, index + 1)
                pool.tensor_tensor(low[hs][:, q], F[:, s, :], high[hs][:, q].bitcast(F32),
                                   ALU.subtract).then_inc(sbb.operands_ready, 1)

            for j in range(2 * BLOCKS):
                rope_and_low_b(0, j, j, j)

            def heads_b(it, first=False, last=False):
                k = SKIP if first else 0
                for ul in range(UNITS_B):
                    hs, qb = divmod(ul, BLOCKS)
                    head = it * 2 + hs + 1
                    if qb == 0 and not (last and hs == 1):
                        pool.tensor_copy(WST[:, 1 - hs, :], WQKB[:, bass.ds(head, 1), :, :].rearrange(
                            "p z a c -> p (z a c)")).then_inc(sbb.wst_ready, 1)
                    for step in range(steps_b(qb)):
                        for item in ring_items_b(ul, step, first, last):
                            if item[0] == "project":
                                rope_and_low_b(1 - hs, item[1], head * 2 * BLOCKS + item[1],
                                               LEAD_B - SKIP + it * RING_B + k)
                            k += 1

            heads_b(0, first=True)
            with pool.Fori(1, ITER_B - 1) as it:
                heads_b(it)
            heads_b(ITER_B - 1, last=True)

        @block.scalar
        def _(act):
            def deviations(n):
                act.wait_ge(var_ready, n + 1)
                act.activation(std[:, :], meanvar[:, :, 1], ACT.Sqrt, bias=eps[:, :]).then_inc(std_ready, 1)

            def transposed_block(n, bank, free=None):
                act.wait_ge(xnt_put, n + 1)
                b = n % BLOCKS
                act.activation(XNT[:, b * BLK:(b + 1) * BLK], bank, ACT.Copy).then_inc(xnt_ready, 1)

            act.wait_ge(const_r, 1)
            for b in range(BLOCKS):
                deviations(b)
            for i in range(0, 9, 2):
                act.wait_ge(wt_put, i + 1)
                bank = QUARTER[i % 4]
                src4 = bank.rearrange("p (a c) -> p a c", c=P)
                if i < 4:
                    ins = act.activation(WQK[:, i * 4:i * 4 + 4, 0:P], src4, ACT.Copy)
                elif i < 6:
                    ins = act.activation(wvT[:, (i - 4) * BLK:(i - 3) * BLK], bank, ACT.Copy)
                elif i < 8:
                    ins = act.activation(WoT[:, (i - 6) * 4:(i - 6) * 4 + 4, :], src4, ACT.Copy)
                else:
                    ins = act.activation(WQK[:, :, P], bank[:, 0:HA], ACT.Copy)
                ins.then_inc(wt_act, 1)
            for b in range(BLOCKS):
                transposed_block(b, O[b % 2][:, :])

            def high_parts_a(hs, blk, item, scores_before):
                act.wait_ge(sa.ring_taken, item + 1)
                wait(act, sa.scores, scores_before)
                q = slice(blk * BLK, (blk + 1) * BLK)
                f = F[:, blk % 2, :]
                act.activation(QL[hs][0:DA, q], f[0:DA, :], ACT.Copy)
                act.activation(QL[hs][DA:P, q], f[0:DA, :], ACT.Copy)
                act.activation(QH[hs][DA:P, q], f[0:DA, :], ACT.Copy)
                act.activation(KH[hs][0:DA, q], f[DA:P, :], ACT.Copy)
                act.activation(KH[hs][DA:P, q], f[DA:P, :], ACT.Copy).then_inc(sa.high_ready, 1)

            for blk in range(BLOCKS):
                high_parts_a(0, blk, blk, 0)

            def exps_a(it, first=False, last=False):
                k = SKIP if first else 0
                todo = []
                for ul in range(UNITS_A):
                    hs, qb = divmod(ul, BLOCKS)
                    for step in range(STEPS_A):
                        g = it * G_A + ul * STEPS_A + step
                        if first and ul == 0 and step < 2:
                            act.wait_ge(v_dve, 32)
                        act.wait_ge(sa.scores, g + 1)
                        wait(act, sa.pv, g - 1)
                        act.activation(PR[:, step % 2, :], ST[step % 2][:, :], ACT.Exp).then_inc(sa.exps, 1)
                        for args in todo:
                            high_parts_a(*args)
                        todo = []
                        for item in ring_items_a(ul, step, first, last):
                            if item[0] == "project":
                                head = it * 2 + hs + 1
                                todo.append((1 - hs, item[1], LEAD_A - SKIP + it * RING_A + k,
                                             (head - 1) * BLOCKS * STEPS_A))
                            k += 1

            exps_a(0, first=True)
            with act.Fori(1, ITER_A - 1) as it:
                exps_a(it)
            exps_a(ITER_A - 1, last=True)

            def relus(r, b):
                for j in range(CH):
                    n = (r * BLOCKS + b) * CH + j
                    act.wait_ge(hid_put, n + 1)
                    wait(act, ffn_put, r * BLOCKS + b)
                    act.activation(HID[:, j, :], QUARTER[j], ACT.Relu, bias=b1c[:, j:j + 1]).then_inc(hid_ready, 1)

            def ffn(r, first_ln):
                deviations(first_ln)
                for b in range(BLOCKS):
                    if b + 1 < BLOCKS:
                        deviations(first_ln + b + 1)
                    transposed_block((1 if r == 0 else 3) * BLOCKS + b, O[b % 2][:, :])
                    relus(r, b)

            for b in range(BLOCKS):
                deviations(BLOCKS + b)
            act.wait_ge(fw_in, 48)
            ffn(0, 2 * BLOCKS)

            for b in range(BLOCKS):
                deviations(3 * BLOCKS + b)
                transposed_block(2 * BLOCKS + b, O[b % 2][:, :])

            def high_part_b(hs, j, index, scores_before):
                act.wait_ge(sbb.rope_summed, index + 1)
                wait(act, sbb.scores, scores_before)
                q = slice(j // 2 * BLK, (j // 2 + 1) * BLK)
                high = (QH, KH)[j % 2]
                act.activation(high[hs][:, q], F[:, j % 2, :], ACT.Copy).then_inc(sbb.high_ready, 1)

            for i in range(0, 2 * TILES, 2):
                act.wait_ge(v_put, 2 * TILES + i + 1)
                if i == 0:
                    act.wait_ge(ones_set, 2)
                act.activation(VBv[:, i // 2, 0:4, 0:DB], QUARTER[i % 4].rearrange("p (a c) -> p a c", c=DB),
                               ACT.Copy).then_inc(v_act, 1)
            for j in range(2 * BLOCKS):
                high_part_b(0, j, j, 0)

            def exps_b(it, first=False, last=False):
                todo = []
                g = it * G_B
                for ul in range(UNITS_B):
                    hs, qb = divmod(ul, BLOCKS)
                    for step in range(steps_b(qb)):
                        c0 = max(0, step - BT * qb) * P
                        if first and ul == 0 and step == 0:
                            act.wait_ge(v_dve, 2 * TILES + TILES)
                        act.wait_ge(sbb.scores, g + 1)
                        wait(act, sbb.pv, g - 1)
                        act.activation(PRB[:, step % 2, c0:BLK], SB[step % 2][:, c0:BLK], ACT.Exp,
                                       scale=1.0 / DB).then_inc(sbb.exps, 1)
                        g = g + 1
                        for args in todo:
                            high_part_b(*args)
                        todo = []
                        for item in ring_items_b(ul, step, first, last):
                            if item[0] == "project":
                                head = it * 2 + hs + 1
                                todo.append((1 - hs, item[1], head * 2 * BLOCKS + item[1],
                                             (head - 1) * (G_B // 2)))

            exps_b(0, first=True)
            with act.Fori(1, ITER_B - 1) as it:
                exps_b(it)
            exps_b(ITER_B - 1, last=True)
            ffn(1, 4 * BLOCKS)

        @block.vector
        def _(dve):
            tick = [0]
            loop_base = [None]

            def link(ins):
                ins.then_inc(chain, 1)
                tick[0] += 1
                dve.wait_ge(chain, tick[0] if loop_base[0] is None else loop_base[0] + tick[0])

            def layer_norm(n, b, src, dst, signal=True):
                for i in range(BT):
                    ins = dve.bn_stats(stats[:, i, :], src[:, b * BT + i, :])
                link(ins)
                for i in range(BT):
                    ins = dve.bn_aggr(meanvar[:, i, :], stats[:, i, :])
                ins.then_inc(var_ready, 1)
                dve.wait_ge(std_ready, n + 1)
                link(dve.reciprocal(rstd[:, :], std[:, :]))
                for i in range(BT):
                    ins = dve.tensor_scalar(dst[:, b * BT + i, :], src[:, b * BT + i, :], meanvar[:, i, 0:1],
                                            rstd[:, i:i + 1], ALU.subtract, ALU.mult)
                if signal:
                    ins.then_inc(xn_ready, 1)
                else:
                    link(ins)

            dve.memset(eps[:, :], EPS)
            for i in range(2):
                dve.memset(QH[i][0:DA, :].bitcast(F32), 0.0)
                link(dve.memset(KL[i][0:DA, :].bitcast(F32), 0.0))
                dve.memset(KL[i][0:AUX, :].bitcast(F32), 1.0)
            dve.memset(ones_r[:, :].bitcast(F32), 1.0).then_inc(const_r, 1)
            for b in range(BLOCKS):
                dve.wait_ge(x_in[b], 16)
                layer_norm(b, b, X, XN)
            dve.wait_ge(consts, 3)
            dve.tensor_copy(ident_r[:, :], ident[:, :])
            dve.tensor_copy(later_keys[:, :], mask_raw[:, 0, :])
            dve.tensor_copy(later_keys_t[:, :], mask_raw[:, 1, :]).then_inc(const_r, 1)
            for i in range(1, 8, 2):
                dve.wait_ge(wt_put, i + 1)
                bank = QUARTER[i % 4]
                src4 = bank.rearrange("p (a c) -> p a c", c=P)
                if i < 4:
                    ins = dve.tensor_copy(WQK[:, i * 4:i * 4 + 4, 0:P], src4)
                elif i < 6:
                    ins = dve.tensor_copy(wvT[:, (i - 4) * BLK:(i - 3) * BLK], bank)
                else:
                    ins = dve.tensor_copy(WoT[:, (i - 6) * 4:(i - 6) * 4 + 4, :], src4)
                ins.then_inc(wt_dve, 1)
            dve.wait_ge(w_in, 80)
            dve.memset(WQK[DA:P, :, P + 1], 1.0)
            dve.tensor_scalar(WQK[0:DA, :, P + 1], sraw, SCALE_A, None, ALU.mult).then_inc(wt_dve, 1)

            def take_projected_a(hs, blk, item, index):
                dve.wait_ge(sa.ring_put, item + 1)
                wait(dve, sa.operands_ready, index - 1)
                dve.tensor_scalar(F[:, blk % 2, :], RING[ring_slot(item, sa)][:, :], WST[:, hs, P:P + 1],
                                  WST[:, hs, P + 1:P + 2], ALU.add, ALU.mult).then_inc(sa.ring_taken, 1)

            def ring_slot(item, s):
                return slots[0] % 2

            slots = [0]

            def take_max(s, item, qt, c, width, chunks, last):
                dve.wait_ge(s.ring_put, item + 1)
                ins = dve.reduce_max(maxes[:, qt, c:c + 1], RING[slots[0] % 2][:, 0:width], X_AXIS)
                ins.then_inc(s.ring_taken, 1)
                if last:
                    dve.wait_ge(s.ring_taken, item + 1)
                    link(dve.tensor_reduce(negmax[:, :], maxes[:, :, 0:chunks], X_AXIS, ALU.max, negate=True))
                    link(dve.tensor_copy(negparts[:, 0:BT].bitcast(F32R), negmax[:, :]))
                    dve.tensor_tensor(negparts[:, BT:AUX], negmax[:, :], negparts[:, 0:BT],
                                      ALU.subtract).then_inc(s.max_ready, 1)

            def take_rows(s, item, dst):
                dve.wait_ge(s.ring_put, item + 1)
                rows = RING[slots[0] % 2][0:AUX, 0:P].unsqueeze(1).broadcast_to((AUX, BT, P))
                dve.tensor_tensor(dst.rearrange("p (a c) -> p a c", c=P), rows, rowmask[:, :, :],
                                  ALU.mult).then_inc(s.ring_taken, 1)

            def take_turned(s, item):
                dve.wait_ge(s.ring_put, item + 1)
                dve.tensor_copy(AT[:, :], RING[slots[0] % 2][:, :]).then_inc(s.ring_taken, 1)

            def take_output(s, item, acc, qb):
                dve.wait_ge(s.ring_put, item + 1)
                a = acc[:, qb * BT:(qb + 1) * BT, :]
                dve.tensor_tensor(a, a, RING[slots[0] % 2][:, :].rearrange("p (a c) -> p a c", c=D),
                                  ALU.add).then_inc(s.ring_taken, 1)

            def normalise_a(ul, units_done):
                hs, qb = divmod(ul, BLOCKS)
                dve.wait_ge(sa.pv, units_done * STEPS_A)
                o = O[ul % 2][:, 0:BT * VA].rearrange("p (a c) -> p a c", c=VA)
                link(dve.reciprocal(rden[:, :], o[:, :, DA]))
                dve.tensor_tensor(A2[:, qb * BT:(qb + 1) * BT, hs * DA:(hs + 1) * DA], o[:, :, 0:DA],
                                  rden[:, :].unsqueeze(2).broadcast_to((P, BT, DA)), ALU.mult
                                  ).then_inc(sa.o_taken, 1)

            for blk in range(BLOCKS):
                slots[0] = blk
                take_projected_a(0, blk, blk, blk)
            for i in range(2 * TILES):
                dve.wait_ge(v_put, i + 1)
                if i == 0:
                    dve.wait_ge(ones_set, 1)
                    dve.wait_ge(vw_in, 48)
                hh = (i % 2) * 8
                dve.tensor_tensor(VAv[:, i // 2, hh:hh + 8, 0:DA], QUARTER[i % 4].rearrange("p (a c) -> p a c", c=DA),
                                  bv_b[:, hh * DA:(hh + 8) * DA].rearrange("p (a c) -> p a c", c=DA),
                                  ALU.add).then_inc(v_dve, 1)
            for i in range(16):
                slots[0] = BLOCKS + i
                take_max(sa, BLOCKS + i, i // 4, i % 4, BLK, BLOCKS, i == 15)
            slots[0] = LEAD_A - 1
            take_rows(sa, LEAD_A - 1, QH[0][0:AUX, 0:BLK])
            dve.wait_ge(xbo, 2)

            def body_a(it, first=False, last=False):
                k = SKIP if first else 0
                for ul in range(UNITS_A):
                    hs, qb = divmod(ul, BLOCKS)
                    nhs, nqb = divmod((ul + 1) % UNITS_A, BLOCKS)
                    u = it * UNITS_A + ul
                    for step in range(STEPS_A):
                        if step == 1 and not (first and ul == 0):
                            normalise_a((ul - 1) % UNITS_A, u)
                        for item in ring_items_a(ul, step, first, last):
                            n = LEAD_A - SKIP + it * RING_A + k
                            slots[0] = LEAD_A - SKIP + k
                            k += 1
                            if item[0] == "max":
                                i = item[1]
                                take_max(sa, n, i // 4, i % 4, BLK, BLOCKS, i == 15)
                            elif item[0] == "rows":
                                take_rows(sa, n, QH[nhs][0:AUX, nqb * BLK:(nqb + 1) * BLK])
                            elif item[0] == "project":
                                take_projected_a(1 - hs, item[1], n, (it * 2 + hs + 1) * BLOCKS + item[1])
                            elif item[0] == "turned":
                                take_turned(sa, n)
                            else:
                                take_output(sa, n, XN, (qb - 1) % BLOCKS)
                return k

            def looped(body, turns):
                before = tick[0]
                loop_base[0] = None
                body(0, first=True)
                start = tick[0]
                with dve.Fori(1, turns - 1) as it:
                    tick[0] = 0
                    loop_base[0] = (it - 1) * links_of[body.__name__] + start
                    body(it)
                    assert tick[0] == links_of[body.__name__], (body.__name__, tick[0])
                loop_base[0] = None
                tick[0] = start + (turns - 2) * links_of[body.__name__]
                return body(turns - 1, last=True)

            links_of = {"body_a": 3 * UNITS_A, "body_b": 3 * UNITS_B}

            k = looped(body_a, ITER_A)
            n = LEAD_A - SKIP + (ITER_A - 1) * RING_A + k
            normalise_a(UNITS_A - 1, ITER_A * UNITS_A)
            slots[0] = LEAD_A - SKIP + k
            take_turned(sa, n)
            slots[0] += 1
            take_output(sa, n + 1, XN, BLOCKS - 1)
            dve.wait_ge(sa.ring_taken, n + 2)

            for b in range(BLOCKS):
                layer_norm(BLOCKS + b, b, XN, XN, signal=False)
                y = XN[:, b * BT:(b + 1) * BT, :]
                a = X[:, b * BT:(b + 1) * BT, :]
                link(dve.tensor_tensor(y, y, gamma_b[:, :].unsqueeze(1).broadcast_to((P, BT, D)), ALU.mult))
                link(dve.tensor_tensor(a, a, y, ALU.add))

            def take_ffn(r, b):
                dve.wait_ge(ffn_put, r * BLOCKS + b + 1)
                a = X[:, b * BT:(b + 1) * BT, :]
                link(dve.tensor_tensor(a, a, RING[b % 2][:, :].rearrange("p (a c) -> p a c", c=D), ALU.add))
                dve.tensor_tensor(a, a, b2_b[:, :].unsqueeze(1).broadcast_to((P, BT, D)), ALU.add
                                  ).then_inc(x_ready, 1)

            def ffn(r, first_ln):
                layer_norm(first_ln, 0, X, XN)
                for b in range(BLOCKS):
                    if b + 1 < BLOCKS:
                        layer_norm(first_ln + b + 1, b + 1, X, XN)
                    take_ffn(r, b)

            ffn(0, 2 * BLOCKS)

            for b in range(BLOCKS):
                dve.wait_ge(x_ready, b + 1)
                layer_norm(3 * BLOCKS + b, b, X, XN)

            def take_projected_b(j, item, index):
                dve.wait_ge(sbb.ring_put, item + 1)
                wait(dve, sbb.operands_ready, index - 1)
                s, r = j % 2, RING[slots[0] % 2]
                q = slice(j // 2 * BLK, (j // 2 + 1) * BLK)
                half = DB // 2
                dve.tensor_tensor(F[:, s, :], r[:, :], COS[:, q], ALU.mult)
                dve.tensor_tensor(SWAP[0:half, s, :], r[half:P, :], SIN[0:half, q], ALU.mult)
                dve.tensor_tensor(SWAP[half:P, s, :], r[0:half, :], SIN[half:P, q], ALU.mult
                                  ).then_inc(sbb.ring_taken, 1)

            def normalise_b(ul, steps_done):
                dve.wait_ge(sbb.pv, steps_done)
                three, fourth = OB[ul % 2]
                o = three[:, 0:3 * VB].rearrange("p (a c) -> p a c", c=VB)
                dve.reciprocal(rden[:, 0:3], o[:, :, DB])
                link(dve.reciprocal(rden[:, 3:4], fourth[:, DB:VB]))
                dve.tensor_tensor(AB[:, 0:3, :], o[:, :, 0:DB], rden[:, 0:3].unsqueeze(2).broadcast_to((P, 3, DB)),
                                  ALU.mult)
                dve.tensor_scalar(AB[:, 3, :], fourth[:, 0:DB], rden[:, 3:4], None, ALU.mult
                                  ).then_inc(sbb.o_taken, 1)

            dve.wait_ge(bweights, 16 * 6)
            for i in range(1, 2 * TILES, 2):
                dve.wait_ge(v_put, 2 * TILES + i + 1)
                dve.tensor_copy(VBv[:, i // 2, 4:8, 0:DB], QUARTER[i % 4].rearrange("p (a c) -> p a c", c=DB)
                                ).then_inc(v_dve, 1)
            for j in range(2 * BLOCKS):
                slots[0] = j
                take_projected_b(j, j, j)
            for i in range(BT):
                slots[0] = 2 * BLOCKS + i
                take_max(sbb, 2 * BLOCKS + i, i, 0, (i + 1) * P, 1, i == BT - 1)
            slots[0] = LEAD_B - 1
            take_rows(sbb, LEAD_B - 1, MROW[:, 0, :])

            def body_b(it, first=False, last=False):
                k = SKIP if first else 0
                done = it * G_B
                for ul in range(UNITS_B):
                    hs, qb = divmod(ul, BLOCKS)
                    nqb = (qb + 1) % BLOCKS
                    u = it * UNITS_B + ul
                    todo = max_items_b(nqb)
                    for step in range(steps_b(qb)):
                        if step == 1 and not (first and ul == 0):
                            normalise_b((ul - 1) % UNITS_B, done)
                        for item in ring_items_b(ul, step, first, last):
                            n = LEAD_B - SKIP + it * RING_B + k
                            slots[0] = LEAD_B - SKIP + k
                            k += 1
                            if item[0] == "max":
                                i, c = todo[item[1]]
                                take_max(sbb, n, i, c, BLK if c < nqb else (i + 1) * P, nqb + 1,
                                         item[1] == len(todo) - 1)
                            elif item[0] == "rows":
                                take_rows(sbb, n, MROW[:, (ul + 1) % 2, :])
                            elif item[0] == "project":
                                take_projected_b(item[1], n, (it * 2 + hs + 1) * 2 * BLOCKS + item[1])
                            elif item[0] == "turned":
                                take_turned(sbb, n)
                            else:
                                take_output(sbb, n, X, (qb - 1) % BLOCKS)
                    done = done + steps_b(qb)
                return k

            k = looped(body_b, ITER_B)
            n = LEAD_B - SKIP + (ITER_B - 1) * RING_B + k
            normalise_b(UNITS_B - 1, ITER_B * G_B)
            slots[0] = LEAD_B - SKIP + k
            take_turned(sbb, n)
            slots[0] += 1
            take_output(sbb, n + 1, X, BLOCKS - 1)
            dve.wait_ge(sbb.ring_taken, n + 2)
            ffn(1, 4 * BLOCKS)

        @block.tensor
        def _(pe):
            slots = [0]

            def turn_block(n, b, bank):
                for i in range(BT):
                    ins = pe.transpose(bank[:, i * P:(i + 1) * P], XN[:, b * BT + i, :], ident[:, :])
                ins.then_inc(xnt_put, 1)

            pe.wait_ge(consts, 1)
            pe.wait_ge(w_in, 80)
            for i in range(9):
                if i == 4:
                    pe.wait_ge(vw_in, 48)
                if i >= 4:
                    pe.wait_ge(wt_act if i % 2 == 0 else wt_dve, (i - 4) // 2 + 1)
                bank = QUARTER[i % 4]
                if i == 8:
                    ins = pe.transpose(bank[:, 0:HA], braw, ident[0:HA, 0:HA])
                else:
                    src = (wqk_raw, wqk_raw, wqk_raw, wqk_raw, wv_raw, wv_raw, wo_raw, wo_raw)[i]
                    at = (i if i < 4 else i % 2) * 4
                    for j in range(4):
                        ins = pe.transpose(bank[:, j * P:(j + 1) * P], src[:, at + j, :], ident[:, :])
                ins.then_inc(wt_put, 1)
            for b in range(BLOCKS):
                pe.wait_ge(xn_ready, b + 1)
                wait(pe, xnt_ready, b - 1)
                turn_block(b, b, O[b % 2])

            def claim(s, item):
                wait(pe, s.ring_taken, item - 1)
                return RING[slots[0] % 2]

            def project_a(hs, blk, item, head):
                bank = claim(sa, item)
                pe.wait_ge(sa.wst_ready, head + 1)
                pe.matmul(bank[:, :], WST[:, hs, 0:P], XNT[:, blk * BLK:(blk + 1) * BLK], start=True,
                          stop=True).then_inc(sa.ring_put, 1)

            def max_a(hs, qb, i, item, head):
                if i == 0 and qb == 0:
                    pe.wait_ge(sa.operands_ready, (head + 1) * BLOCKS)
                bank = claim(sa, item)
                qt, c = divmod(i, BLOCKS)
                at = qb * BLK + qt * P
                pe.matmul(bank[:, :], QL[hs][:, at:at + P], KH[hs][:, c * BLK:(c + 1) * BLK], start=True,
                          stop=True).then_inc(sa.ring_put, 1)

            def rows(s, item, unit):
                bank = claim(s, item)
                pe.wait_ge(s.max_ready, unit + 1)
                pe.transpose(bank[0:AUX, 0:P], negparts[:, :], ident[:, :]).then_inc(s.ring_put, 1)

            def turned(s, item, src, units_done):
                bank = claim(s, item)
                pe.wait_ge(s.o_taken, units_done)
                for i in range(BT):
                    ins = pe.transpose(bank[:, i * P:(i + 1) * P], src[:, i, :], ident[:, :])
                ins.then_inc(s.ring_put, 1)

            def output(s, item, w):
                bank = claim(s, item)
                pe.wait_ge(s.ring_taken, item)
                for i in range(BT):
                    ins = pe.matmul(bank[:, i * D:(i + 1) * D], AT[:, i * P:(i + 1) * P], w, start=True, stop=True)
                ins.then_inc(s.ring_put, 1)

            for blk in range(BLOCKS):
                pe.wait_ge(xnt_ready, blk + 1)
                slots[0] = blk
                project_a(0, blk, blk, 0)
            pe.wait_ge(wt_act, 5)
            pe.wait_ge(wt_dve, 4)
            for i in range(2 * TILES):
                wait(pe, v_dve, i - 3)
                pe.matmul(QUARTER[i % 4], XNT[:, i // 2 * P:(i // 2 + 1) * P], wvT[:, (i % 2) * BLK:(i % 2 + 1) * BLK],
                          start=True, stop=True).then_inc(v_put, 1)
            for i in range(16):
                slots[0] = BLOCKS + i
                max_a(0, 0, i, BLOCKS + i, 0)
            slots[0] = LEAD_A - 1
            rows(sa, LEAD_A - 1, 0)
            pe.wait_ge(v_dve, 2 * TILES)

            def pv_a(ul, step, g, head, j):
                if j == 0:
                    pe.wait_ge(sa.exps, g + 1)
                m = 2 * step + j
                for qt in range(BT):
                    ins = pe.matmul(O[ul % 2][:, qt * VA:(qt + 1) * VA],
                                    PR[:, step % 2, j * BLK + qt * P:j * BLK + (qt + 1) * P],
                                    V[:, m, bass.ds(head * VA, VA)],
                                    start=(m == 0 and qt == 0), stop=(m == TILES - 1), skip_group_check=True)
                if j == 1:
                    ins.then_inc(sa.pv, 1)

            def body_a(it, first=False, last=False):
                k = SKIP if first else 0
                before = None
                for ul in range(UNITS_A):
                    hs, qb = divmod(ul, BLOCKS)
                    nhs, nqb = divmod((ul + 1) % UNITS_A, BLOCKS)
                    u = it * UNITS_A + ul
                    head = it * 2 + hs
                    next_head = it * 2 + (ul + 1) // BLOCKS
                    q = slice(qb * BLK, (qb + 1) * BLK)
                    for step in range(STEPS_A):
                        g = it * G_A + ul * STEPS_A + step
                        if step == 0:
                            pe.wait_ge(sa.ring_taken, LEAD_A - SKIP + it * RING_A + k)
                        wait(pe, sa.exps, g - 1)
                        items = ring_items_a(ul, step, first, last)
                        place = 0

                        def ring_items(count):
                            nonlocal k, place
                            for item in items[place:place + count]:
                                n = LEAD_A - SKIP + it * RING_A + k
                                slots[0] = LEAD_A - SKIP + k
                                k += 1
                                if item[0] == "max":
                                    max_a(nhs, nqb, item[1], n, next_head)
                                elif item[0] == "rows":
                                    rows(sa, n, u + 1)
                                elif item[0] == "project":
                                    project_a(1 - hs, item[1], n, head + 1)
                                elif item[0] == "turned":
                                    pqb = (qb - 1) % BLOCKS
                                    turned(sa, n, A2[:, pqb * BT:(pqb + 1) * BT, :], u)
                                else:
                                    pair = it - 1 if ul == 0 else it
                                    output(sa, n, WoT[:, bass.ds(pair, 1), :].rearrange("p a c -> p (a c)"))
                            place += count

                        for j in range(2):
                            keys = slice((2 * step + j) * P, (2 * step + j + 1) * P)
                            tile = ST[step % 2][:, j * BLK:(j + 1) * BLK]
                            pe.matmul(tile, KH[hs][:, keys], QL[hs][:, q], start=True, stop=False)
                            ins = pe.matmul(tile, KL[hs][:, keys], QH[hs][:, q], start=False, stop=True)
                            if j == 0 and len(items) > 3:
                                ring_items(len(items) - 3)
                        ins.then_inc(sa.scores, 1)
                        ring_items(1)
                        if not (first and ul == 0 and step == 0):
                            pul, pstep = (ul, step - 1) if step else ((ul - 1) % UNITS_A, STEPS_A - 1)
                            phead = head if step or qb else head - 1
                            if pstep == 0:
                                wait(pe, sa.o_taken, u - 1)
                            pv_a(pul, pstep, g - 1, phead, 0)
                            ring_items(1)
                            pv_a(pul, pstep, g - 1, phead, 1)
                        ring_items(len(items) - place)
                return k

            body_a(0, first=True)
            with pe.Fori(1, ITER_A - 1) as it:
                body_a(it)
            k = body_a(ITER_A - 1, last=True)
            for j in range(2):
                pv_a(UNITS_A - 1, STEPS_A - 1, ITER_A * G_A - 1, HA - 1, j)
            n = LEAD_A - SKIP + (ITER_A - 1) * RING_A + k
            slots[0] = LEAD_A - SKIP + k
            turned(sa, n, A2[:, (BLOCKS - 1) * BT:BLOCKS * BT, :], ITER_A * UNITS_A)
            slots[0] += 1
            output(sa, n + 1, WoT[:, ITER_A - 1, :])
            pe.wait_ge(sa.ring_taken, n + 2)

            def hidden(r, b):
                pe.wait_ge(xnt_ready, (1 if r == 0 else 3) * BLOCKS + b + 1)
                for j in range(CH):
                    wait(pe, hid_ready, (r * BLOCKS + b - 1) * CH + j + 1)
                    pe.matmul(QUARTER[j], W1s[:, j * P:(j + 1) * P], XNT[:, b * BLK:(b + 1) * BLK], start=True,
                              stop=True).then_inc(hid_put, 1)

            def ffn(r, first_ln):
                pe.wait_ge(fw_in, 48)
                base = (1 if r == 0 else 3) * BLOCKS
                pe.wait_ge(xn_ready, base + 1)
                turn_block(base, 0, O[0])
                for b in range(BLOCKS):
                    hidden(r, b)
                    if b + 1 < BLOCKS:
                        pe.wait_ge(xn_ready, base + b + 2)
                        turn_block(base + b + 1, b + 1, O[(b + 1) % 2])
                    wait(pe, x_ready, r * BLOCKS + b - 1)
                    pe.wait_ge(hid_ready, (r * BLOCKS + b + 1) * CH)
                    for i in range(BT):
                        for j in range(CH):
                            ins = pe.matmul(RING[b % 2][:, i * D:(i + 1) * D], HID[:, j, i * P:(i + 1) * P],
                                            W2s[:, j, :], start=(j == 0), stop=(j == CH - 1))
                    ins.then_inc(ffn_put, 1)

            ffn(0, 2)

            for b in range(BLOCKS):
                pe.wait_ge(xn_ready, 2 * BLOCKS + b + 1)
                wait(pe, xnt_ready, 2 * BLOCKS + b - 1)
                turn_block(2 * BLOCKS + b, b, O[b % 2])
            pe.wait_ge(bweights, 16 * 6)
            pe.wait_ge(x_ready, BLOCKS)
            pe.wait_ge(xnt_ready, 3 * BLOCKS)
            for i in range(2 * TILES):
                if i >= 4:
                    if i % 2 == 0:
                        pe.wait_ge(v_act, (i - 4) // 2 + 1)
                    else:
                        pe.wait_ge(v_dve, 2 * TILES + (i - 4) // 2 + 1)
                pe.matmul(QUARTER[i % 4], XNT[:, i // 2 * P:(i // 2 + 1) * P], wav[:, (i % 2) * BLK:(i % 2 + 1) * BLK],
                          start=True, stop=True).then_inc(v_put, 1)

            def project_b(hs, j, item, head):
                bank = claim(sbb, item)
                pe.wait_ge(sbb.wst_ready, head + 1)
                blk = j // 2
                pe.matmul(bank[:, :], WST[:, hs, (j % 2) * DB:(j % 2 + 1) * DB], XNT[:, blk * BLK:(blk + 1) * BLK],
                          start=True, stop=True).then_inc(sbb.ring_put, 1)

            def max_b(hs, qb, i, c, item, head, first_of_head):
                if first_of_head:
                    pe.wait_ge(sbb.operands_ready, (head + 1) * 2 * BLOCKS)
                bank = claim(sbb, item)
                width = BLK if c < qb else (i + 1) * P
                at = qb * BLK + i * P
                if c == qb:
                    pe.matmul(bank[:, i * P:(i + 1) * P], ident_r[:, :], later_keys[:, :], start=True, stop=True)
                pe.matmul(bank[:, 0:width], QH[hs][:, at:at + P], KH[hs][:, c * BLK:c * BLK + width],
                          start=(c < qb), stop=True, skip_group_check=True).then_inc(sbb.ring_put, 1)

            for j in range(2 * BLOCKS):
                slots[0] = j
                project_b(0, j, j, 0)
            for i in range(BT):
                slots[0] = 2 * BLOCKS + i
                max_b(0, 0, i, 0, 2 * BLOCKS + i, 0, i == 0)
            slots[0] = LEAD_B - 1
            rows(sbb, LEAD_B - 1, 0)
            pe.wait_ge(v_act, TILES)
            pe.wait_ge(v_dve, 3 * TILES)

            def pv_b(ul, step, g, head, half):
                qb = ul % BLOCKS
                if half == 0:
                    pe.wait_ge(sbb.exps, g + 1)
                for qt in range(max(2 * half, step - BT * qb), 2 * half + 2):
                    bank, at = (OB[ul % 2][0], qt * VB) if qt < 3 else (OB[ul % 2][1], 0)
                    ins = pe.matmul(bank[:, at:at + VB], PRB[:, step % 2, qt * P:(qt + 1) * P],
                                    V[:, step, bass.ds(head * VB, VB)], start=(step == 0 and qt in (0, 3)),
                                    stop=(step == BT * qb + qt), skip_group_check=True)
                if half == 1:
                    ins.then_inc(sbb.pv, 1)

            def body_b(it, first=False, last=False):
                k = SKIP if first else 0
                g = it * G_B
                for ul in range(UNITS_B):
                    hs, qb = divmod(ul, BLOCKS)
                    nhs, nqb = divmod((ul + 1) % UNITS_B, BLOCKS)
                    u = it * UNITS_B + ul
                    head = it * 2 + hs
                    next_head = it * 2 + (ul + 1) // BLOCKS
                    todo = max_items_b(nqb)
                    for step in range(steps_b(qb)):
                        if step == 0:
                            pe.wait_ge(sbb.ring_taken, LEAD_B - SKIP + it * RING_B + k)
                        wait(pe, sbb.exps, g - 1)
                        keys = slice(step * P, (step + 1) * P)
                        c0 = max(0, step - BT * qb) * P
                        q = slice(qb * BLK + c0, (qb + 1) * BLK)
                        tile = SB[step % 2][:, c0:BLK]
                        diagonal = step >= BT * qb
                        if diagonal:
                            pe.matmul(SB[step % 2][:, c0:c0 + P], ident_r[:, :], later_keys_t[:, :],
                                      start=True, stop=True)
                        pe.matmul(tile, KH[hs][:, keys], QH[hs][:, q], start=not diagonal, stop=False,
                                  skip_group_check=True)
                        pe.matmul(tile, KL[hs][:, keys], QH[hs][:, q], start=False, stop=False,
                                  skip_group_check=True)
                        pe.matmul(tile, KH[hs][:, keys], QL[hs][:, q], start=False, stop=False,
                                  skip_group_check=True)
                        pe.matmul(tile, ones_r[:, :], MROW[:, ul % 2, c0:BLK], start=False, stop=True,
                                  skip_group_check=True).then_inc(sbb.scores, 1)
                        items = ring_items_b(ul, step, first, last)
                        place = 0

                        def ring_items(count):
                            nonlocal k, place
                            for item in items[place:place + count]:
                                n = LEAD_B - SKIP + it * RING_B + k
                                slots[0] = LEAD_B - SKIP + k
                                k += 1
                                if item[0] == "max":
                                    i, c = todo[item[1]]
                                    max_b(nhs, nqb, i, c, n, next_head, item[1] == 0 and nqb == 0)
                                elif item[0] == "rows":
                                    rows(sbb, n, u + 1)
                                elif item[0] == "project":
                                    project_b(1 - hs, item[1], n, head + 1)
                                elif item[0] == "turned":
                                    turned(sbb, n, AB, u)
                                else:
                                    phead = head if qb else head - 1
                                    output(sbb, n, WAO[:, bass.ds(phead, 1), :].rearrange("p a c -> p (a c)"))
                            place += count

                        ring_items(1)
                        if not (first and ul == 0 and step == 0):
                            pul, pstep = (ul, step - 1) if step else ((ul - 1) % UNITS_B, steps_b((qb - 1) % BLOCKS) - 1)
                            phead = head if step or qb else head - 1
                            if step == 1:
                                wait(pe, sbb.o_taken, u - 1)
                            pv_b(pul, pstep, g - 1, phead, 0)
                            ring_items(1)
                            pv_b(pul, pstep, g - 1, phead, 1)
                        ring_items(len(items) - place)
                        g = g + 1
                return k

            body_b(0, first=True)
            with pe.Fori(1, ITER_B - 1) as it:
                body_b(it)
            k = body_b(ITER_B - 1, last=True)
            for half in range(2):
                pv_b(UNITS_B - 1, TILES - 1, ITER_B * G_B - 1, HB - 1, half)
            n = LEAD_B - SKIP + (ITER_B - 1) * RING_B + k
            slots[0] = LEAD_B - SKIP + k
            turned(sbb, n, AB, ITER_B * UNITS_B)
            slots[0] += 1
            output(sbb, n + 1, WAO[:, HB - 1, :])
            pe.wait_ge(sbb.ring_taken, n + 2)
            ffn(1, 4)


def rope_tables():
    half = DB // 2
    freqs = np.power(np.float32(10000.0), -np.arange(half, dtype=np.float32) / np.float32(half)).astype(np.float32)
    radians = np.arange(T, dtype=np.float32)[None, :] * freqs[:, None]
    cos, sin = np.cos(radians), np.sin(radians)
    return (np.concatenate([cos, cos]).astype(np.float32), np.concatenate([-sin, sin]).astype(np.float32))


_INS = ['L0_attn_a_x', 'L0_attn_a_adaptive_scale', 'L0_attn_a_Wq', 'L0_attn_a_bq', 'L0_attn_a_Wk', 'L0_attn_a_bk',
        'L0_attn_a_Wv', 'L0_attn_a_bv', 'L0_attn_a_Wo', 'L0_attn_a_bo', 'L0_attn_a_gamma', 'L0_attn_a_beta',
        'L0_attn_b_w_aq', 'L0_attn_b_w_ak', 'L0_attn_b_w_av', 'L0_attn_b_w_ao', 'L0_ffn_W1', 'L0_ffn_b1',
        'L0_ffn_W2', 'L0_ffn_b2']


def kernel(**inputs):
    import concourse.bacc as bacc
    from concourse.bass_utils import run_bass_kernel_spmd

    nc = bacc.Bacc("TRN2", target_bir_lowering=False, num_devices=1)
    cos, sin = rope_tables()
    arrays, args = {}, []
    for name, a in [*((n, inputs[n]) for n in _INS), ("rope_cos", cos), ("rope_sin", sin)]:
        a = np.ascontiguousarray(a)
        arrays[f"in_{name}"] = a
        args.append(nc.dram_tensor(f"in_{name}", a.shape, mybir.dt.from_np(a.dtype), kind="ExternalInput").ap())
    args.append(nc.dram_tensor("out_0", (1, T, D), F32, kind="ExternalOutput").ap())
    build(nc, *args)
    r = run_bass_kernel_spmd(nc, [arrays], core_ids=[0])
    return r.results[0]["out_0"]
```

```python
from contextlib import ExitStack

import numpy as np

import concourse.bass as bass
from concourse import mybir

F32 = mybir.dt.float32
F32R = mybir.dt.float32r
F16 = mybir.dt.float16
BF16 = mybir.dt.bfloat16
ALU = mybir.AluOpType
ACT = mybir.ActivationFunctionType
X_AXIS = mybir.AxisListType.X

P = 128
T = 2048
D = 128
TILES = T // P
BLK = 512
BLOCKS = T // BLK
BT = BLK // P
EPS = 1e-5

HA, DA = 16, 64
VA = DA + 1
SCALE_A = DA ** -0.5
ITER_A = HA // 2
UNITS_A = 2 * BLOCKS
STEPS_A = TILES // 2
G_A = UNITS_A * STEPS_A
SLOTS_A = 4
LAG_A = 2
LOW_BY_DVE = (1, 4, 7)
HEAD_STEPS = (1, 5)
PIECES = ((0, 1), (2,), (3,), (4,))
WV_AT = 2 * DA + 2
BV_AT = WV_AT + DA
WCOL = BV_AT + DA
V2_AT = DA + 2
V3_AT = V2_AT + DA
VCOL = V3_AT + DA

HB, DB = 8, 128
VB = DB + 1
ITER_B = HB // 2
UNITS_B = 2 * BLOCKS
MASKED = -1e30
INTER = 512
CH = INTER // P

LIFT = 2.0 ** 8
AUX = 2 * BT


def steps_b(qb):
    return BT * (qb + 1)


G_B = 2 * sum(steps_b(q) for q in range(BLOCKS))


def ring_items_a(ul, step, first, last):
    hs, qb = divmod(ul, BLOCKS)
    items = []
    has_next = not (last and ul == UNITS_A - 1)
    if has_next:
        at = [0, 3, 5, 7, 10, 12, 14, 16, 16]
        items += [("max", i) for i in range(at[step], at[step + 1])]
    if ((ul - 1) % UNITS_A) // BLOCKS == 1 and not (first and ul == 0):
        items += [("turned",)] if step == 3 else [("output",)] if step == 4 else []
    if not (last and hs == 1) and qb < 3 and step in HEAD_STEPS:
        part = HEAD_STEPS.index(step)
        items += [("project", 2 * qb + part)] if qb < 2 else [("values", part)]
    if has_next and step == STEPS_A - 1:
        items += [("rows",)]
    return items


def after_a(ul, step, delay, first, last):
    at = ul * STEPS_A + step - delay
    if at < 0:
        return ()
    before = ring_items_a(at // STEPS_A, at % STEPS_A, first, last)
    return next((item for item in before if item[0] in ("project", "values")), ())


def max_items_b(qb):
    return [(i, c) for i in range(BT) for c in range(qb + 1)]


VALUES_B = {(2, 4): 0, (2, 7): 1, (2, 10): 2, (3, 9): 3}
PROJECT_B = {(1, 5): [0], (2, 3): [1], (2, 6): [2], (2, 9): [3], (3, 1): [4], (3, 3): [5], (3, 5): [6], (3, 8): [7]}
MAXIMA_B = {0: [(2, 0, 4, 0, 4)], 1: [(2, 4, 12, 0, 4)], 2: [(3, 0, 16, 0, 8)],
            3: [(0, 0, 4, 2, 6), (1, 0, 8, 7, 15)]}


def ring_items_b(ul, step, first, last):
    hs, qb = divmod(ul, BLOCKS)
    next_qb = (qb + 1) % BLOCKS
    next_head = not (last and hs == 1)
    items = []
    if step == steps_b(qb) - 3 and (next_qb or next_head):
        items += [("spread", next_qb)]
    for target, lo, hi, begin, end in MAXIMA_B[qb]:
        if target < qb and not next_head:
            continue
        if begin <= step < end:
            a, b = (lo + (hi - lo) * (step - begin + d) // (end - begin) for d in (0, 1))
            items += [("max", target, j) for j in range(a, b)]
        if step == end % steps_b(qb) and hi == len(max_items_b(target)):
            items += [("rows", target)]
    if not (first and ul == 0):
        items += [("turned",)] if step == 2 else [("output",)] if step == 3 else []
    if next_head:
        items += [("project", b) for b in PROJECT_B.get((qb, step), [])]
        items += [("values", VALUES_B[qb, step])] if (qb, step) in VALUES_B else []
    return items


def target_unit(ul, target):
    hs, qb = divmod(ul, BLOCKS)
    return (hs + (target < qb)) * BLOCKS + target


def count_items(items_of, units, steps_of, last=False):
    return sum(len(items_of(ul, s, False, last)) for ul in range(units) for s in range(steps_of(ul)))


RING_A = count_items(ring_items_a, UNITS_A, lambda ul: STEPS_A)
RING_B = count_items(ring_items_b, UNITS_B, lambda ul: steps_b(ul % BLOCKS))
RING_A_LAST = count_items(ring_items_a, UNITS_A, lambda ul: STEPS_A, last=True)
assert RING_A % 2 == 0 and RING_B % 2 == 0
LEAD_A = BLOCKS + 2 + 16 + 1
LEAD_B = 2 * BLOCKS + BLOCKS + (BT + 1) + (2 * BT + 1) + 1
SKIP = 2
END_A = LEAD_A - SKIP + (ITER_A - 1) * RING_A + RING_A_LAST + 2


def build(nc, x, adaptive_scale, Wq, bq, Wk, bk, Wv, bv, Wo, bo, gamma, beta,
          w_aq, w_ak, w_av, w_ao, W1, b1, W2, b2, rope_cos, rope_sin, out):
    ctx = ExitStack()
    with ctx:
        def sb(name, shape, dt=F32):
            return ctx.enter_context(nc.sbuf_tensor(name, shape, dt))

        def pb(name, shape):
            return ctx.enter_context(nc.psum_tensor(name, shape, F32))

        def sem(name):
            return ctx.enter_context(nc.semaphore(name))

        X = sb("X", [P, TILES, D])
        XN = sb("XN", [P, TILES, D])
        XNT = sb("XNT", [P, T])
        VP = sb("VP", [P, 2, TILES, VCOL], BF16)
        PAB = sb("PAB", [P, 2 * TILES * VB])
        RAW = sb("RAW", [P, 4 * HA * DA])
        PR = sb("PR", [P, 2, 2 * BLK])
        VF = sb("VF", [P, 2, BLK])
        F = sb("F", [P, 2, BLK])
        WST = sb("WST", [P, 2, 3 * DB])
        AT = sb("AT", [P, BLK])
        AB = sb("AB", [P, BT, DB])
        SHARED = sb("SHARED", [P, max(HA * WCOL + 8 * D + T, 2 * T + HB * D)])
        W1s = sb("W1s", [P, INTER])
        W2s = sb("W2s", [P, CH, D])
        ident = sb("ident", [P, P])
        rowmask = sb("rowmask", [AUX, BT, P])
        bo_b = sb("bo_b", [P, D])
        gamma_b = sb("gamma_b", [P, D])
        beta_b = sb("beta_b", [P, D])
        b2_b = sb("b2_b", [P, D])
        b1c = sb("b1c", [P, CH])
        eps = sb("eps", [P, 1])
        lift = sb("lift", [P, 1])
        stats = sb("stats", [P, BT, 6])
        meanvar = sb("meanvar", [P, BT, 2])
        std = sb("std", [P, BT])
        rstd = sb("rstd", [P, BT])
        maxes = sb("maxes", [P, BT, BLOCKS])
        negmax = sb("negmax", [P, BT])
        negparts = sb("negparts", [P, AUX])
        rden = sb("rden", [P, BT])
        KH = [sb(f"KH{i}", [P, T], F32R) for i in range(2)]
        KL = [sb(f"KL{i}", [P, T], F32R) for i in range(2)]
        QH = [sb(f"QH{i}", [P, T], F32R) for i in range(2)]
        QL = [sb(f"QL{i}", [P, T], F32R) for i in range(2)]
        ident_r = sb("ident_r", [P, P], F32R)
        later_keys = sb("later_keys", [P, P], F32R)
        later_keys_t = sb("later_keys_t", [P, P], F32R)
        ones_r = sb("ones_r", [AUX, P], F32R)
        MROW = sb("MROW", [AUX, 2, BLK], F32R)

        wqk_raw = RAW[:, 0:HA * P].rearrange("p (h c) -> p h c", c=P)
        wv_raw = RAW[:, HA * P:HA * P + HA * DA].rearrange("p (j c) -> p j c", c=P)
        wo_raw = RAW[:, HA * P + HA * DA:HA * P + 2 * HA * DA].rearrange("p (j c) -> p j c", c=P)
        braw = F[0:HA, 1, 0:P]
        sraw = F[0:DA, 1, P:P + HA]
        WQK = SHARED[:, 0:HA * WCOL].rearrange("p (h c) -> p h c", c=WCOL)
        WoT = SHARED[:, HA * WCOL:HA * WCOL + 8 * D].rearrange("p (j c) -> p j c", c=D)
        A2 = SHARED[:, HA * WCOL + 8 * D:HA * WCOL + 8 * D + T].rearrange("p (t c) -> p t c", c=D)
        COS = SHARED[:, 0:T]
        SIN = SHARED[:, T:2 * T]
        WAO = SHARED[:, 2 * T:2 * T + HB * D].rearrange("p (h c) -> p h c", c=D)
        WQKB = RAW[:, 0:HB * 2 * DB].rearrange("p (h a c) -> p h a c", a=2, c=DB)
        WVB = RAW[:, HB * 2 * DB:HB * 3 * DB].rearrange("p (h c) -> p h c", c=DB)
        half_ab = SLOTS_A * BLK
        PA = PAB[:, 0:half_ab].bitcast(F16).rearrange("p (s q) -> p s q", s=SLOTS_A)
        PB = PAB[:, half_ab:2 * half_ab].bitcast(F16).rearrange("p (s q) -> p s q", s=SLOTS_A)
        VBS = PAB[:, :].rearrange("p (a t c) -> p a t c", a=2, c=VB)
        PRB = PR[:, 0, :].rearrange("p (s q) -> p s q", s=2)
        MB = VF
        SWAP = PR[:, 1, :].rearrange("p (s q) -> p s q", s=2)
        HID = PR[:, :, :].rearrange("p a (b q) -> p (a b) q", b=2)
        mask_raw = F[:, 0, 0:2 * P].rearrange("p (a c) -> p a c", a=2)

        ST = [pb(f"ST{i}", [P, 2 * BLK]) for i in range(2)]
        RING = [pb(f"RING{i}", [P, BLK]) for i in range(2)]
        O = [pb(f"O{i}", [P, BLK]) for i in range(2)]
        QUARTER = [ST[i // 2][:, (i % 2) * BLK:(i % 2 + 1) * BLK] for i in range(4)]
        SB = [QUARTER[0], QUARTER[1]]
        OB = [(O[0], QUARTER[2]), (O[1], QUARTER[3])]

        x_in = [sem(f"x_in{b}") for b in range(BLOCKS)]
        w_in = sem("w_in")
        vw_in = sem("vw_in")
        c_in = sem("c_in")
        fw_in = sem("fw_in")
        consts = sem("consts")
        const_r = sem("const_r")
        chain = sem("chain")
        pchain = sem("pchain")
        var_ready = sem("var_ready")
        std_ready = sem("std_ready")
        xn_ready = sem("xn_ready")
        xnt_put = sem("xnt_put")
        xnt_ready = sem("xnt_ready")
        wt_put = sem("wt_put")
        wt_act = sem("wt_act")
        wt_dve = sem("wt_dve")
        ones_set = sem("ones_set")
        k_low = sem("k_low")
        p_low_pool = sem("p_low_pool")
        p_low_dve = sem("p_low_dve")
        v_high = sem("v_high")
        v_rest = sem("v_rest")
        v_ready = sem("v_ready")
        xbo = sem("xbo")
        bweights = sem("bweights")
        hid_put = sem("hid_put")
        hid_ready = sem("hid_ready")
        ffn_put = sem("ffn_put")
        x_ready = sem("x_ready")
        out_done = sem("out_done")

        class Phase:
            pass

        def phase(n):
            s = Phase()
            s.wst_ready = sem(f"wst_ready_{n}")
            s.ring_put = sem(f"ring_put_{n}")
            s.ring_taken = sem(f"ring_taken_{n}")
            s.rope_summed = sem(f"rope_summed_{n}")
            s.high_ready = sem(f"high_ready_{n}")
            s.operands_ready = sem(f"operands_ready_{n}")
            s.max_ready = sem(f"max_ready_{n}")
            s.scores = sem(f"scores_{n}")
            s.filled = sem(f"filled_{n}")
            s.primed = sem(f"primed_{n}")
            s.exps = sem(f"exps_{n}")
            s.pv = sem(f"pv_{n}")
            s.o_taken = sem(f"o_taken_{n}")
            return s

        sa, sbb = phase("a"), phase("b")

        def wait(eng, s, value):
            if not isinstance(value, int) or value > 0:
                eng.wait_ge(s, value)

        block = ctx.enter_context(nc.Block())

        @block.sync
        def _(sp):
            xin = x[0].rearrange("(t p) c -> p t c", p=P)
            for b in range(BLOCKS):
                sp.dma_start(X[:, b * BT:(b + 1) * BT, :], xin[:, b * BT:(b + 1) * BT, :]).then_inc(x_in[b], 16)
            sp.dma_start(wqk_raw[0:DA, :, :], Wq.rearrange("(h d) c -> d h c", d=DA)).then_inc(w_in, 16)
            sp.dma_start(wqk_raw[DA:P, :, :], Wk.rearrange("(h d) c -> d h c", d=DA)).then_inc(w_in, 16)
            sp.dma_start(braw[:, 0:DA], bq.rearrange("(h d) -> h d", d=DA)).then_inc(w_in, 16)
            sp.dma_start(braw[:, DA:P], bk.rearrange("(h d) -> h d", d=DA)).then_inc(w_in, 16)
            sp.dma_start(sraw, adaptive_scale.partition_broadcast(DA)).then_inc(w_in, 16)
            sp.dma_start(wv_raw, Wv.rearrange("(j p) c -> p j c", p=P)).then_inc(vw_in, 16)
            sp.dma_start(wo_raw, Wo.rearrange("p (j c) -> p j c", c=P)).then_inc(vw_in, 16)
            sp.dma_start(WQK[:, :, BV_AT:WCOL], bv.rearrange("(h d) -> h d", d=DA).partition_broadcast(P)
                         ).then_inc(vw_in, 16)
            for dst, src in ((bo_b, bo), (gamma_b, gamma), (beta_b, beta), (b2_b, b2)):
                sp.dma_start(dst[:, :], src.partition_broadcast(P)).then_inc(c_in, 16)
            sp.dma_start(b1c[:, :], b1.rearrange("(j p) -> p j", p=P), allow_slow_non_contiguous=True).then_inc(fw_in, 16)
            sp.dma_start(W1s[:, :], W1).then_inc(fw_in, 16)
            sp.dma_start(W2s[:, :, :], W2.rearrange("(j p) n -> p j n", p=P)).then_inc(fw_in, 16)
            wait(sp, wt_put, 8)
            sp.dma_start(WQKB[:, :, 0, :], w_aq).then_inc(bweights, 16)
            sp.dma_start(WQKB[:, :, 1, :], w_ak).then_inc(bweights, 16)
            sp.dma_start(WVB, w_av).then_inc(bweights, 16)
            wait(sp, sa.ring_taken, END_A)
            sp.dma_start(COS, rope_cos).then_inc(bweights, 16)
            sp.dma_start(SIN, rope_sin).then_inc(bweights, 16)
            sp.dma_start(WAO, w_ao.rearrange("h d m -> d h m")).then_inc(bweights, 16)
            oout = out[0].rearrange("(t p) c -> p t c", p=P)
            for b in range(BLOCKS):
                wait(sp, x_ready, BLOCKS + b + 1)
                sp.dma_start(oout[:, b * BT:(b + 1) * BT, :], X[:, b * BT:(b + 1) * BT, :]).then_inc(out_done, 16)
            wait(sp, out_done, 16 * BLOCKS)

        @block.gpsimd
        def _(pool):
            tick = [0]

            def link(ins):
                tick[0] += 1
                ins.then_inc(pchain, 1)
                pool.wait_ge(pchain, tick[0])

            link(pool.memset(ident[:, :], 0.0))
            pool.affine_select(out=ident[:, :], in_=ident[:, :], compare_op=ALU.not_equal, fill=1.0, base=0,
                               pattern=[[-1, P]], channel_multiplier=1).then_inc(consts, 1)
            link(pool.memset(mask_raw, 0.0))
            pool.affine_select(out=mask_raw[:, 0, :], in_=mask_raw[:, 0, :], compare_op=ALU.is_ge, fill=MASKED,
                               base=0, pattern=[[-1, P]], channel_multiplier=1)
            pool.affine_select(out=mask_raw[:, 1, :], in_=mask_raw[:, 1, :], compare_op=ALU.is_ge, fill=MASKED,
                               base=0, pattern=[[1, P]], channel_multiplier=-1).then_inc(consts, 1)
            link(pool.memset(rowmask[:, :, :], 0.0))
            for half in range(2):
                ins = pool.affine_select(out=rowmask[:, :, :], in_=rowmask[:, :, :], compare_op=ALU.not_equal,
                                         fill=1.0, base=-half * BT, pattern=[[-1, BT], [0, P]],
                                         channel_multiplier=1)
                if half == 0:
                    link(ins)
            ins.then_inc(consts, 1)
            pool.wait_ge(wt_act, 5)
            pool.wait_ge(wt_dve, 5)
            pool.tensor_copy(WST[:, 0, 0:WCOL], WQK[:, 0, :]).then_inc(sa.wst_ready, 1)
            pool.memset(VP[:, :, :, DA:DA + 1], 1.0).then_inc(ones_set, 1)

            def q_low(hs, blk, index):
                pool.wait_ge(sa.high_ready, index * 5 + 2)
                at = QL[hs][0:DA, blk * BLK:(blk + 1) * BLK]
                pool.tensor_tensor(at, F[0:DA, blk % 2, :], at.bitcast(F32), ALU.subtract
                                   ).then_inc(sa.operands_ready, 1)

            def values_rest(hs, half, index):
                vp = VP[:, hs, half * 8:half * 8 + 8, :]
                vf = VF[:, half, :].rearrange("p (t c) -> p t c", c=DA)
                pool.wait_ge(v_high, 2 * index + 1)
                pool.tensor_tensor(vf, vf, vp[:, :, 0:DA], ALU.subtract).then_inc(v_rest, 1)

            def values_third(hs, half, index):
                vp = VP[:, hs, half * 8:half * 8 + 8, :]
                vf = VF[:, half, :].rearrange("p (t c) -> p t c", c=DA)
                pool.wait_ge(v_high, 2 * index + 2)
                pool.tensor_tensor(vp[:, :, V3_AT:VCOL], vf, vp[:, :, V2_AT:V3_AT], ALU.subtract
                                   ).then_inc(v_ready, 1)

            def p_low(step, g):
                pool.wait_ge(sa.exps, g + 1)
                wait(pool, sa.pv, g - SLOTS_A + 1)
                s = step % SLOTS_A
                pool.tensor_tensor(PB[:, s, :], PR[:, step % 2, :], PA[:, s, :], ALU.subtract
                                   ).then_inc(p_low_pool, 1)

            for blk in range(BLOCKS):
                q_low(0, blk, blk)
            for half in range(2):
                values_rest(0, half, half)
                values_third(0, half, half)
            pool.wait_ge(c_in, 64)
            pool.wait_ge(xnt_put, BLOCKS)
            pool.tensor_tensor(XN[:, :, :], XN[:, :, :], bo_b[:, :].unsqueeze(1).broadcast_to((P, TILES, D)),
                               ALU.add).then_inc(xbo, 1)
            pool.tensor_tensor(X[:, :, :], X[:, :, :], beta_b[:, :].unsqueeze(1).broadcast_to((P, TILES, D)),
                               ALU.add).then_inc(xbo, 1)

            def turn_a(it, first=False, last=False):
                for ul in range(UNITS_A):
                    hs, qb = divmod(ul, BLOCKS)
                    head = it * 2 + hs + 1
                    if qb == 0 and not (last and hs == 1):
                        pool.tensor_copy(WST[:, 1 - hs, 0:WCOL], WQK[:, bass.ds(head, 1), :].rearrange(
                            "p a c -> p (a c)")).then_inc(sa.wst_ready, 1)
                    for step in range(STEPS_A):
                        two, three = (after_a(ul, step, d, first, last) for d in (2, 3))
                        if two and two[0] == "project":
                            q_low(1 - hs, two[1], head * BLOCKS + two[1])
                        elif two:
                            values_rest(1 - hs, two[1], head * 2 + two[1])
                        if three and three[0] == "values":
                            values_third(1 - hs, three[1], head * 2 + three[1])
                        if step not in LOW_BY_DVE:
                            p_low(step, it * G_A + ul * STEPS_A + step)

            turn_a(0, first=True)
            with pool.Fori(1, ITER_A - 1) as it:
                turn_a(it)
            turn_a(ITER_A - 1, last=True)

            pool.wait_ge(bweights, 16 * 6)
            pool.wait_ge(sa.pv, ITER_A * G_A)
            pool.memset(VBS[:, :, :, DB:VB], 1.0).then_inc(ones_set, 1)

            def stage_b(par, head):
                pool.tensor_copy(WST[:, par, 0:2 * DB], WQKB[:, bass.ds(head, 1), :, :].rearrange(
                    "p z a c -> p (z a c)"))
                pool.tensor_copy(WST[:, par, 2 * DB:3 * DB], WVB[:, bass.ds(head, 1), :].rearrange(
                    "p z c -> p (z c)")).then_inc(sbb.wst_ready, 1)

            stage_b(0, 0)

            def rope_and_low_b(hs, j, index, item):
                pool.wait_ge(sbb.ring_taken, item + 1)
                s = j % 2
                q = slice(j // 2 * BLK, (j // 2 + 1) * BLK)
                high, low = ((QH, QL), (KH, KL))[j % 2]
                pool.tensor_tensor(F[:, s, :], F[:, s, :], SWAP[:, s, :], ALU.add).then_inc(sbb.rope_summed, 1)
                pool.wait_ge(sbb.high_ready, index + 1)
                pool.tensor_tensor(low[hs][:, q], F[:, s, :], high[hs][:, q].bitcast(F32),
                                   ALU.subtract).then_inc(sbb.operands_ready, 1)

            for j in range(2 * BLOCKS):
                rope_and_low_b(0, j, j, j)

            def heads_b(it, first=False, last=False):
                k = SKIP if first else 0
                for ul in range(UNITS_B):
                    hs, qb = divmod(ul, BLOCKS)
                    head = it * 2 + hs + 1
                    if qb == 0 and not (last and hs == 1):
                        stage_b(1 - hs, head)
                    for step in range(steps_b(qb)):
                        for item in ring_items_b(ul, step, first, last):
                            if item[0] == "project":
                                rope_and_low_b(1 - hs, item[1], head * 2 * BLOCKS + item[1],
                                               LEAD_B - SKIP + it * RING_B + k)
                            k += 1

            heads_b(0, first=True)
            with pool.Fori(1, ITER_B - 1) as it:
                heads_b(it)
            heads_b(ITER_B - 1, last=True)

        @block.scalar
        def _(act):
            def deviations(n):
                act.wait_ge(var_ready, n + 1)
                act.activation(std[:, :], meanvar[:, :, 1], ACT.Sqrt, bias=eps[:, :]).then_inc(std_ready, 1)

            def transposed_block(n, bank, free=None):
                act.wait_ge(xnt_put, n + 1)
                b = n % BLOCKS
                act.activation(XNT[:, b * BLK:(b + 1) * BLK], bank, ACT.Copy).then_inc(xnt_ready, 1)

            act.wait_ge(const_r, 1)
            for b in range(BLOCKS):
                deviations(b)
            for i in range(0, 9, 2):
                act.wait_ge(wt_put, i + 1)
                bank = QUARTER[i % 4]
                src4 = bank.rearrange("p (a c) -> p a c", c=P)
                if i < 4:
                    ins = act.activation(WQK[:, i * 4:i * 4 + 4, 0:P], src4, ACT.Copy)
                elif i < 6:
                    ins = act.activation(WQK[:, 0:8, WV_AT:BV_AT], bank.rearrange("p (a c) -> p a c", c=DA), ACT.Copy)
                elif i < 8:
                    ins = act.activation(WoT[:, (i - 6) * 4:(i - 6) * 4 + 4, :], src4, ACT.Copy)
                else:
                    ins = act.activation(WQK[:, :, P], bank[:, 0:HA], ACT.Copy)
                ins.then_inc(wt_act, 1)
            for b in range(BLOCKS):
                transposed_block(b, O[b % 2][:, :])

            def high_parts_a(hs, blk, item, scores_before, pieces):
                act.wait_ge(sa.ring_taken, item + 1)
                wait(act, sa.scores, scores_before)
                q = slice(blk * BLK, (blk + 1) * BLK)
                f = F[:, blk % 2, :]
                places = ((KH[hs], DA, DA), (QL[hs], 0, 0), (KH[hs], 0, DA), (QL[hs], DA, 0), (QH[hs], DA, 0))
                for i in pieces:
                    dst, to, at = places[i]
                    act.activation(dst[to:to + DA, q], f[at:at + DA, :], ACT.Copy).then_inc(sa.high_ready, 1)

            def values_first(hs, half, item):
                vp = VP[:, hs, half * 8:half * 8 + 8, :]
                vf = VF[:, half, :].rearrange("p (t c) -> p t c", c=DA)
                act.wait_ge(sa.ring_taken, item + 1)
                act.activation(vp[:, :, 0:DA], vf, ACT.Copy).then_inc(v_high, 1)

            def values_second(hs, half, index):
                act.wait_ge(v_rest, index + 1)
                act.activation(VP[:, hs, half * 8:half * 8 + 8, V2_AT:V3_AT],
                               VF[:, half, :].rearrange("p (t c) -> p t c", c=DA), ACT.Copy).then_inc(v_high, 1)

            for blk in range(BLOCKS):
                high_parts_a(0, blk, blk, 0, range(5))
            for half in range(2):
                values_first(0, half, BLOCKS + half)
                values_second(0, half, half)

            def low_taken(g, ul, step, it):
                before = ul * STEPS_A + step - 2
                if isinstance(it, int) and it * G_A + before < 0:
                    return
                by_dve = before % STEPS_A in LOW_BY_DVE
                s, per_unit = (p_low_dve, len(LOW_BY_DVE)) if by_dve else (p_low_pool, STEPS_A - len(LOW_BY_DVE))
                units, at = divmod(before, STEPS_A)
                count = units * per_unit + sum((i in LOW_BY_DVE) == by_dve for i in range(at + 1))
                act.wait_ge(s, it * (UNITS_A * per_unit) + count)

            def exps_a(it, first=False, last=False):
                k = SKIP if first else 0
                numbers = {}
                for ul in range(UNITS_A):
                    hs, qb = divmod(ul, BLOCKS)
                    for step in range(STEPS_A):
                        g = it * G_A + ul * STEPS_A + step
                        low_taken(g, ul, step, it)
                        act.wait_ge(sa.scores, g + 1)
                        act.activation(PR[:, step % 2, :], ST[step % 2][:, :], ACT.Exp, bias=lift[:, :])
                        wait(act, sa.pv, g - SLOTS_A + 1)
                        act.activation(PA[:, step % SLOTS_A, :], ST[step % 2][:, :], ACT.Exp, bias=lift[:, :]
                                       ).then_inc(sa.exps, 1)
                        head = it * 2 + hs + 1
                        for delay, pieces in enumerate(PIECES, 1):
                            item = after_a(ul, step, delay, first, last)
                            if item and item[0] == "project":
                                high_parts_a(1 - hs, item[1], LEAD_A - SKIP + it * RING_A + numbers[item],
                                             (head - 1) * BLOCKS * STEPS_A, pieces)
                            elif item and delay == 1:
                                values_first(1 - hs, item[1], LEAD_A - SKIP + it * RING_A + numbers[item])
                            elif item and delay == 2:
                                values_second(1 - hs, item[1], head * 2 + item[1])
                        for item in ring_items_a(ul, step, first, last):
                            numbers[item] = k
                            k += 1

            exps_a(0, first=True)
            with act.Fori(1, ITER_A - 1) as it:
                exps_a(it)
            exps_a(ITER_A - 1, last=True)

            def relus(r, b):
                for j in range(CH):
                    n = (r * BLOCKS + b) * CH + j
                    act.wait_ge(hid_put, n + 1)
                    wait(act, ffn_put, r * BLOCKS + b)
                    act.activation(HID[:, j, :], QUARTER[j], ACT.Relu, bias=b1c[:, j:j + 1]).then_inc(hid_ready, 1)

            def ffn(r, first_ln):
                deviations(first_ln)
                for b in range(BLOCKS):
                    if b + 1 < BLOCKS:
                        deviations(first_ln + b + 1)
                    transposed_block((1 if r == 0 else 3) * BLOCKS + b, O[b % 2][:, :])
                    relus(r, b)

            for b in range(BLOCKS):
                deviations(BLOCKS + b)
            act.wait_ge(fw_in, 48)
            ffn(0, 2 * BLOCKS)

            for b in range(BLOCKS):
                deviations(3 * BLOCKS + b)
                transposed_block(2 * BLOCKS + b, O[b % 2][:, :])

            def high_part_b(hs, j, index, scores_before):
                act.wait_ge(sbb.rope_summed, index + 1)
                wait(act, sbb.scores, scores_before)
                q = slice(j // 2 * BLK, (j // 2 + 1) * BLK)
                high = (QH, KH)[j % 2]
                act.activation(high[hs][:, q], F[:, j % 2, :], ACT.Copy).then_inc(sbb.high_ready, 1)

            for j in range(2 * BLOCKS):
                high_part_b(0, j, j, 0)

            def fill(parity, slot, c0):
                act.activation(SB[parity][:, c0:BLK], MB[:, slot, c0:BLK], ACT.Copy).then_inc(sbb.filled, 1)

            act.wait_ge(sbb.primed, 1)
            act.wait_ge(sbb.ring_taken, LEAD_B)
            for step in range(2):
                fill(step, 0, step * P)

            def exps_b(it, first=False, last=False):
                k = SKIP if first else 0
                g = it * G_B
                todo = []
                for ul in range(UNITS_B):
                    hs, qb = divmod(ul, BLOCKS)
                    n = steps_b(qb)
                    spread = None
                    for step in range(n):
                        c0 = max(0, step - BT * qb) * P
                        act.wait_ge(sbb.scores, g + 1)
                        wait(act, sbb.pv, g - 1)
                        act.activation(PRB[:, step % 2, c0:BLK], SB[step % 2][:, c0:BLK], ACT.Exp,
                                       scale=1.0 / DB).then_inc(sbb.exps, 1)
                        g = g + 1
                        for item in ring_items_b(ul, step, first, last):
                            if item[0] == "spread":
                                spread = LEAD_B - SKIP + it * RING_B + k
                            k += 1
                        if step + 2 < n or spread is not None:
                            act.wait_ge(sbb.exps, g)
                        if step + 2 < n:
                            fill(step % 2, ul % 2, max(0, step + 2 - BT * qb) * P)
                        elif spread is not None:
                            if step + 2 == n:
                                act.wait_ge(sbb.ring_taken, spread + 1)
                            after = step + 2 - n
                            fill(step % 2, (ul + 1) % 2, after * P if qb == BLOCKS - 1 else 0)
                        for args in todo:
                            high_part_b(*args)
                        todo = [(1 - hs, item[1], (it * 2 + hs + 1) * 2 * BLOCKS + item[1],
                                 (it * 2 + hs) * (G_B // 2))
                                for item in ring_items_b(ul, step, first, last) if item[0] == "project"]

            exps_b(0, first=True)
            with act.Fori(1, ITER_B - 1) as it:
                exps_b(it)
            exps_b(ITER_B - 1, last=True)
            ffn(1, 4 * BLOCKS)

        @block.vector
        def _(dve):
            tick = [0]
            loop_base = [None]

            def link(ins):
                ins.then_inc(chain, 1)
                tick[0] += 1
                dve.wait_ge(chain, tick[0] if loop_base[0] is None else loop_base[0] + tick[0])

            def layer_norm(n, b, src, dst, signal=True):
                for i in range(BT):
                    ins = dve.bn_stats(stats[:, i, :], src[:, b * BT + i, :])
                link(ins)
                for i in range(BT):
                    ins = dve.bn_aggr(meanvar[:, i, :], stats[:, i, :])
                ins.then_inc(var_ready, 1)
                dve.wait_ge(std_ready, n + 1)
                link(dve.reciprocal(rstd[:, :], std[:, :]))
                for i in range(BT):
                    ins = dve.tensor_scalar(dst[:, b * BT + i, :], src[:, b * BT + i, :], meanvar[:, i, 0:1],
                                            rstd[:, i:i + 1], ALU.subtract, ALU.mult)
                if signal:
                    ins.then_inc(xn_ready, 1)
                else:
                    link(ins)

            dve.memset(eps[:, :], EPS)
            dve.memset(lift[:, :], float(np.log(LIFT)))
            for i in range(2):
                dve.memset(QH[i][0:DA, :].bitcast(F32), 0.0)
                link(dve.memset(KL[i][0:DA, :].bitcast(F32), 0.0))
                dve.memset(KL[i][0:AUX, :].bitcast(F32), 1.0)
            dve.memset(ones_r[:, :].bitcast(F32), 1.0).then_inc(const_r, 1)
            for b in range(BLOCKS):
                dve.wait_ge(x_in[b], 16)
                layer_norm(b, b, X, XN)
            dve.wait_ge(consts, 3)
            dve.tensor_copy(ident_r[:, :], ident[:, :])
            dve.tensor_copy(later_keys[:, :], mask_raw[:, 0, :])
            dve.tensor_copy(later_keys_t[:, :], mask_raw[:, 1, :]).then_inc(const_r, 1)
            for i in range(1, 8, 2):
                dve.wait_ge(wt_put, i + 1)
                bank = QUARTER[i % 4]
                src4 = bank.rearrange("p (a c) -> p a c", c=P)
                if i < 4:
                    ins = dve.tensor_copy(WQK[:, i * 4:i * 4 + 4, 0:P], src4)
                elif i < 6:
                    ins = dve.tensor_copy(WQK[:, 8:HA, WV_AT:BV_AT], bank.rearrange("p (a c) -> p a c", c=DA))
                else:
                    ins = dve.tensor_copy(WoT[:, (i - 6) * 4:(i - 6) * 4 + 4, :], src4)
                ins.then_inc(wt_dve, 1)
            dve.wait_ge(w_in, 80)
            dve.memset(WQK[DA:P, :, P + 1], 1.0)
            dve.tensor_scalar(WQK[0:DA, :, P + 1], sraw, SCALE_A, None, ALU.mult).then_inc(wt_dve, 1)

            def take_projected_a(hs, blk, bank, item, index):
                dve.wait_ge(sa.ring_put, item + 1)
                wait(dve, sa.operands_ready, index - 1)
                wait(dve, sa.high_ready, (index - 1) * 5)
                wait(dve, k_low, index - 1)
                dve.tensor_scalar(F[:, blk % 2, :], bank[:, :], WST[:, hs, P:P + 1],
                                  WST[:, hs, P + 1:P + 2], ALU.add, ALU.mult).then_inc(sa.ring_taken, 1)

            def take_k_low(hs, blk, index):
                dve.wait_ge(sa.high_ready, index * 5 + 1)
                q = slice(blk * BLK, (blk + 1) * BLK)
                dve.tensor_tensor(KL[hs][DA:P, q], F[DA:P, blk % 2, :], KH[hs][DA:P, q].bitcast(F32),
                                  ALU.subtract).then_inc(k_low, 1)

            def take_values_a(hs, half, bank, item, index):
                dve.wait_ge(sa.ring_put, item + 1)
                wait(dve, v_ready, index - 1)
                dve.tensor_tensor(VF[:, half, :].rearrange("p (t c) -> p t c", c=DA),
                                  bank[:, :].rearrange("p (t c) -> p t c", c=DA),
                                  WST[:, hs, BV_AT:WCOL].unsqueeze(1).broadcast_to((P, 8, DA)),
                                  ALU.add).then_inc(sa.ring_taken, 1)

            def take_p_low(step, g):
                dve.wait_ge(sa.exps, g + 1)
                wait(dve, sa.pv, g - SLOTS_A + 1)
                s = step % SLOTS_A
                dve.tensor_tensor(PB[:, s, :], PR[:, step % 2, :], PA[:, s, :], ALU.subtract
                                  ).then_inc(p_low_dve, 1)

            def take_max(s, bank, item, qt, c, width, chunks, last):
                dve.wait_ge(s.ring_put, item + 1)
                dve.reduce_max(maxes[:, qt, c:c + 1], bank[:, 0:width], X_AXIS).then_inc(s.ring_taken, 1)
                if last:
                    dve.wait_ge(s.ring_taken, item + 1)
                    link(dve.tensor_reduce(negmax[:, :], maxes[:, :, 0:chunks], X_AXIS, ALU.max, negate=True))
                    link(dve.tensor_copy(negparts[:, 0:BT].bitcast(F32R), negmax[:, :]))
                    dve.tensor_tensor(negparts[:, BT:AUX], negmax[:, :], negparts[:, 0:BT],
                                      ALU.subtract).then_inc(s.max_ready, 1)

            def take_rows(s, bank, item, dst):
                dve.wait_ge(s.ring_put, item + 1)
                rows = bank[0:AUX, 0:P].unsqueeze(1).broadcast_to((AUX, BT, P))
                dve.tensor_tensor(dst.rearrange("p (a c) -> p a c", c=P), rows, rowmask[:, :, :],
                                  ALU.mult).then_inc(s.ring_taken, 1)

            def take_turned(s, bank, item):
                dve.wait_ge(s.ring_put, item + 1)
                dve.tensor_copy(AT[:, :], bank[:, :]).then_inc(s.ring_taken, 1)

            def take_output(s, bank, item, acc, qb):
                dve.wait_ge(s.ring_put, item + 1)
                a = acc[:, qb * BT:(qb + 1) * BT, :]
                dve.tensor_tensor(a, a, bank[:, :].rearrange("p (a c) -> p a c", c=D),
                                  ALU.add).then_inc(s.ring_taken, 1)

            def normalise_a(ul, units_done):
                hs, qb = divmod(ul, BLOCKS)
                dve.wait_ge(sa.pv, units_done * STEPS_A)
                o = O[ul % 2][:, 0:BT * VA].rearrange("p (a c) -> p a c", c=VA)
                link(dve.reciprocal(rden[:, :], o[:, :, DA]))
                dve.tensor_tensor(A2[:, qb * BT:(qb + 1) * BT, hs * DA:(hs + 1) * DA], o[:, :, 0:DA],
                                  rden[:, :].unsqueeze(2).broadcast_to((P, BT, DA)), ALU.mult
                                  ).then_inc(sa.o_taken, 1)

            for blk in range(BLOCKS):
                take_projected_a(0, blk, RING[blk % 2], blk, blk)
                if blk:
                    take_k_low(0, blk - 1, blk - 1)
            take_k_low(0, BLOCKS - 1, BLOCKS - 1)
            for half in range(2):
                take_values_a(0, half, RING[(BLOCKS + half) % 2], BLOCKS + half, half)
            for i in range(16):
                n = BLOCKS + 2 + i
                take_max(sa, RING[n % 2], n, i // 4, i % 4, BLK, BLOCKS, i == 15)
            take_rows(sa, RING[(LEAD_A - 1) % 2], LEAD_A - 1, QH[0][0:AUX, 0:BLK])
            dve.wait_ge(xbo, 2)

            def body_a(it, first=False, last=False):
                k = SKIP if first else 0
                for ul in range(UNITS_A):
                    hs, qb = divmod(ul, BLOCKS)
                    nhs, nqb = divmod((ul + 1) % UNITS_A, BLOCKS)
                    u = it * UNITS_A + ul
                    index = (it * 2 + hs + 1) * BLOCKS
                    for step in range(STEPS_A):
                        if step == LAG_A and not (first and ul == 0):
                            normalise_a((ul - 1) % UNITS_A, u)
                        two = after_a(ul, step, 2, first, last)
                        if two and two[0] == "project":
                            take_k_low(1 - hs, two[1], index + two[1])
                        late = (step - 1) % STEPS_A in LOW_BY_DVE and not (first and ul == 0 and step == 0)
                        for i, item in enumerate(ring_items_a(ul, step, first, last)):
                            n = LEAD_A - SKIP + it * RING_A + k
                            bank = RING[(LEAD_A - SKIP + k) % 2]
                            k += 1
                            if item[0] == "max":
                                j = item[1]
                                take_max(sa, bank, n, j // 4, j % 4, BLK, BLOCKS, j == 15)
                            elif item[0] == "rows":
                                take_rows(sa, bank, n, QH[nhs][0:AUX, nqb * BLK:(nqb + 1) * BLK])
                            elif item[0] == "project":
                                take_projected_a(1 - hs, item[1], bank, n, index + item[1])
                            elif item[0] == "values":
                                take_values_a(1 - hs, item[1], bank, n, (it * 2 + hs + 1) * 2 + item[1])
                            elif item[0] == "turned":
                                take_turned(sa, bank, n)
                            else:
                                take_output(sa, bank, n, XN, (qb - 1) % BLOCKS)
                            if i == 0 and late:
                                take_p_low((step - 1) % STEPS_A, it * G_A + ul * STEPS_A + step - 1)
                                late = False
                        if late:
                            take_p_low((step - 1) % STEPS_A, it * G_A + ul * STEPS_A + step - 1)
                return k

            def looped(body, turns):
                before = tick[0]
                loop_base[0] = None
                body(0, first=True)
                start = tick[0]
                with dve.Fori(1, turns - 1) as it:
                    tick[0] = 0
                    loop_base[0] = (it - 1) * links_of[body.__name__] + start
                    body(it)
                    assert tick[0] == links_of[body.__name__], (body.__name__, tick[0])
                loop_base[0] = None
                tick[0] = start + (turns - 2) * links_of[body.__name__]
                return body(turns - 1, last=True)

            links_of = {"body_a": 3 * UNITS_A, "body_b": 3 * UNITS_B}

            looped(body_a, ITER_A)
            take_p_low(STEPS_A - 1, ITER_A * G_A - 1)
            normalise_a(UNITS_A - 1, ITER_A * UNITS_A)
            take_turned(sa, RING[(END_A - 2) % 2], END_A - 2)
            take_output(sa, RING[(END_A - 1) % 2], END_A - 1, XN, BLOCKS - 1)
            dve.wait_ge(sa.ring_taken, END_A)

            for b in range(BLOCKS):
                layer_norm(BLOCKS + b, b, XN, XN, signal=False)
                y = XN[:, b * BT:(b + 1) * BT, :]
                a = X[:, b * BT:(b + 1) * BT, :]
                link(dve.tensor_tensor(y, y, gamma_b[:, :].unsqueeze(1).broadcast_to((P, BT, D)), ALU.mult))
                link(dve.tensor_tensor(a, a, y, ALU.add))

            def take_ffn(r, b):
                dve.wait_ge(ffn_put, r * BLOCKS + b + 1)
                a = X[:, b * BT:(b + 1) * BT, :]
                link(dve.tensor_tensor(a, a, RING[b % 2][:, :].rearrange("p (a c) -> p a c", c=D), ALU.add))
                dve.tensor_tensor(a, a, b2_b[:, :].unsqueeze(1).broadcast_to((P, BT, D)), ALU.add
                                  ).then_inc(x_ready, 1)

            def ffn(r, first_ln):
                layer_norm(first_ln, 0, X, XN)
                for b in range(BLOCKS):
                    if b + 1 < BLOCKS:
                        layer_norm(first_ln + b + 1, b + 1, X, XN)
                    take_ffn(r, b)

            ffn(0, 2 * BLOCKS)

            for b in range(BLOCKS):
                dve.wait_ge(x_ready, b + 1)
                layer_norm(3 * BLOCKS + b, b, X, XN)

            def take_projected_b(j, bank, item, index):
                dve.wait_ge(sbb.ring_put, item + 1)
                wait(dve, sbb.operands_ready, index - 1)
                s, r = j % 2, bank
                q = slice(j // 2 * BLK, (j // 2 + 1) * BLK)
                half = DB // 2
                dve.tensor_tensor(F[:, s, :], r[:, :], COS[:, q], ALU.mult)
                dve.tensor_tensor(SWAP[0:half, s, :], r[half:P, :], SIN[0:half, q], ALU.mult)
                dve.tensor_tensor(SWAP[half:P, s, :], r[0:half, :], SIN[half:P, q], ALU.mult
                                  ).then_inc(sbb.ring_taken, 1)

            def normalise_b(ul, steps_done):
                dve.wait_ge(sbb.pv, steps_done)
                three, fourth = OB[ul % 2]
                o = three[:, 0:3 * VB].rearrange("p (a c) -> p a c", c=VB)
                dve.reciprocal(rden[:, 0:3], o[:, :, DB])
                link(dve.reciprocal(rden[:, 3:4], fourth[:, DB:VB]))
                dve.tensor_tensor(AB[:, 0:3, :], o[:, :, 0:DB], rden[:, 0:3].unsqueeze(2).broadcast_to((P, 3, DB)),
                                  ALU.mult)
                dve.tensor_scalar(AB[:, 3, :], fourth[:, 0:DB], rden[:, 3:4], None, ALU.mult
                                  ).then_inc(sbb.o_taken, 1)

            def take_values_b(hs, part, bank, item):
                dve.wait_ge(sbb.ring_put, item + 1)
                dve.tensor_copy(VBS[:, hs, part * BT:(part + 1) * BT, 0:DB],
                                bank[:, :].rearrange("p (t c) -> p t c", c=DB)).then_inc(sbb.ring_taken, 1)

            dve.wait_ge(bweights, 16 * 6)
            for j in range(2 * BLOCKS):
                take_projected_b(j, RING[j % 2], j, j)
            for part in range(BLOCKS):
                n = 2 * BLOCKS + part
                take_values_b(0, part, RING[n % 2], n)
            for i in range(BT):
                n = 3 * BLOCKS + i
                take_max(sbb, RING[n % 2], n, i, 0, (i + 1) * P, 1, i == BT - 1)
            take_rows(sbb, RING[(n + 1) % 2], n + 1, MROW[:, 0, :])
            for i, (qt, c) in enumerate(max_items_b(1)):
                n = LEAD_B - 2 - 2 * BT + i
                take_max(sbb, RING[n % 2], n, qt, c, BLK if c < 1 else (qt + 1) * P, 2, i == 2 * BT - 1)
            take_rows(sbb, RING[(LEAD_B - 2) % 2], LEAD_B - 2, MROW[:, 1, :])

            def take_spread(slot, bank, item, steps_before):
                dve.wait_ge(sbb.ring_put, item + 1)
                wait(dve, sbb.filled, steps_before)
                dve.tensor_copy(MB[:, slot, :], bank[:, :]).then_inc(sbb.ring_taken, 1)

            take_spread(0, RING[(LEAD_B - 1) % 2], LEAD_B - 1, 0)

            def body_b(it, first=False, last=False):
                k = SKIP if first else 0
                done = it * G_B
                for ul in range(UNITS_B):
                    hs, qb = divmod(ul, BLOCKS)
                    nqb = (qb + 1) % BLOCKS
                    u = it * UNITS_B + ul
                    todo = max_items_b(nqb)
                    for step in range(steps_b(qb)):
                        if step == 1 and not (first and ul == 0):
                            normalise_b((ul - 1) % UNITS_B, done)
                        for item in ring_items_b(ul, step, first, last):
                            n = LEAD_B - SKIP + it * RING_B + k
                            bank = RING[(LEAD_B - SKIP + k) % 2]
                            k += 1
                            if item[0] == "max":
                                target = item[1]
                                todo = max_items_b(target)
                                i, c = todo[item[2]]
                                take_max(sbb, bank, n, i, c, BLK if c < target else (i + 1) * P, target + 1,
                                         item[2] == len(todo) - 1)
                            elif item[0] == "rows":
                                take_rows(sbb, bank, n, MROW[:, item[1] % 2, :])
                            elif item[0] == "spread":
                                take_spread(item[1] % 2, bank, n, done)
                            elif item[0] == "project":
                                take_projected_b(item[1], bank, n, (it * 2 + hs + 1) * 2 * BLOCKS + item[1])
                            elif item[0] == "values":
                                take_values_b(1 - hs, item[1], bank, n)
                            elif item[0] == "turned":
                                take_turned(sbb, bank, n)
                            else:
                                take_output(sbb, bank, n, X, (qb - 1) % BLOCKS)
                    done = done + steps_b(qb)
                return k

            k = looped(body_b, ITER_B)
            n = LEAD_B - SKIP + (ITER_B - 1) * RING_B + k
            normalise_b(UNITS_B - 1, ITER_B * G_B)
            take_turned(sbb, RING[n % 2], n)
            take_output(sbb, RING[(n + 1) % 2], n + 1, X, BLOCKS - 1)
            dve.wait_ge(sbb.ring_taken, n + 2)
            ffn(1, 4 * BLOCKS)

        @block.tensor
        def _(pe):
            def turn_block(n, b, bank):
                for i in range(BT):
                    ins = pe.transpose(bank[:, i * P:(i + 1) * P], XN[:, b * BT + i, :], ident[:, :])
                ins.then_inc(xnt_put, 1)

            pe.wait_ge(consts, 1)
            pe.wait_ge(w_in, 80)
            for i in range(9):
                if i == 4:
                    pe.wait_ge(vw_in, 48)
                if i >= 4:
                    pe.wait_ge(wt_act if i % 2 == 0 else wt_dve, (i - 4) // 2 + 1)
                bank = QUARTER[i % 4]
                if i == 8:
                    ins = pe.transpose(bank[:, 0:HA], braw, ident[0:HA, 0:HA])
                else:
                    src = (wqk_raw, wqk_raw, wqk_raw, wqk_raw, wv_raw, wv_raw, wo_raw, wo_raw)[i]
                    at = (i if i < 4 else i % 2) * 4
                    for j in range(4):
                        ins = pe.transpose(bank[:, j * P:(j + 1) * P], src[:, at + j, :], ident[:, :])
                ins.then_inc(wt_put, 1)
            for b in range(BLOCKS):
                pe.wait_ge(xn_ready, b + 1)
                wait(pe, xnt_ready, b - 1)
                turn_block(b, b, O[b % 2])

            def claim(s, item):
                wait(pe, s.ring_taken, item - 1)

            def project_a(hs, blk, bank, item, head):
                claim(sa, item)
                pe.wait_ge(sa.wst_ready, head + 1)
                pe.matmul(bank[:, :], WST[:, hs, 0:P], XNT[:, blk * BLK:(blk + 1) * BLK], start=True,
                          stop=True).then_inc(sa.ring_put, 1)

            def values_a(hs, half, bank, item, head):
                claim(sa, item)
                for t in range(8):
                    m = half * 8 + t
                    ins = pe.matmul(bank[:, t * DA:(t + 1) * DA], XNT[:, m * P:(m + 1) * P],
                                    WST[:, hs, WV_AT:BV_AT], start=True, stop=True)
                ins.then_inc(sa.ring_put, 1)

            def max_a(hs, qb, i, bank, item, head):
                if i == 0 and qb == 0:
                    pe.wait_ge(sa.operands_ready, (head + 1) * BLOCKS)
                    pe.wait_ge(k_low, (head + 1) * BLOCKS)
                    pe.wait_ge(sa.high_ready, (head + 1) * BLOCKS * 5)
                claim(sa, item)
                qt, c = divmod(i, BLOCKS)
                at = qb * BLK + qt * P
                pe.matmul(bank[:, :], QL[hs][:, at:at + P], KH[hs][:, c * BLK:(c + 1) * BLK], start=True,
                          stop=True).then_inc(sa.ring_put, 1)

            def rows(s, bank, item, unit):
                claim(s, item)
                pe.wait_ge(s.max_ready, unit + 1)
                pe.transpose(bank[0:AUX, 0:P], negparts[:, :], ident[:, :]).then_inc(s.ring_put, 1)

            def turned(s, bank, item, src, units_done):
                claim(s, item)
                pe.wait_ge(s.o_taken, units_done)
                for i in range(BT):
                    ins = pe.transpose(bank[:, i * P:(i + 1) * P], src[:, i, :], ident[:, :])
                ins.then_inc(s.ring_put, 1)

            def output(s, bank, item, w):
                claim(s, item)
                pe.wait_ge(s.ring_taken, item)
                for i in range(BT):
                    ins = pe.matmul(bank[:, i * D:(i + 1) * D], AT[:, i * P:(i + 1) * P], w, start=True, stop=True)
                ins.then_inc(s.ring_put, 1)

            pe.wait_ge(wt_act, 5)
            pe.wait_ge(wt_dve, 5)
            for blk in range(BLOCKS):
                pe.wait_ge(xnt_ready, blk + 1)
                project_a(0, blk, RING[blk % 2], blk, 0)
            for half in range(2):
                values_a(0, half, RING[(BLOCKS + half) % 2], BLOCKS + half, 0)
            for i in range(16):
                n = BLOCKS + 2 + i
                max_a(0, 0, i, RING[n % 2], n, 0)
            rows(sa, RING[(LEAD_A - 1) % 2], LEAD_A - 1, 0)

            def pv_a(ul, step, unit, j):
                if j == 0:
                    by_dve = step in LOW_BY_DVE
                    s, per_unit = ((p_low_dve, len(LOW_BY_DVE)) if by_dve
                                   else (p_low_pool, STEPS_A - len(LOW_BY_DVE)))
                    pe.wait_ge(s, unit * per_unit + sum((i in LOW_BY_DVE) == by_dve for i in range(step + 1)))
                m = 2 * step + j
                hs = ul // BLOCKS
                v = VP[:, hs, m, :]
                for qt in range(BT):
                    at = j * BLK + qt * P
                    high, low = PA[:, step % SLOTS_A, at:at + P], PB[:, step % SLOTS_A, at:at + P]
                    both = O[ul % 2][:, qt * VA:(qt + 1) * VA]
                    o = O[ul % 2][:, qt * VA:qt * VA + DA]
                    pe.matmul(both, high, v[:, 0:VA], start=(m == 0 and qt == 0), stop=False, skip_group_check=True)
                    pe.matmul(o, high, v[:, V2_AT:V3_AT], start=False, stop=False, skip_group_check=True)
                    pe.matmul(o, high, v[:, V3_AT:VCOL], start=False, stop=False, skip_group_check=True)
                    pe.matmul(o, low, v[:, V2_AT:V3_AT], start=False, stop=False, skip_group_check=True)
                    ins = pe.matmul(both, low, v[:, 0:VA], start=False, stop=(m == TILES - 1), skip_group_check=True)
                if j == 1:
                    ins.then_inc(sa.pv, 1)

            def body_a(it, first=False, last=False):
                k = SKIP if first else 0
                before = None
                for ul in range(UNITS_A):
                    hs, qb = divmod(ul, BLOCKS)
                    nhs, nqb = divmod((ul + 1) % UNITS_A, BLOCKS)
                    u = it * UNITS_A + ul
                    head = it * 2 + hs
                    next_head = it * 2 + (ul + 1) // BLOCKS
                    q = slice(qb * BLK, (qb + 1) * BLK)
                    for step in range(STEPS_A):
                        g = it * G_A + ul * STEPS_A + step
                        if step == 0:
                            pe.wait_ge(sa.ring_taken, LEAD_A - SKIP + it * RING_A + k)
                        wait(pe, sa.exps, g - 1)
                        items = ring_items_a(ul, step, first, last)
                        place = 0

                        def ring_items(count):
                            nonlocal k, place
                            for item in items[place:place + count]:
                                n = LEAD_A - SKIP + it * RING_A + k
                                bank = RING[(LEAD_A - SKIP + k) % 2]
                                k += 1
                                if item[0] == "max":
                                    max_a(nhs, nqb, item[1], bank, n, next_head)
                                elif item[0] == "rows":
                                    rows(sa, bank, n, u + 1)
                                elif item[0] == "project":
                                    project_a(1 - hs, item[1], bank, n, head + 1)
                                elif item[0] == "values":
                                    values_a(1 - hs, item[1], bank, n, head + 1)
                                elif item[0] == "turned":
                                    pqb = (qb - 1) % BLOCKS
                                    turned(sa, bank, n, A2[:, pqb * BT:(pqb + 1) * BT, :], u)
                                else:
                                    pair = it - 1 if ul == 0 else it
                                    output(sa, bank, n, WoT[:, bass.ds(pair, 1), :].rearrange("p a c -> p (a c)"))
                            place += count

                        for j in range(2):
                            keys = slice((2 * step + j) * P, (2 * step + j + 1) * P)
                            tile = ST[step % 2][:, j * BLK:(j + 1) * BLK]
                            pe.matmul(tile, KH[hs][:, keys], QL[hs][:, q], start=True, stop=False)
                            ins = pe.matmul(tile, KL[hs][:, keys], QH[hs][:, q], start=False, stop=True)
                            if j == 0 and len(items) > 3:
                                ring_items(len(items) - 3)
                        ins.then_inc(sa.scores, 1)
                        ring_items(1)
                        if not (first and ul == 0 and step < LAG_A):
                            same = step >= LAG_A
                            pul, pstep = (ul if same else (ul - 1) % UNITS_A), (step - LAG_A) % STEPS_A
                            if pstep == 0:
                                wait(pe, sa.o_taken, u - 1)
                                if qb == 0:
                                    pe.wait_ge(v_ready, head * 2 + 2)
                            pv_a(pul, pstep, u if same else u - 1, 0)
                            ring_items(1)
                            pv_a(pul, pstep, u if same else u - 1, 1)
                        ring_items(len(items) - place)
                return k

            body_a(0, first=True)
            with pe.Fori(1, ITER_A - 1) as it:
                body_a(it)
            body_a(ITER_A - 1, last=True)
            for step in range(STEPS_A - LAG_A, STEPS_A):
                for j in range(2):
                    pv_a(UNITS_A - 1, step, ITER_A * UNITS_A - 1, j)
            turned(sa, RING[(END_A - 2) % 2], END_A - 2, A2[:, (BLOCKS - 1) * BT:BLOCKS * BT, :], ITER_A * UNITS_A)
            output(sa, RING[(END_A - 1) % 2], END_A - 1, WoT[:, ITER_A - 1, :])
            pe.wait_ge(sa.ring_taken, END_A)

            def hidden(r, b):
                pe.wait_ge(xnt_ready, (1 if r == 0 else 3) * BLOCKS + b + 1)
                for j in range(CH):
                    wait(pe, hid_ready, (r * BLOCKS + b - 1) * CH + j + 1)
                    pe.matmul(QUARTER[j], W1s[:, j * P:(j + 1) * P], XNT[:, b * BLK:(b + 1) * BLK], start=True,
                              stop=True).then_inc(hid_put, 1)

            def ffn(r, first_ln):
                pe.wait_ge(fw_in, 48)
                base = (1 if r == 0 else 3) * BLOCKS
                pe.wait_ge(xn_ready, base + 1)
                turn_block(base, 0, O[0])
                for b in range(BLOCKS):
                    hidden(r, b)
                    if b + 1 < BLOCKS:
                        pe.wait_ge(xn_ready, base + b + 2)
                        turn_block(base + b + 1, b + 1, O[(b + 1) % 2])
                    wait(pe, x_ready, r * BLOCKS + b - 1)
                    pe.wait_ge(hid_ready, (r * BLOCKS + b + 1) * CH)
                    for i in range(BT):
                        for j in range(CH):
                            ins = pe.matmul(RING[b % 2][:, i * D:(i + 1) * D], HID[:, j, i * P:(i + 1) * P],
                                            W2s[:, j, :], start=(j == 0), stop=(j == CH - 1))
                    ins.then_inc(ffn_put, 1)

            ffn(0, 2)

            for b in range(BLOCKS):
                pe.wait_ge(xn_ready, 2 * BLOCKS + b + 1)
                wait(pe, xnt_ready, 2 * BLOCKS + b - 1)
                turn_block(2 * BLOCKS + b, b, O[b % 2])
            pe.wait_ge(bweights, 16 * 6)
            pe.wait_ge(x_ready, BLOCKS)
            pe.wait_ge(xnt_ready, 3 * BLOCKS)

            def project_b(hs, j, bank, item, head):
                claim(sbb, item)
                pe.wait_ge(sbb.wst_ready, head + 1)
                blk = j // 2
                pe.matmul(bank[:, :], WST[:, hs, (j % 2) * DB:(j % 2 + 1) * DB], XNT[:, blk * BLK:(blk + 1) * BLK],
                          start=True, stop=True).then_inc(sbb.ring_put, 1)

            def values_b(hs, part, bank, item, head):
                claim(sbb, item)
                for t in range(BT):
                    m = part * BT + t
                    ins = pe.matmul(bank[:, t * DB:(t + 1) * DB], XNT[:, m * P:(m + 1) * P],
                                    WST[:, hs, 2 * DB:3 * DB], start=True, stop=True)
                ins.then_inc(sbb.ring_put, 1)

            def max_b(hs, qb, i, c, bank, item, head):
                if (i, c) == (0, 0):
                    pe.wait_ge(sbb.operands_ready, head * 2 * BLOCKS + 2 * (qb + 1))
                claim(sbb, item)
                width = BLK if c < qb else (i + 1) * P
                at = qb * BLK + i * P
                if c == qb:
                    pe.matmul(bank[:, i * P:(i + 1) * P], ident_r[:, :], later_keys[:, :], start=True, stop=True)
                pe.matmul(bank[:, 0:width], QH[hs][:, at:at + P], KH[hs][:, c * BLK:c * BLK + width],
                          start=(c < qb), stop=True, skip_group_check=True).then_inc(sbb.ring_put, 1)

            for j in range(2 * BLOCKS):
                project_b(0, j, RING[j % 2], j, 0)
            for part in range(BLOCKS):
                n = 2 * BLOCKS + part
                values_b(0, part, RING[n % 2], n, 0)
            for i in range(BT):
                n = 3 * BLOCKS + i
                max_b(0, 0, i, 0, RING[n % 2], n, 0)
            rows(sbb, RING[(n + 1) % 2], n + 1, 0)
            for i, (qt, c) in enumerate(max_items_b(1)):
                n = LEAD_B - 2 - 2 * BT + i
                max_b(0, 1, qt, c, RING[n % 2], n, 0)
            rows(sbb, RING[(LEAD_B - 2) % 2], LEAD_B - 2, 1)

            def spread(slot, bank, item):
                claim(sbb, item)
                pe.wait_ge(sbb.ring_taken, item)
                pe.matmul(bank[:, :], ones_r[:, :], MROW[:, slot, :], start=True, stop=True
                          ).then_inc(sbb.ring_put, 1)

            spread(0, RING[(LEAD_B - 1) % 2], LEAD_B - 1)
            for i in range(2):
                ins = pe.matmul(SB[i][:, :], ones_r[:, :], MROW[:, 0, :], start=True, stop=True)
            ins.then_inc(sbb.primed, 1)
            pe.wait_ge(ones_set, 2)

            def pv_b(ul, step, g, half):
                qb = ul % BLOCKS
                if half == 0:
                    pe.wait_ge(sbb.exps, g + 1)
                for qt in range(max(2 * half, step - BT * qb), 2 * half + 2):
                    bank, at = (OB[ul % 2][0], qt * VB) if qt < 3 else (OB[ul % 2][1], 0)
                    ins = pe.matmul(bank[:, at:at + VB], PRB[:, step % 2, qt * P:(qt + 1) * P],
                                    VBS[:, ul // BLOCKS, step, :], start=(step == 0 and qt in (0, 3)),
                                    stop=(step == BT * qb + qt), skip_group_check=True)
                if half == 1:
                    ins.then_inc(sbb.pv, 1)

            def body_b(it, first=False, last=False):
                k = SKIP if first else 0
                g = it * G_B
                for ul in range(UNITS_B):
                    hs, qb = divmod(ul, BLOCKS)
                    nhs, nqb = divmod((ul + 1) % UNITS_B, BLOCKS)
                    u = it * UNITS_B + ul
                    head = it * 2 + hs
                    for step in range(steps_b(qb)):
                        pe.wait_ge(sbb.filled, g + 1)
                        keys = slice(step * P, (step + 1) * P)
                        c0 = max(0, step - BT * qb) * P
                        q = slice(qb * BLK + c0, (qb + 1) * BLK)
                        tile = SB[step % 2][:, c0:BLK]
                        diagonal = step >= BT * qb
                        if diagonal:
                            pe.matmul(SB[step % 2][:, c0:c0 + P], ident_r[:, :], later_keys_t[:, :],
                                      start=False, stop=False, skip_group_check=True)
                        pe.matmul(tile, KH[hs][:, keys], QH[hs][:, q], start=False, stop=False,
                                  skip_group_check=True)
                        pe.matmul(tile, KL[hs][:, keys], QH[hs][:, q], start=False, stop=False,
                                  skip_group_check=True)
                        pe.matmul(tile, KH[hs][:, keys], QL[hs][:, q], start=False, stop=True,
                                  skip_group_check=True).then_inc(sbb.scores, 1)
                        items = ring_items_b(ul, step, first, last)
                        place = 0

                        def ring_items(count):
                            nonlocal k, place
                            for item in items[place:place + count]:
                                n = LEAD_B - SKIP + it * RING_B + k
                                bank = RING[(LEAD_B - SKIP + k) % 2]
                                k += 1
                                if item[0] == "max":
                                    i, c = max_items_b(item[1])[item[2]]
                                    other = item[1] < qb
                                    max_b(1 - hs if other else hs, item[1], i, c, bank, n, head + other)
                                elif item[0] == "rows":
                                    rows(sbb, bank, n, it * UNITS_B + target_unit(ul, item[1]))
                                elif item[0] == "spread":
                                    spread(item[1] % 2, bank, n)
                                elif item[0] == "project":
                                    project_b(1 - hs, item[1], bank, n, head + 1)
                                elif item[0] == "values":
                                    values_b(1 - hs, item[1], bank, n, head + 1)
                                elif item[0] == "turned":
                                    turned(sbb, bank, n, AB, u)
                                else:
                                    phead = head if qb else head - 1
                                    output(sbb, bank, n, WAO[:, bass.ds(phead, 1), :].rearrange("p a c -> p (a c)"))
                            place += count

                        ring_items(1)
                        if not (first and ul == 0 and step == 0):
                            pul, pstep = (ul, step - 1) if step else ((ul - 1) % UNITS_B, steps_b((qb - 1) % BLOCKS) - 1)
                            if step == 1:
                                wait(pe, sbb.o_taken, u - 1)
                            pv_b(pul, pstep, g - 1, 0)
                            ring_items(1)
                            pv_b(pul, pstep, g - 1, 1)
                        ring_items(len(items) - place)
                        g = g + 1
                return k

            body_b(0, first=True)
            with pe.Fori(1, ITER_B - 1) as it:
                body_b(it)
            k = body_b(ITER_B - 1, last=True)
            for half in range(2):
                pv_b(UNITS_B - 1, TILES - 1, ITER_B * G_B - 1, half)
            n = LEAD_B - SKIP + (ITER_B - 1) * RING_B + k
            turned(sbb, RING[n % 2], n, AB, ITER_B * UNITS_B)
            output(sbb, RING[(n + 1) % 2], n + 1, WAO[:, HB - 1, :])
            pe.wait_ge(sbb.ring_taken, n + 2)
            ffn(1, 4)


def rope_tables():
    half = DB // 2
    freqs = np.power(np.float32(10000.0), -np.arange(half, dtype=np.float32) / np.float32(half)).astype(np.float32)
    radians = np.arange(T, dtype=np.float32)[None, :] * freqs[:, None]
    cos, sin = np.cos(radians), np.sin(radians)
    return (np.concatenate([cos, cos]).astype(np.float32), np.concatenate([-sin, sin]).astype(np.float32))


_INS = ['L0_attn_a_x', 'L0_attn_a_adaptive_scale', 'L0_attn_a_Wq', 'L0_attn_a_bq', 'L0_attn_a_Wk', 'L0_attn_a_bk',
        'L0_attn_a_Wv', 'L0_attn_a_bv', 'L0_attn_a_Wo', 'L0_attn_a_bo', 'L0_attn_a_gamma', 'L0_attn_a_beta',
        'L0_attn_b_w_aq', 'L0_attn_b_w_ak', 'L0_attn_b_w_av', 'L0_attn_b_w_ao', 'L0_ffn_W1', 'L0_ffn_b1',
        'L0_ffn_W2', 'L0_ffn_b2']


def kernel(**inputs):
    import concourse.bacc as bacc
    from concourse.bass_utils import run_bass_kernel_spmd

    nc = bacc.Bacc("TRN2", target_bir_lowering=False, num_devices=1)
    cos, sin = rope_tables()
    arrays, args = {}, []
    for name, a in [*((n, inputs[n]) for n in _INS), ("rope_cos", cos), ("rope_sin", sin)]:
        a = np.ascontiguousarray(a)
        arrays[f"in_{name}"] = a
        args.append(nc.dram_tensor(f"in_{name}", a.shape, mybir.dt.from_np(a.dtype), kind="ExternalInput").ap())
    args.append(nc.dram_tensor("out_0", (1, T, D), F32, kind="ExternalOutput").ap())
    build(nc, *args)
    r = run_bass_kernel_spmd(nc, [arrays], core_ids=[0])
    return r.results[0]["out_0"]
```

```python
from contextlib import ExitStack

import numpy as np

import concourse.bass as bass
from concourse import mybir

F32 = mybir.dt.float32
F32R = mybir.dt.float32r
F16 = mybir.dt.float16
BF16 = mybir.dt.bfloat16
ALU = mybir.AluOpType
ACT = mybir.ActivationFunctionType
X_AXIS = mybir.AxisListType.X

P = 128
T = 2048
D = 128
TILES = T // P
BLK = 512
BLOCKS = T // BLK
BT = BLK // P
EPS = 1e-5

HA, DA = 16, 64
SCALE_A = DA ** -0.5
ITER_A = HA // 2
UNITS_A = 2 * BLOCKS
STEPS_A = TILES // 2
G_A = UNITS_A * STEPS_A
SLOTS_A = 4
LAG_A = 2
LOW_BY_DVE = ()
HEAD_STEPS = (3, 7)
PIECES = ((0, 1), (2,), (3,), (4,))
WV_AT = 2 * DA + 2
BV_AT = WV_AT + DA
WCOL = BV_AT + DA
V1_AT = 2
V2_AT = V1_AT + DA
V3_AT = V2_AT + DA
VCOL = V3_AT + DA

HB, DB = 8, 128
VB = DB + 1
ITER_B = HB // 2
UNITS_B = 2 * BLOCKS
MASKED = -1e30
INTER = 512
CH = INTER // P

SETTLE = [("y", 0), ("y", 1), ("y", 2), ("x", 0), ("x", 1), ("y", 3), ("x", 2), ("x", 3)]
SLOTS_LN = 8

LIFT = 2.0 ** 8
AUX = 2 * BT


def steps_b(qb):
    return BT * (qb + 1)


G_B = 2 * sum(steps_b(q) for q in range(BLOCKS))


def ring_items_a(ul, step, first, last):
    hs, qb = divmod(ul, BLOCKS)
    items = []
    has_next = not (last and ul == UNITS_A - 1)
    if has_next:
        at = [0, 3, 5, 7, 10, 12, 14, 16, 16]
        items += [("max", i) for i in range(at[step], at[step + 1])]
    if ((ul - 1) % UNITS_A) // BLOCKS == 1 and not (first and ul == 0):
        items += [("turned",)] if step == 3 else [("output",)] if step == 4 else []
    if not (last and hs == 1) and qb < 3 and step in HEAD_STEPS:
        part = HEAD_STEPS.index(step)
        items += [("project", 2 * qb + part)] if qb < 2 else [("values", part)]
    if has_next and step == STEPS_A - 1:
        items += [("rows",)]
    return items


def after_a(ul, step, delay, first, last):
    at = ul * STEPS_A + step - delay
    if at < 0:
        return ()
    before = ring_items_a(at // STEPS_A, at % STEPS_A, first, last)
    return next((item for item in before if item[0] in ("project", "values")), ())


def max_items_b(qb):
    return [(i, c) for i in range(BT) for c in range(qb + 1)]


VALUES_B = {(2, 4): 0, (2, 7): 1, (2, 10): 2, (3, 9): 3}
PROJECT_B = {(1, 5): [0], (2, 3): [1], (2, 6): [2], (2, 9): [3], (3, 1): [4], (3, 3): [5], (3, 5): [6], (3, 8): [7]}
MAXIMA_B = {0: [(2, 0, 4, 0, 4)], 1: [(2, 4, 12, 0, 4)], 2: [(3, 0, 16, 0, 8)],
            3: [(0, 0, 4, 2, 6), (1, 0, 8, 7, 15)]}


def ring_items_b(ul, step, first, last):
    hs, qb = divmod(ul, BLOCKS)
    next_qb = (qb + 1) % BLOCKS
    next_head = not (last and hs == 1)
    items = []
    if step == steps_b(qb) - 3 and (next_qb or next_head):
        items += [("spread", next_qb)]
    for target, lo, hi, begin, end in MAXIMA_B[qb]:
        if target < qb and not next_head:
            continue
        if begin <= step < end:
            a, b = (lo + (hi - lo) * (step - begin + d) // (end - begin) for d in (0, 1))
            items += [("max", target, j) for j in range(a, b)]
        if step == end % steps_b(qb) and hi == len(max_items_b(target)):
            items += [("rows", target)]
    if not (first and ul == 0):
        items += [("turned",)] if step == 2 else [("output",)] if step == 3 else []
    if next_head:
        items += [("project", b) for b in PROJECT_B.get((qb, step), [])]
        items += [("values", VALUES_B[qb, step])] if (qb, step) in VALUES_B else []
    return items


def target_unit(ul, target):
    hs, qb = divmod(ul, BLOCKS)
    return (hs + (target < qb)) * BLOCKS + target


def count_items(items_of, units, steps_of, last=False):
    return sum(len(items_of(ul, s, False, last)) for ul in range(units) for s in range(steps_of(ul)))


RING_A = count_items(ring_items_a, UNITS_A, lambda ul: STEPS_A)
RING_B = count_items(ring_items_b, UNITS_B, lambda ul: steps_b(ul % BLOCKS))
RING_A_LAST = count_items(ring_items_a, UNITS_A, lambda ul: STEPS_A, last=True)
assert RING_A % 2 == 0 and RING_B % 2 == 0
LEAD_A = BLOCKS + 2 + 16 + 1
LEAD_B = 2 * BLOCKS + BLOCKS + (BT + 1) + (2 * BT + 1) + 1
SKIP = 2
END_A = LEAD_A - SKIP + (ITER_A - 1) * RING_A + RING_A_LAST + 2


def build(nc, x, adaptive_scale, Wq, bq, Wk, bk, Wv, bv, Wo, bo, gamma, beta,
          w_aq, w_ak, w_av, w_ao, W1, b1, W2, b2, rope_cos, rope_sin, out):
    ctx = ExitStack()
    with ctx:
        def sb(name, shape, dt=F32):
            return ctx.enter_context(nc.sbuf_tensor(name, shape, dt))

        def pb(name, shape):
            return ctx.enter_context(nc.psum_tensor(name, shape, F32))

        def sem(name):
            return ctx.enter_context(nc.semaphore(name))

        X = sb("X", [P, TILES, D])
        XN = sb("XN", [P, TILES, D])
        XNT = sb("XNT", [P, T])
        VP = sb("VP", [P, 2, TILES, VCOL], BF16)
        PAB = sb("PAB", [P, 2 * TILES * VB])
        RAW = sb("RAW", [P, 4 * HA * DA])
        PR = sb("PR", [P, 2, 2 * BLK])
        VF = sb("VF", [P, 2, BLK])
        F = sb("F", [P, 2, BLK])
        WST = sb("WST", [P, 2, 3 * DB])
        OSUM = sb("OSUM", [P, 2, BT // 2, DA])
        AT = sb("AT", [P, BLK])
        AB = sb("AB", [P, BT, DB])
        SHARED = sb("SHARED", [P, max(HA * WCOL + 8 * D + T, 2 * T + HB * D)])
        W1s = sb("W1s", [P, INTER])
        W2s = sb("W2s", [P, CH, D])
        ident = sb("ident", [P, P])
        rowmask = sb("rowmask", [AUX, BT, P])
        bo_b = sb("bo_b", [P, D])
        gamma_b = sb("gamma_b", [P, D])
        beta_b = sb("beta_b", [P, D])
        b2_b = sb("b2_b", [P, D])
        b1c = sb("b1c", [P, CH])
        eps = sb("eps", [P, 1])
        lift = sb("lift", [P, 1])
        stats = sb("stats", [P, BT, 6])
        meanvar = sb("meanvar", [P, SLOTS_LN, BT, 2])
        std = sb("std", [P, SLOTS_LN, BT])
        rstd = sb("rstd", [P, SLOTS_LN, BT])
        maxes = sb("maxes", [P, BT, BLOCKS])
        negmax = sb("negmax", [P, BT])
        negparts = sb("negparts", [P, AUX])
        rden = sb("rden", [P, BT])
        KH = [sb(f"KH{i}", [P, T], F32R) for i in range(2)]
        KL = [sb(f"KL{i}", [P, T], F32R) for i in range(2)]
        QH = [sb(f"QH{i}", [P, T], F32R) for i in range(2)]
        QL = [sb(f"QL{i}", [P, T], F32R) for i in range(2)]
        ident_r = sb("ident_r", [P, P], F32R)
        later_keys = sb("later_keys", [P, P], F32R)
        later_keys_t = sb("later_keys_t", [P, P], F32R)
        ones_r = sb("ones_r", [AUX, P], F32R)
        MROW = sb("MROW", [AUX, 2, BLK], F32R)

        wqk_raw = RAW[:, 0:HA * P].rearrange("p (h c) -> p h c", c=P)
        wv_raw = RAW[:, HA * P:HA * P + HA * DA].rearrange("p (j c) -> p j c", c=P)
        wo_raw = RAW[:, HA * P + HA * DA:HA * P + 2 * HA * DA].rearrange("p (j c) -> p j c", c=P)
        braw = F[0:HA, 1, 0:P]
        sraw = F[0:DA, 1, P:P + HA]
        WQK = SHARED[:, 0:HA * WCOL].rearrange("p (h c) -> p h c", c=WCOL)
        WoT = SHARED[:, HA * WCOL:HA * WCOL + 8 * D].rearrange("p (j c) -> p j c", c=D)
        A2 = SHARED[:, HA * WCOL + 8 * D:HA * WCOL + 8 * D + T].rearrange("p (t c) -> p t c", c=D)
        COS = SHARED[:, 0:T]
        SIN = SHARED[:, T:2 * T]
        WAO = SHARED[:, 2 * T:2 * T + HB * D].rearrange("p (h c) -> p h c", c=D)
        WQKB = RAW[:, 0:HB * 2 * DB].rearrange("p (h a c) -> p h a c", a=2, c=DB)
        WVB = RAW[:, HB * 2 * DB:HB * 3 * DB].rearrange("p (h c) -> p h c", c=DB)
        half_ab = SLOTS_A * BLK
        PA = PAB[:, 0:half_ab].bitcast(F16).rearrange("p (s q) -> p s q", s=SLOTS_A)
        PB = PAB[:, half_ab:2 * half_ab].bitcast(F16).rearrange("p (s q) -> p s q", s=SLOTS_A)
        VBS = PAB[:, :].rearrange("p (a t c) -> p a t c", a=2, c=VB)
        PRB = PR[:, 0, :].rearrange("p (s q) -> p s q", s=2)
        MB = VF
        SWAP = PR[:, 1, :].rearrange("p (s q) -> p s q", s=2)
        HID = [VP[:, :, :, :].rearrange("p a t c -> p (a t c)")[:, 0:2 * CH * BLK].bitcast(F32),
               PAB[:, 0:CH * BLK]]
        HID = [h.rearrange("p (j q) -> p j q", j=CH) for h in HID]
        mask_raw = F[:, 0, 0:2 * P].rearrange("p (a c) -> p a c", a=2)

        ST = [pb(f"ST{i}", [P, 2 * BLK]) for i in range(2)]
        RING = [pb(f"RING{i}", [P, BLK]) for i in range(2)]
        OO = pb("OO", [P, 2 * BLK])
        O = [OO[:, 0:BLK], OO[:, BLK:2 * BLK]]
        QUARTER = [ST[i // 2][:, (i % 2) * BLK:(i % 2 + 1) * BLK] for i in range(4)]
        SB = [QUARTER[0], QUARTER[1]]
        OB = [(O[0], QUARTER[2]), (O[1], QUARTER[3])]

        x_in = [sem(f"x_in{b}") for b in range(BLOCKS)]
        w_in = sem("w_in")
        vw_in = sem("vw_in")
        c_in = sem("c_in")
        fw_in = sem("fw_in")
        consts = sem("consts")
        const_r = sem("const_r")
        chain = sem("chain")
        pchain = sem("pchain")
        var_ready = sem("var_ready")
        std_ready = sem("std_ready")
        rstd_ready = sem("rstd_ready")
        y_applied = sem("y_applied")
        y_ready = sem("y_ready")
        xn_ready = sem("xn_ready")
        xnt_put = sem("xnt_put")
        xnt_ready = sem("xnt_ready")
        wt_put = sem("wt_put")
        wt_act = sem("wt_act")
        wt_dve = sem("wt_dve")
        ones_set = sem("ones_set")
        k_low = sem("k_low")
        p_low_pool = sem("p_low_pool")
        p_low_dve = sem("p_low_dve")
        v_high = sem("v_high")
        v_rest = sem("v_rest")
        v_ready = sem("v_ready")
        a2_ready = sem("a2_ready")
        xbo = sem("xbo")
        bweights = sem("bweights")
        hid_put = sem("hid_put")
        hid_ready = sem("hid_ready")
        ffn_put = sem("ffn_put")
        x_ready = sem("x_ready")
        out_done = sem("out_done")

        class Phase:
            pass

        def phase(n):
            s = Phase()
            s.wst_ready = sem(f"wst_ready_{n}")
            s.ring_put = sem(f"ring_put_{n}")
            s.ring_taken = sem(f"ring_taken_{n}")
            s.rope_summed = sem(f"rope_summed_{n}")
            s.high_ready = sem(f"high_ready_{n}")
            s.operands_ready = sem(f"operands_ready_{n}")
            s.max_ready = sem(f"max_ready_{n}")
            s.scores = sem(f"scores_{n}")
            s.filled = sem(f"filled_{n}")
            s.primed = sem(f"primed_{n}")
            s.exps = sem(f"exps_{n}")
            s.pv = sem(f"pv_{n}")
            s.o_taken = sem(f"o_taken_{n}")
            return s

        sa, sbb = phase("a"), phase("b")

        def wait(eng, s, value):
            if not isinstance(value, int) or value > 0:
                eng.wait_ge(s, value)

        block = ctx.enter_context(nc.Block())

        @block.sync
        def _(sp):
            xin = x[0].rearrange("(t p) c -> p t c", p=P)
            for b in range(BLOCKS):
                sp.dma_start(X[:, b * BT:(b + 1) * BT, :], xin[:, b * BT:(b + 1) * BT, :]).then_inc(x_in[b], 16)
            sp.dma_start(wqk_raw[0:DA, :, :], Wq.rearrange("(h d) c -> d h c", d=DA)).then_inc(w_in, 16)
            sp.dma_start(wqk_raw[DA:P, :, :], Wk.rearrange("(h d) c -> d h c", d=DA)).then_inc(w_in, 16)
            sp.dma_start(braw[:, 0:DA], bq.rearrange("(h d) -> h d", d=DA)).then_inc(w_in, 16)
            sp.dma_start(braw[:, DA:P], bk.rearrange("(h d) -> h d", d=DA)).then_inc(w_in, 16)
            sp.dma_start(sraw, adaptive_scale.partition_broadcast(DA)).then_inc(w_in, 16)
            sp.dma_start(wv_raw, Wv.rearrange("(j p) c -> p j c", p=P)).then_inc(vw_in, 16)
            sp.dma_start(wo_raw, Wo.rearrange("p (j c) -> p j c", c=P)).then_inc(vw_in, 16)
            sp.dma_start(WQK[:, :, BV_AT:WCOL], bv.rearrange("(h d) -> h d", d=DA).partition_broadcast(P)
                         ).then_inc(vw_in, 16)
            for dst, src in ((bo_b, bo), (gamma_b, gamma), (beta_b, beta), (b2_b, b2)):
                sp.dma_start(dst[:, :], src.partition_broadcast(P)).then_inc(c_in, 16)
            sp.dma_start(b1c[:, :], b1.rearrange("(j p) -> p j", p=P), allow_slow_non_contiguous=True
                         ).then_inc(fw_in, 16)
            sp.dma_start(W1s[:, :], W1).then_inc(fw_in, 16)
            sp.dma_start(W2s[:, :, :], W2.rearrange("(j p) n -> p j n", p=P)).then_inc(fw_in, 16)
            wait(sp, wt_put, 8)
            sp.dma_start(WQKB[:, :, 0, :], w_aq).then_inc(bweights, 16)
            sp.dma_start(WQKB[:, :, 1, :], w_ak).then_inc(bweights, 16)
            sp.dma_start(WVB, w_av).then_inc(bweights, 16)
            wait(sp, sa.ring_taken, END_A)
            sp.dma_start(COS, rope_cos).then_inc(bweights, 16)
            sp.dma_start(SIN, rope_sin).then_inc(bweights, 16)
            sp.dma_start(WAO, w_ao.rearrange("h d m -> d h m")).then_inc(bweights, 16)
            oout = out[0].rearrange("(t p) c -> p t c", p=P)
            for b in range(BLOCKS):
                wait(sp, x_ready, BLOCKS + b + 1)
                sp.dma_start(oout[:, b * BT:(b + 1) * BT, :], X[:, b * BT:(b + 1) * BT, :]).then_inc(out_done, 16)
            wait(sp, out_done, 16 * BLOCKS)

        @block.gpsimd
        def _(pool):
            tick = [0]

            def link(ins):
                tick[0] += 1
                ins.then_inc(pchain, 1)
                pool.wait_ge(pchain, tick[0])

            link(pool.memset(ident[:, :], 0.0))
            pool.affine_select(out=ident[:, :], in_=ident[:, :], compare_op=ALU.not_equal, fill=1.0, base=0,
                               pattern=[[-1, P]], channel_multiplier=1).then_inc(consts, 1)
            link(pool.memset(mask_raw, 0.0))
            pool.affine_select(out=mask_raw[:, 0, :], in_=mask_raw[:, 0, :], compare_op=ALU.is_ge, fill=MASKED,
                               base=0, pattern=[[-1, P]], channel_multiplier=1)
            pool.affine_select(out=mask_raw[:, 1, :], in_=mask_raw[:, 1, :], compare_op=ALU.is_ge, fill=MASKED,
                               base=0, pattern=[[1, P]], channel_multiplier=-1).then_inc(consts, 1)
            link(pool.memset(rowmask[:, :, :], 0.0))
            for half in range(2):
                ins = pool.affine_select(out=rowmask[:, :, :], in_=rowmask[:, :, :], compare_op=ALU.not_equal,
                                         fill=1.0, base=-half * BT, pattern=[[-1, BT], [0, P]],
                                         channel_multiplier=1)
                if half == 0:
                    link(ins)
            ins.then_inc(consts, 1)
            for i in range(2):
                pool.memset(QH[i][0:DA, :].bitcast(F32), 0.0)
                link(pool.memset(KL[i][0:DA, :].bitcast(F32), 0.0))
                ins = pool.memset(KL[i][0:AUX, :].bitcast(F32), 1.0)
            ins.then_inc(consts, 1)
            pool.wait_ge(wt_act, 5)
            pool.wait_ge(wt_dve, 5)
            pool.tensor_copy(WST[:, 0, 0:WCOL], WQK[:, 0, :]).then_inc(sa.wst_ready, 1)
            pool.memset(VP[:, :, :, 0:V1_AT], 1.0).then_inc(ones_set, 1)

            def q_low(hs, blk, index):
                pool.wait_ge(sa.high_ready, index * 5 + 2)
                at = QL[hs][0:DA, blk * BLK:(blk + 1) * BLK]
                pool.tensor_tensor(at, F[0:DA, blk % 2, :], at.bitcast(F32), ALU.subtract
                                   ).then_inc(sa.operands_ready, 1)

            def values_rest(hs, half, index):
                vp = VP[:, hs, half * 8:half * 8 + 8, :]
                vf = VF[:, half, :].rearrange("p (t c) -> p t c", c=DA)
                pool.wait_ge(v_high, 2 * index + 1)
                pool.tensor_tensor(vf, vf, vp[:, :, V1_AT:V2_AT], ALU.subtract).then_inc(v_rest, 1)

            def values_third(hs, half, index):
                vp = VP[:, hs, half * 8:half * 8 + 8, :]
                vf = VF[:, half, :].rearrange("p (t c) -> p t c", c=DA)
                pool.wait_ge(v_high, 2 * index + 2)
                pool.tensor_tensor(vp[:, :, V3_AT:VCOL], vf, vp[:, :, V2_AT:V3_AT], ALU.subtract
                                   ).then_inc(v_ready, 1)

            def p_low(step, g):
                pool.wait_ge(sa.exps, g + 1)
                wait(pool, sa.pv, g - SLOTS_A + 1)
                s = step % SLOTS_A
                pool.tensor_tensor(PB[:, s, :], PR[:, step % 2, :], PA[:, s, :], ALU.subtract
                                   ).then_inc(p_low_pool, 1)

            for blk in range(BLOCKS):
                q_low(0, blk, blk)
            for half in range(2):
                values_rest(0, half, half)
                values_third(0, half, half)
            pool.wait_ge(c_in, 64)
            pool.wait_ge(xnt_put, BLOCKS)
            pool.tensor_tensor(XN[:, :, :], XN[:, :, :], bo_b[:, :].unsqueeze(1).broadcast_to((P, TILES, D)),
                               ALU.add).then_inc(xbo, 1)
            pool.tensor_tensor(X[:, :, :], X[:, :, :], beta_b[:, :].unsqueeze(1).broadcast_to((P, TILES, D)),
                               ALU.add).then_inc(xbo, 1)

            def turn_a(it, first=False, last=False):
                for ul in range(UNITS_A):
                    hs, qb = divmod(ul, BLOCKS)
                    head = it * 2 + hs + 1
                    if qb == 0 and not (last and hs == 1):
                        pool.tensor_copy(WST[:, 1 - hs, 0:WCOL], WQK[:, bass.ds(head, 1), :].rearrange(
                            "p a c -> p (a c)")).then_inc(sa.wst_ready, 1)
                    for step in range(STEPS_A):
                        two, three = (after_a(ul, step, d, first, last) for d in (2, 3))
                        if two and two[0] == "project":
                            q_low(1 - hs, two[1], head * BLOCKS + two[1])
                        elif two:
                            values_rest(1 - hs, two[1], head * 2 + two[1])
                        if three and three[0] == "values":
                            values_third(1 - hs, three[1], head * 2 + three[1])
                        if step not in LOW_BY_DVE:
                            p_low(step, it * G_A + ul * STEPS_A + step)

            turn_a(0, first=True)
            with pool.Fori(1, ITER_A - 1) as it:
                turn_a(it)
            turn_a(ITER_A - 1, last=True)

            for b in range(BLOCKS):
                pool.wait_ge(y_applied, b + 1)
                y = XN[:, b * BT:(b + 1) * BT, :]
                pool.tensor_tensor(y, y, gamma_b[:, :].unsqueeze(1).broadcast_to((P, BT, D)), ALU.mult
                                   ).then_inc(y_ready, 1)

            pool.wait_ge(bweights, 16 * 6)

            def stage_b(par, head):
                pool.tensor_copy(WST[:, par, 0:2 * DB], WQKB[:, bass.ds(head, 1), :, :].rearrange(
                    "p z a c -> p (z a c)"))
                pool.tensor_copy(WST[:, par, 2 * DB:3 * DB], WVB[:, bass.ds(head, 1), :].rearrange(
                    "p z c -> p (z c)")).then_inc(sbb.wst_ready, 1)

            stage_b(0, 0)

            def rope_sum_b(j, item):
                pool.wait_ge(sbb.ring_taken, item + 1)
                s = j % 2
                pool.tensor_tensor(F[:, s, :], F[:, s, :], SWAP[:, s, :], ALU.add).then_inc(sbb.rope_summed, 1)

            def low_b(hs, j, index):
                q = slice(j // 2 * BLK, (j // 2 + 1) * BLK)
                high, low = ((QH, QL), (KH, KL))[j % 2]
                pool.wait_ge(sbb.high_ready, index + 1)
                pool.tensor_tensor(low[hs][:, q], F[:, j % 2, :], high[hs][:, q].bitcast(F32),
                                   ALU.subtract).then_inc(sbb.operands_ready, 1)

            for b in range(BLOCKS):
                for j in (2 * b, 2 * b + 1):
                    rope_sum_b(j, j)
                for j in (2 * b, 2 * b + 1):
                    low_b(0, j, j)
            pool.wait_ge(x_ready, BLOCKS)
            pool.memset(VBS[:, :, :, DB:VB], 1.0).then_inc(ones_set, 1)

            def heads_b(it, first=False, last=False):
                k = SKIP if first else 0
                for ul in range(UNITS_B):
                    hs, qb = divmod(ul, BLOCKS)
                    head = it * 2 + hs + 1
                    if qb == 0 and not (last and hs == 1):
                        stage_b(1 - hs, head)
                    for step in range(steps_b(qb)):
                        for item in ring_items_b(ul, step, first, last):
                            if item[0] == "project":
                                rope_sum_b(item[1], LEAD_B - SKIP + it * RING_B + k)
                                low_b(1 - hs, item[1], head * 2 * BLOCKS + item[1])
                            k += 1

            heads_b(0, first=True)
            with pool.Fori(1, ITER_B - 1) as it:
                heads_b(it)
            heads_b(ITER_B - 1, last=True)

        @block.scalar
        def _(act):
            def deviations(n):
                act.wait_ge(var_ready, n + 1)
                slot = n % SLOTS_LN
                act.activation(std[:, slot, :], meanvar[:, slot, :, 1], ACT.Sqrt, bias=eps[:, :]
                               ).then_inc(std_ready, 1)

            def transposed_block(n, bank):
                act.wait_ge(xnt_put, n + 1)
                b = n % BLOCKS
                act.activation(XNT[:, b * BLK:(b + 1) * BLK], bank, ACT.Copy).then_inc(xnt_ready, 1)

            act.wait_ge(const_r, 1)
            for b in range(BLOCKS):
                deviations(b)
            for i in range(0, 9, 2):
                act.wait_ge(wt_put, i + 1)
                bank = QUARTER[i % 4]
                src4 = bank.rearrange("p (a c) -> p a c", c=P)
                if i < 4:
                    ins = act.activation(WQK[:, i * 4:i * 4 + 4, 0:P], src4, ACT.Copy)
                elif i < 6:
                    ins = act.activation(WQK[:, 0:8, WV_AT:BV_AT], bank.rearrange("p (a c) -> p a c", c=DA), ACT.Copy)
                elif i < 8:
                    ins = act.activation(WoT[:, (i - 6) * 4:(i - 6) * 4 + 4, :], src4, ACT.Copy)
                else:
                    ins = act.activation(WQK[:, :, P], bank[:, 0:HA], ACT.Copy)
                ins.then_inc(wt_act, 1)
            for b in range(BLOCKS):
                transposed_block(b, O[b % 2][:, :])

            def high_parts_a(hs, blk, item, scores_before, pieces):
                act.wait_ge(sa.ring_taken, item + 1)
                wait(act, sa.scores, scores_before)
                q = slice(blk * BLK, (blk + 1) * BLK)
                f = F[:, blk % 2, :]
                places = ((KH[hs], DA, DA), (QL[hs], 0, 0), (KH[hs], 0, DA), (QL[hs], DA, 0), (QH[hs], DA, 0))
                for i in pieces:
                    dst, to, at = places[i]
                    act.activation(dst[to:to + DA, q], f[at:at + DA, :], ACT.Copy).then_inc(sa.high_ready, 1)

            def values_first(hs, half, item):
                vp = VP[:, hs, half * 8:half * 8 + 8, :]
                vf = VF[:, half, :].rearrange("p (t c) -> p t c", c=DA)
                act.wait_ge(sa.ring_taken, item + 1)
                act.activation(vp[:, :, V1_AT:V2_AT], vf, ACT.Copy).then_inc(v_high, 1)

            def values_second(hs, half, index):
                act.wait_ge(v_rest, index + 1)
                act.activation(VP[:, hs, half * 8:half * 8 + 8, V2_AT:V3_AT],
                               VF[:, half, :].rearrange("p (t c) -> p t c", c=DA), ACT.Copy).then_inc(v_high, 1)

            for blk in range(BLOCKS):
                high_parts_a(0, blk, blk, 0, range(5))
            for half in range(2):
                values_first(0, half, BLOCKS + half)
                values_second(0, half, half)

            def low_taken(g, ul, step, it):
                before = ul * STEPS_A + step - 2
                if isinstance(it, int) and it * G_A + before < 0:
                    return
                by_dve = before % STEPS_A in LOW_BY_DVE
                s, per_unit = (p_low_dve, len(LOW_BY_DVE)) if by_dve else (p_low_pool, STEPS_A - len(LOW_BY_DVE))
                units, at = divmod(before, STEPS_A)
                count = units * per_unit + sum((i in LOW_BY_DVE) == by_dve for i in range(at + 1))
                act.wait_ge(s, it * (UNITS_A * per_unit) + count)

            def exps_a(it, first=False, last=False):
                k = SKIP if first else 0
                numbers = {}
                for ul in range(UNITS_A):
                    hs, qb = divmod(ul, BLOCKS)
                    for step in range(STEPS_A):
                        g = it * G_A + ul * STEPS_A + step
                        low_taken(g, ul, step, it)
                        act.wait_ge(sa.scores, g + 1)
                        act.activation(PR[:, step % 2, :], ST[step % 2][:, :], ACT.Exp, bias=lift[:, :])
                        wait(act, sa.pv, g - SLOTS_A + 1)
                        act.activation(PA[:, step % SLOTS_A, :], ST[step % 2][:, :], ACT.Exp, bias=lift[:, :]
                                       ).then_inc(sa.exps, 1)
                        head = it * 2 + hs + 1
                        for delay, pieces in enumerate(PIECES, 1):
                            item = after_a(ul, step, delay, first, last)
                            if item and item[0] == "project":
                                high_parts_a(1 - hs, item[1], LEAD_A - SKIP + it * RING_A + numbers[item],
                                             (head - 1) * BLOCKS * STEPS_A, pieces)
                            elif item and delay == 1:
                                values_first(1 - hs, item[1], LEAD_A - SKIP + it * RING_A + numbers[item])
                            elif item and delay == 2:
                                values_second(1 - hs, item[1], head * 2 + item[1])
                        for item in ring_items_a(ul, step, first, last):
                            numbers[item] = k
                            k += 1

            exps_a(0, first=True)
            with act.Fori(1, ITER_A - 1) as it:
                exps_a(it)
            exps_a(ITER_A - 1, last=True)

            def relus(r, b):
                for j in range(CH):
                    n = (r * BLOCKS + b) * CH + j
                    act.wait_ge(hid_put, n + 1)
                    wait(act, ffn_put, r * BLOCKS + b - 1)
                    act.activation(HID[b % 2][:, j, :], QUARTER[j], ACT.Relu, bias=b1c[:, j:j + 1]
                                   ).then_inc(hid_ready, 1)

            for i in range(5):
                deviations(BLOCKS + i)
            transposed_block(BLOCKS, O[0][:, :])
            for i in range(5, 7):
                deviations(BLOCKS + i)
            transposed_block(BLOCKS + 1, O[0][:, :])
            deviations(BLOCKS + 7)
            act.wait_ge(fw_in, 48)
            relus(0, 0)
            transposed_block(BLOCKS + 2, O[0][:, :])
            relus(0, 1)
            transposed_block(BLOCKS + 3, O[0][:, :])
            relus(0, 2)
            deviations(3 * BLOCKS)
            relus(0, 3)
            deviations(3 * BLOCKS + 1)

            def high_part_b(hs, j, index, scores_before):
                act.wait_ge(sbb.rope_summed, index + 1)
                wait(act, sbb.scores, scores_before)
                q = slice(j // 2 * BLK, (j // 2 + 1) * BLK)
                high = (QH, KH)[j % 2]
                act.activation(high[hs][:, q], F[:, j % 2, :], ACT.Copy).then_inc(sbb.high_ready, 1)

            for b in range(BLOCKS):
                transposed_block(2 * BLOCKS + b, O[0][:, :])
                if b + 2 < BLOCKS:
                    deviations(3 * BLOCKS + b + 2)
                for j in (2 * b, 2 * b + 1):
                    high_part_b(0, j, j, 0)

            def fill(parity, slot, c0):
                act.activation(SB[parity][:, c0:BLK], MB[:, slot, c0:BLK], ACT.Copy).then_inc(sbb.filled, 1)

            act.wait_ge(sbb.primed, 1)
            act.wait_ge(sbb.ring_taken, LEAD_B)
            for step in range(2):
                fill(step, 0, step * P)

            def exps_b(it, first=False, last=False):
                k = SKIP if first else 0
                g = it * G_B
                todo = []
                for ul in range(UNITS_B):
                    hs, qb = divmod(ul, BLOCKS)
                    n = steps_b(qb)
                    spread = None
                    for step in range(n):
                        c0 = max(0, step - BT * qb) * P
                        act.wait_ge(sbb.scores, g + 1)
                        wait(act, sbb.pv, g - 1)
                        act.activation(PRB[:, step % 2, c0:BLK], SB[step % 2][:, c0:BLK], ACT.Exp,
                                       scale=1.0 / DB).then_inc(sbb.exps, 1)
                        g = g + 1
                        for item in ring_items_b(ul, step, first, last):
                            if item[0] == "spread":
                                spread = LEAD_B - SKIP + it * RING_B + k
                            k += 1
                        if step + 2 < n or spread is not None:
                            act.wait_ge(sbb.exps, g)
                        if step + 2 < n:
                            fill(step % 2, ul % 2, max(0, step + 2 - BT * qb) * P)
                        elif spread is not None:
                            if step + 2 == n:
                                act.wait_ge(sbb.ring_taken, spread + 1)
                            after = step + 2 - n
                            fill(step % 2, (ul + 1) % 2, after * P if qb == BLOCKS - 1 else 0)
                        for args in todo:
                            high_part_b(*args)
                        todo = [(1 - hs, item[1], (it * 2 + hs + 1) * 2 * BLOCKS + item[1],
                                 (it * 2 + hs) * (G_B // 2))
                                for item in ring_items_b(ul, step, first, last) if item[0] == "project"]

            exps_b(0, first=True)
            with act.Fori(1, ITER_B - 1) as it:
                exps_b(it)
            exps_b(ITER_B - 1, last=True)
            for b in range(3):
                deviations(4 * BLOCKS + b)
            transposed_block(3 * BLOCKS, O[0][:, :])
            deviations(4 * BLOCKS + 3)
            for b in range(BLOCKS):
                if b + 1 < BLOCKS:
                    transposed_block(3 * BLOCKS + b + 1, O[0][:, :])
                relus(1, b)

        @block.vector
        def _(dve):
            tick = [0]
            loop_base = [None]

            def link(ins):
                ins.then_inc(chain, 1)
                tick[0] += 1
                dve.wait_ge(chain, tick[0] if loop_base[0] is None else loop_base[0] + tick[0])

            def statistics(n, b, src):
                for i in range(BT):
                    ins = dve.bn_stats(stats[:, i, :], src[:, b * BT + i, :])
                link(ins)
                for i in range(BT):
                    ins = dve.bn_aggr(meanvar[:, n % SLOTS_LN, i, :], stats[:, i, :])
                ins.then_inc(var_ready, 1)

            def normalise(n, b, src=X, signal=xn_ready):
                slot = n % SLOTS_LN
                dve.wait_ge(std_ready, n + 1)
                dve.reciprocal(rstd[:, slot, :], std[:, slot, :]).then_inc(rstd_ready, 1)
                dve.wait_ge(rstd_ready, n + 1)
                for i in range(BT):
                    ins = dve.tensor_scalar(XN[:, b * BT + i, :], src[:, b * BT + i, :], meanvar[:, slot, i, 0:1],
                                            rstd[:, slot, i:i + 1], ALU.subtract, ALU.mult)
                ins.then_inc(signal, 1)

            dve.memset(eps[:, :], EPS)
            dve.memset(lift[:, :], float(np.log(LIFT)))
            dve.memset(ones_r[:, :].bitcast(F32), 1.0).then_inc(const_r, 1)
            dve.wait_ge(x_in[0], 16)
            statistics(0, 0, X)
            for b in range(BLOCKS):
                if b + 1 < BLOCKS:
                    dve.wait_ge(x_in[b + 1], 16)
                    dve.wait_ge(var_ready, b + 1)
                    statistics(b + 1, b + 1, X)
                normalise(b, b)
            dve.wait_ge(consts, 3)
            dve.tensor_copy(ident_r[:, :], ident[:, :])
            dve.tensor_copy(later_keys[:, :], mask_raw[:, 0, :])
            dve.tensor_copy(later_keys_t[:, :], mask_raw[:, 1, :]).then_inc(const_r, 1)
            for i in range(1, 8, 2):
                dve.wait_ge(wt_put, i + 1)
                bank = QUARTER[i % 4]
                src4 = bank.rearrange("p (a c) -> p a c", c=P)
                if i < 4:
                    ins = dve.tensor_copy(WQK[:, i * 4:i * 4 + 4, 0:P], src4)
                elif i < 6:
                    ins = dve.tensor_copy(WQK[:, 8:HA, WV_AT:BV_AT], bank.rearrange("p (a c) -> p a c", c=DA))
                else:
                    ins = dve.tensor_copy(WoT[:, (i - 6) * 4:(i - 6) * 4 + 4, :], src4)
                ins.then_inc(wt_dve, 1)
            dve.wait_ge(w_in, 80)
            dve.memset(WQK[DA:P, :, P + 1], 1.0)
            dve.tensor_scalar(WQK[0:DA, :, P + 1], sraw, SCALE_A, None, ALU.mult).then_inc(wt_dve, 1)

            def take_projected_a(hs, blk, bank, item, index):
                dve.wait_ge(sa.ring_put, item + 1)
                wait(dve, sa.operands_ready, index - 1)
                wait(dve, sa.high_ready, (index - 1) * 5)
                wait(dve, k_low, index - 1)
                dve.tensor_scalar(F[:, blk % 2, :], bank[:, :], WST[:, hs, P:P + 1],
                                  WST[:, hs, P + 1:P + 2], ALU.add, ALU.mult).then_inc(sa.ring_taken, 1)

            def take_k_low(hs, blk, index):
                dve.wait_ge(sa.high_ready, index * 5 + 1)
                q = slice(blk * BLK, (blk + 1) * BLK)
                dve.tensor_tensor(KL[hs][DA:P, q], F[DA:P, blk % 2, :], KH[hs][DA:P, q].bitcast(F32),
                                  ALU.subtract).then_inc(k_low, 1)

            def take_values_a(hs, half, bank, item, index):
                dve.wait_ge(sa.ring_put, item + 1)
                wait(dve, v_ready, index - 1)
                dve.tensor_tensor(VF[:, half, :].rearrange("p (t c) -> p t c", c=DA),
                                  bank[:, :].rearrange("p (t c) -> p t c", c=DA),
                                  WST[:, hs, BV_AT:WCOL].unsqueeze(1).broadcast_to((P, 8, DA)),
                                  ALU.add).then_inc(sa.ring_taken, 1)

            def take_p_low(step, g):
                dve.wait_ge(sa.exps, g + 1)
                wait(dve, sa.pv, g - SLOTS_A + 1)
                s = step % SLOTS_A
                dve.tensor_tensor(PB[:, s, :], PR[:, step % 2, :], PA[:, s, :], ALU.subtract
                                  ).then_inc(p_low_dve, 1)

            def take_max(s, bank, item, qt, c, width, chunks, last):
                dve.wait_ge(s.ring_put, item + 1)
                dve.reduce_max(maxes[:, qt, c:c + 1], bank[:, 0:width], X_AXIS).then_inc(s.ring_taken, 1)
                if last:
                    dve.wait_ge(s.ring_taken, item + 1)
                    link(dve.tensor_reduce(negmax[:, :], maxes[:, :, 0:chunks], X_AXIS, ALU.max, negate=True))
                    link(dve.tensor_copy(negparts[:, 0:BT].bitcast(F32R), negmax[:, :]))
                    dve.tensor_tensor(negparts[:, BT:AUX], negmax[:, :], negparts[:, 0:BT],
                                      ALU.subtract).then_inc(s.max_ready, 1)

            def take_rows(s, bank, item, dst):
                dve.wait_ge(s.ring_put, item + 1)
                rows = bank[0:AUX, 0:P].unsqueeze(1).broadcast_to((AUX, BT, P))
                dve.tensor_tensor(dst.rearrange("p (a c) -> p a c", c=P), rows, rowmask[:, :, :],
                                  ALU.mult).then_inc(s.ring_taken, 1)

            def take_turned(s, bank, item):
                dve.wait_ge(s.ring_put, item + 1)
                dve.tensor_copy(AT[:, :], bank[:, :]).then_inc(s.ring_taken, 1)

            def take_output(s, bank, item, acc, qb):
                dve.wait_ge(s.ring_put, item + 1)
                a = acc[:, qb * BT:(qb + 1) * BT, :]
                dve.tensor_tensor(a, a, bank[:, :].rearrange("p (a c) -> p a c", c=D),
                                  ALU.add).then_inc(s.ring_taken, 1)

            def normalise_a(ul, units_done):
                hs, qb = divmod(ul, BLOCKS)
                dve.wait_ge(sa.pv, units_done * STEPS_A)
                o = OO[:, :].rearrange("p (b x) -> p b x", b=2)[:, :, 0:2 * VCOL].rearrange(
                    "p b (q c) -> p b q c", c=VCOL)
                for b in range(2):
                    dve.reciprocal(rden[:, 2 * b:2 * b + 2], o[:, b, :, 0])
                    dve.tensor_reduce(OSUM[:, b, :, :], o[:, b, :, V1_AT:VCOL].rearrange(
                        "p q (a c) -> p q c a", a=3), X_AXIS, ALU.add).then_inc(sa.o_taken, 1)
                dve.wait_ge(sa.o_taken, units_done * 2)
                dve.tensor_tensor(A2[:, qb * BT:(qb + 1) * BT, hs * DA:(hs + 1) * DA],
                                  OSUM[:, :, :, :].rearrange("p b q c -> p (b q) c"),
                                  rden[:, :].unsqueeze(2).broadcast_to((P, BT, DA)), ALU.mult
                                  ).then_inc(a2_ready, 1)

            for blk in range(BLOCKS):
                take_projected_a(0, blk, RING[blk % 2], blk, blk)
                if blk:
                    take_k_low(0, blk - 1, blk - 1)
            take_k_low(0, BLOCKS - 1, BLOCKS - 1)
            for half in range(2):
                take_values_a(0, half, RING[(BLOCKS + half) % 2], BLOCKS + half, half)
            dve.wait_ge(consts, 4)
            for i in range(16):
                n = BLOCKS + 2 + i
                take_max(sa, RING[n % 2], n, i // 4, i % 4, BLK, BLOCKS, i == 15)
            take_rows(sa, RING[(LEAD_A - 1) % 2], LEAD_A - 1, QH[0][0:AUX, 0:BLK])
            dve.wait_ge(xbo, 2)

            def body_a(it, first=False, last=False):
                k = SKIP if first else 0
                for ul in range(UNITS_A):
                    hs, qb = divmod(ul, BLOCKS)
                    nhs, nqb = divmod((ul + 1) % UNITS_A, BLOCKS)
                    u = it * UNITS_A + ul
                    index = (it * 2 + hs + 1) * BLOCKS
                    for step in range(STEPS_A):
                        if step == LAG_A and not (first and ul == 0):
                            normalise_a((ul - 1) % UNITS_A, u)
                        two = after_a(ul, step, 2, first, last)
                        if two and two[0] == "project":
                            take_k_low(1 - hs, two[1], index + two[1])
                        late = (step - 1) % STEPS_A in LOW_BY_DVE and not (first and ul == 0 and step == 0)
                        for i, item in enumerate(ring_items_a(ul, step, first, last)):
                            n = LEAD_A - SKIP + it * RING_A + k
                            bank = RING[(LEAD_A - SKIP + k) % 2]
                            k += 1
                            if item[0] == "max":
                                j = item[1]
                                take_max(sa, bank, n, j // 4, j % 4, BLK, BLOCKS, j == 15)
                            elif item[0] == "rows":
                                take_rows(sa, bank, n, QH[nhs][0:AUX, nqb * BLK:(nqb + 1) * BLK])
                            elif item[0] == "project":
                                take_projected_a(1 - hs, item[1], bank, n, index + item[1])
                            elif item[0] == "values":
                                take_values_a(1 - hs, item[1], bank, n, (it * 2 + hs + 1) * 2 + item[1])
                            elif item[0] == "turned":
                                take_turned(sa, bank, n)
                            else:
                                take_output(sa, bank, n, XN, (qb - 1) % BLOCKS)
                            if i == 0 and late:
                                take_p_low((step - 1) % STEPS_A, it * G_A + ul * STEPS_A + step - 1)
                                late = False
                        if late:
                            take_p_low((step - 1) % STEPS_A, it * G_A + ul * STEPS_A + step - 1)
                return k

            def looped(body, turns):
                before = tick[0]
                loop_base[0] = None
                body(0, first=True)
                start = tick[0]
                with dve.Fori(1, turns - 1) as it:
                    tick[0] = 0
                    loop_base[0] = (it - 1) * links_of[body.__name__] + start
                    body(it)
                    assert tick[0] == links_of[body.__name__], (body.__name__, tick[0])
                loop_base[0] = None
                tick[0] = start + (turns - 2) * links_of[body.__name__]
                return body(turns - 1, last=True)

            links_of = {"body_a": 2 * UNITS_A, "body_b": 3 * UNITS_B}

            looped(body_a, ITER_A)
            def settle(*places):
                for i in places:
                    what, b = SETTLE[i]
                    if what == "x":
                        a = X[:, b * BT:(b + 1) * BT, :]
                        dve.wait_ge(y_ready, b + 1)
                        link(dve.tensor_tensor(a, a, XN[:, b * BT:(b + 1) * BT, :], ALU.add))
                    else:
                        dve.wait_ge(sa.ring_taken, END_A if b == 3 else END_A - 2)
                    dve.wait_ge(var_ready, BLOCKS + i)
                    statistics(BLOCKS + i, b, X if what == "x" else XN)

            def normalise_settled(i):
                what, b = SETTLE[i]
                normalise(BLOCKS + i, b, *((XN, y_applied) if what == "y" else (X, xn_ready)))

            settle(0, 1, 2)
            if STEPS_A - 1 in LOW_BY_DVE:
                take_p_low(STEPS_A - 1, ITER_A * G_A - 1)
            for i in range(3):
                normalise_settled(i)
            settle(3)
            normalise_a(UNITS_A - 1, ITER_A * UNITS_A)
            normalise_settled(3)
            settle(4)
            take_turned(sa, RING[(END_A - 2) % 2], END_A - 2)
            normalise_settled(4)
            take_output(sa, RING[(END_A - 1) % 2], END_A - 1, XN, BLOCKS - 1)
            settle(5, 6)
            normalise_settled(5)
            normalise_settled(6)
            settle(7)
            normalise_settled(7)

            def take_ffn(r, b):
                dve.wait_ge(ffn_put, r * BLOCKS + b + 1)
                a = X[:, b * BT:(b + 1) * BT, :]
                link(dve.tensor_tensor(a, a, O[1][:, :].rearrange("p (a c) -> p a c", c=D), ALU.add))
                dve.tensor_tensor(a, a, b2_b[:, :].unsqueeze(1).broadcast_to((P, BT, D)), ALU.add
                                  ).then_inc(x_ready, 1)

            def take_projected_b(j, bank, item, index):
                dve.wait_ge(sbb.ring_put, item + 1)
                wait(dve, sbb.operands_ready, index - 1)
                s, r = j % 2, bank
                q = slice(j // 2 * BLK, (j // 2 + 1) * BLK)
                half = DB // 2
                dve.tensor_tensor(F[:, s, :], r[:, :], COS[:, q], ALU.mult)
                dve.tensor_tensor(SWAP[0:half, s, :], r[half:P, :], SIN[0:half, q], ALU.mult)
                dve.tensor_tensor(SWAP[half:P, s, :], r[0:half, :], SIN[half:P, q], ALU.mult
                                  ).then_inc(sbb.ring_taken, 1)

            def normalise_b(ul, steps_done):
                dve.wait_ge(sbb.pv, steps_done)
                three, fourth = OB[ul % 2]
                o = three[:, 0:3 * VB].rearrange("p (a c) -> p a c", c=VB)
                dve.reciprocal(rden[:, 0:3], o[:, :, DB])
                link(dve.reciprocal(rden[:, 3:4], fourth[:, DB:VB]))
                dve.tensor_tensor(AB[:, 0:3, :], o[:, :, 0:DB], rden[:, 0:3].unsqueeze(2).broadcast_to((P, 3, DB)),
                                  ALU.mult)
                dve.tensor_scalar(AB[:, 3, :], fourth[:, 0:DB], rden[:, 3:4], None, ALU.mult
                                  ).then_inc(sbb.o_taken, 1)

            def take_values_b(hs, part, bank, item):
                dve.wait_ge(sbb.ring_put, item + 1)
                dve.tensor_copy(VBS[:, hs, part * BT:(part + 1) * BT, 0:DB],
                                bank[:, :].rearrange("p (t c) -> p t c", c=DB)).then_inc(sbb.ring_taken, 1)

            for b in range(BLOCKS):
                take_ffn(0, b)
                dve.wait_ge(x_ready, b + 1)
                dve.wait_ge(var_ready, 3 * BLOCKS + b)
                statistics(3 * BLOCKS + b, b, X)
                if b == 2:
                    dve.wait_ge(bweights, 16 * 6)
                if b >= 2:
                    for j in (2 * b - 4, 2 * b - 3):
                        take_projected_b(j, RING[j % 2], j, j)
                if b != 1:
                    for i in ((0,), (), (1, 2), (3,))[b]:
                        normalise(3 * BLOCKS + i, i)
            for j in range(BLOCKS, 2 * BLOCKS):
                take_projected_b(j, RING[j % 2], j, j)
            for part in range(BLOCKS):
                n = 2 * BLOCKS + part
                take_values_b(0, part, RING[n % 2], n)
            for i in range(BT):
                n = 3 * BLOCKS + i
                take_max(sbb, RING[n % 2], n, i, 0, (i + 1) * P, 1, i == BT - 1)
            take_rows(sbb, RING[(n + 1) % 2], n + 1, MROW[:, 0, :])
            for i, (qt, c) in enumerate(max_items_b(1)):
                n = LEAD_B - 2 - 2 * BT + i
                take_max(sbb, RING[n % 2], n, qt, c, BLK if c < 1 else (qt + 1) * P, 2, i == 2 * BT - 1)
            take_rows(sbb, RING[(LEAD_B - 2) % 2], LEAD_B - 2, MROW[:, 1, :])

            def take_spread(slot, bank, item, steps_before):
                dve.wait_ge(sbb.ring_put, item + 1)
                wait(dve, sbb.filled, steps_before)
                dve.tensor_copy(MB[:, slot, :], bank[:, :]).then_inc(sbb.ring_taken, 1)

            take_spread(0, RING[(LEAD_B - 1) % 2], LEAD_B - 1, 0)

            def body_b(it, first=False, last=False):
                k = SKIP if first else 0
                done = it * G_B
                for ul in range(UNITS_B):
                    hs, qb = divmod(ul, BLOCKS)
                    u = it * UNITS_B + ul
                    for step in range(steps_b(qb)):
                        if step == 1 and not (first and ul == 0):
                            normalise_b((ul - 1) % UNITS_B, done)
                        for item in ring_items_b(ul, step, first, last):
                            n = LEAD_B - SKIP + it * RING_B + k
                            bank = RING[(LEAD_B - SKIP + k) % 2]
                            k += 1
                            if item[0] == "max":
                                target = item[1]
                                todo = max_items_b(target)
                                i, c = todo[item[2]]
                                take_max(sbb, bank, n, i, c, BLK if c < target else (i + 1) * P, target + 1,
                                         item[2] == len(todo) - 1)
                            elif item[0] == "rows":
                                take_rows(sbb, bank, n, MROW[:, item[1] % 2, :])
                            elif item[0] == "spread":
                                take_spread(item[1] % 2, bank, n, done)
                            elif item[0] == "project":
                                take_projected_b(item[1], bank, n, (it * 2 + hs + 1) * 2 * BLOCKS + item[1])
                            elif item[0] == "values":
                                take_values_b(1 - hs, item[1], bank, n)
                            elif item[0] == "turned":
                                take_turned(sbb, bank, n)
                            else:
                                take_output(sbb, bank, n, X, (qb - 1) % BLOCKS)
                    done = done + steps_b(qb)
                return k

            k = looped(body_b, ITER_B)
            n = LEAD_B - SKIP + (ITER_B - 1) * RING_B + k

            def last_ln(b):
                dve.wait_ge(var_ready, 4 * BLOCKS + b)
                statistics(4 * BLOCKS + b, b, X)

            dve.wait_ge(sbb.ring_taken, n)
            last_ln(0)
            last_ln(1)
            normalise_b(UNITS_B - 1, ITER_B * G_B)
            normalise(4 * BLOCKS, 0)
            last_ln(2)
            take_turned(sbb, RING[n % 2], n)
            normalise(4 * BLOCKS + 1, 1)
            take_output(sbb, RING[(n + 1) % 2], n + 1, X, BLOCKS - 1)
            dve.wait_ge(sbb.ring_taken, n + 2)
            normalise(4 * BLOCKS + 2, 2)
            last_ln(3)
            normalise(4 * BLOCKS + 3, 3)
            for b in range(BLOCKS):
                take_ffn(1, b)

        @block.tensor
        def _(pe):
            def turn_block(n, b, bank):
                for i in range(BT):
                    ins = pe.transpose(bank[:, i * P:(i + 1) * P], XN[:, b * BT + i, :], ident[:, :])
                ins.then_inc(xnt_put, 1)

            pe.wait_ge(consts, 1)
            pe.wait_ge(w_in, 80)
            for i in range(9):
                if i == 4:
                    pe.wait_ge(vw_in, 48)
                if i >= 4:
                    pe.wait_ge(wt_act if i % 2 == 0 else wt_dve, (i - 4) // 2 + 1)
                bank = QUARTER[i % 4]
                if i == 8:
                    ins = pe.transpose(bank[:, 0:HA], braw, ident[0:HA, 0:HA])
                else:
                    src = (wqk_raw, wqk_raw, wqk_raw, wqk_raw, wv_raw, wv_raw, wo_raw, wo_raw)[i]
                    at = (i if i < 4 else i % 2) * 4
                    for j in range(4):
                        ins = pe.transpose(bank[:, j * P:(j + 1) * P], src[:, at + j, :], ident[:, :])
                ins.then_inc(wt_put, 1)
            for b in range(BLOCKS):
                pe.wait_ge(xn_ready, b + 1)
                wait(pe, xnt_ready, b - 1)
                turn_block(b, b, O[b % 2])

            def claim(s, item):
                wait(pe, s.ring_taken, item - 1)

            def project_a(hs, blk, bank, item, head):
                claim(sa, item)
                pe.wait_ge(sa.wst_ready, head + 1)
                pe.matmul(bank[:, :], WST[:, hs, 0:P], XNT[:, blk * BLK:(blk + 1) * BLK], start=True,
                          stop=True).then_inc(sa.ring_put, 1)

            def values_a(hs, half, bank, item, head):
                claim(sa, item)
                for t in range(8):
                    m = half * 8 + t
                    ins = pe.matmul(bank[:, t * DA:(t + 1) * DA], XNT[:, m * P:(m + 1) * P],
                                    WST[:, hs, WV_AT:BV_AT], start=True, stop=True)
                ins.then_inc(sa.ring_put, 1)

            def max_a(hs, qb, i, bank, item, head):
                if i == 0 and qb == 0:
                    pe.wait_ge(sa.operands_ready, (head + 1) * BLOCKS)
                    pe.wait_ge(k_low, (head + 1) * BLOCKS)
                    pe.wait_ge(sa.high_ready, (head + 1) * BLOCKS * 5)
                claim(sa, item)
                qt, c = divmod(i, BLOCKS)
                at = qb * BLK + qt * P
                pe.matmul(bank[:, :], QL[hs][:, at:at + P], KH[hs][:, c * BLK:(c + 1) * BLK], start=True,
                          stop=True).then_inc(sa.ring_put, 1)

            def rows(s, bank, item, unit):
                claim(s, item)
                pe.wait_ge(s.max_ready, unit + 1)
                pe.transpose(bank[0:AUX, 0:P], negparts[:, :], ident[:, :]).then_inc(s.ring_put, 1)

            def turned(s, bank, item, src, units_done):
                claim(s, item)
                pe.wait_ge(a2_ready if s is sa else s.o_taken, units_done)
                for i in range(BT):
                    ins = pe.transpose(bank[:, i * P:(i + 1) * P], src[:, i, :], ident[:, :])
                ins.then_inc(s.ring_put, 1)

            def output(s, bank, item, w, adjacent=True):
                claim(s, item)
                if adjacent:
                    pe.wait_ge(s.ring_taken, item)
                for i in range(BT):
                    ins = pe.matmul(bank[:, i * D:(i + 1) * D], AT[:, i * P:(i + 1) * P], w, start=True, stop=True)
                ins.then_inc(s.ring_put, 1)

            pe.wait_ge(wt_act, 5)
            pe.wait_ge(wt_dve, 5)
            for blk in range(BLOCKS):
                pe.wait_ge(xnt_ready, blk + 1)
                project_a(0, blk, RING[blk % 2], blk, 0)
            for half in range(2):
                values_a(0, half, RING[(BLOCKS + half) % 2], BLOCKS + half, 0)
            pe.wait_ge(consts, 4)
            for i in range(16):
                n = BLOCKS + 2 + i
                max_a(0, 0, i, RING[n % 2], n, 0)
            rows(sa, RING[(LEAD_A - 1) % 2], LEAD_A - 1, 0)

            def pv_a(ul, step, unit, j):
                if j == 0:
                    by_dve = step in LOW_BY_DVE
                    s, per_unit = ((p_low_dve, len(LOW_BY_DVE)) if by_dve
                                   else (p_low_pool, STEPS_A - len(LOW_BY_DVE)))
                    pe.wait_ge(s, unit * per_unit + sum((i in LOW_BY_DVE) == by_dve for i in range(step + 1)))
                m = 2 * step + j
                hs = ul // BLOCKS
                v = VP[:, hs, m, :]
                for qt in range(BT):
                    if m == 0 and qt % 2 == 0:
                        wait(pe, sa.o_taken, unit * 2 - 1 + qt // 2)
                    at = j * BLK + qt * P
                    high, low = PA[:, step % SLOTS_A, at:at + P], PB[:, step % SLOTS_A, at:at + P]
                    o = O[qt // 2][:, (qt % 2) * VCOL:(qt % 2 + 1) * VCOL]
                    pe.matmul(o, high, v, start=(m == 0 and qt % 2 == 0), stop=False, skip_group_check=True)
                    ins = pe.matmul(o[:, 0:V3_AT], low, v[:, 0:V3_AT], start=False,
                                    stop=(m == TILES - 1), skip_group_check=True)
                if j == 1:
                    ins.then_inc(sa.pv, 1)

            def body_a(it, first=False, last=False):
                k = SKIP if first else 0
                for ul in range(UNITS_A):
                    hs, qb = divmod(ul, BLOCKS)
                    nhs, nqb = divmod((ul + 1) % UNITS_A, BLOCKS)
                    u = it * UNITS_A + ul
                    head = it * 2 + hs
                    next_head = it * 2 + (ul + 1) // BLOCKS
                    q = slice(qb * BLK, (qb + 1) * BLK)
                    for step in range(STEPS_A):
                        g = it * G_A + ul * STEPS_A + step
                        if step == 0:
                            pe.wait_ge(sa.ring_taken, LEAD_A - SKIP + it * RING_A + k)
                        wait(pe, sa.exps, g - 1)
                        items = ring_items_a(ul, step, first, last)
                        place = 0

                        def ring_items(count):
                            nonlocal k, place
                            for item in items[place:place + count]:
                                n = LEAD_A - SKIP + it * RING_A + k
                                bank = RING[(LEAD_A - SKIP + k) % 2]
                                k += 1
                                if item[0] == "max":
                                    max_a(nhs, nqb, item[1], bank, n, next_head)
                                elif item[0] == "rows":
                                    rows(sa, bank, n, u + 1)
                                elif item[0] == "project":
                                    project_a(1 - hs, item[1], bank, n, head + 1)
                                elif item[0] == "values":
                                    values_a(1 - hs, item[1], bank, n, head + 1)
                                elif item[0] == "turned":
                                    pqb = (qb - 1) % BLOCKS
                                    turned(sa, bank, n, A2[:, pqb * BT:(pqb + 1) * BT, :], u)
                                else:
                                    pair = it - 1 if ul == 0 else it
                                    output(sa, bank, n, WoT[:, bass.ds(pair, 1), :].rearrange("p a c -> p (a c)"),
                                           item is items[0])
                            place += count

                        for j in range(2):
                            keys = slice((2 * step + j) * P, (2 * step + j + 1) * P)
                            tile = ST[step % 2][:, j * BLK:(j + 1) * BLK]
                            pe.matmul(tile, KH[hs][:, keys], QL[hs][:, q], start=True, stop=False)
                            ins = pe.matmul(tile, KL[hs][:, keys], QH[hs][:, q], start=False, stop=True)
                            if j == 0 and len(items) > 3:
                                ring_items(len(items) - 3)
                        ins.then_inc(sa.scores, 1)
                        ring_items(1)
                        if not (first and ul == 0 and step < LAG_A):
                            same = step >= LAG_A
                            pul, pstep = (ul if same else (ul - 1) % UNITS_A), (step - LAG_A) % STEPS_A
                            if pstep == 0:
                                ring_items(len(items) - place)
                                if qb == 0:
                                    pe.wait_ge(v_ready, head * 2 + 2)
                            pv_a(pul, pstep, u if same else u - 1, 0)
                            ring_items(1)
                            pv_a(pul, pstep, u if same else u - 1, 1)
                        ring_items(len(items) - place)
                return k

            body_a(0, first=True)
            with pe.Fori(1, ITER_A - 1) as it:
                body_a(it)
            body_a(ITER_A - 1, last=True)
            for step in range(STEPS_A - LAG_A, STEPS_A):
                for j in range(2):
                    pv_a(UNITS_A - 1, step, ITER_A * UNITS_A - 1, j)
            turned(sa, RING[(END_A - 2) % 2], END_A - 2, A2[:, (BLOCKS - 1) * BT:BLOCKS * BT, :], ITER_A * UNITS_A)
            output(sa, RING[(END_A - 1) % 2], END_A - 1, WoT[:, ITER_A - 1, :])
            pe.wait_ge(sa.ring_taken, END_A)

            def hidden(r, b):
                pe.wait_ge(xnt_ready, (1 if r == 0 else 3) * BLOCKS + b + 1)
                for j in range(CH):
                    wait(pe, hid_ready, (r * BLOCKS + b - 1) * CH + j + 1)
                    pe.matmul(QUARTER[j], W1s[:, j * P:(j + 1) * P], XNT[:, b * BLK:(b + 1) * BLK], start=True,
                              stop=True).then_inc(hid_put, 1)

            def turn_x(n):
                pe.wait_ge(xn_ready, n + 1)
                wait(pe, xnt_ready, n)
                turn_block(n, n % BLOCKS, O[0])

            def ffn_out(r, b):
                wait(pe, x_ready, r * BLOCKS + b)
                pe.wait_ge(hid_ready, (r * BLOCKS + b + 1) * CH)
                for i in range(BT):
                    for j in range(CH):
                        ins = pe.matmul(O[1][:, i * D:(i + 1) * D], HID[b % 2][:, j, i * P:(i + 1) * P],
                                        W2s[:, j, :], start=(j == 0), stop=(j == CH - 1))
                ins.then_inc(ffn_put, 1)

            pe.wait_ge(fw_in, 48)
            turn_x(4)
            turn_x(5)
            hidden(0, 0)
            turn_x(6)
            hidden(0, 1)
            ffn_out(0, 0)
            turn_x(7)
            hidden(0, 2)
            ffn_out(0, 1)
            hidden(0, 3)

            def project_b(hs, j, bank, item, head):
                claim(sbb, item)
                pe.wait_ge(sbb.wst_ready, head + 1)
                blk = j // 2
                pe.matmul(bank[:, :], WST[:, hs, (j % 2) * DB:(j % 2 + 1) * DB], XNT[:, blk * BLK:(blk + 1) * BLK],
                          start=True, stop=True).then_inc(sbb.ring_put, 1)

            def values_b(hs, part, bank, item, head):
                claim(sbb, item)
                for t in range(BT):
                    m = part * BT + t
                    ins = pe.matmul(bank[:, t * DB:(t + 1) * DB], XNT[:, m * P:(m + 1) * P],
                                    WST[:, hs, 2 * DB:3 * DB], start=True, stop=True)
                ins.then_inc(sbb.ring_put, 1)

            def max_b(hs, qb, i, c, bank, item, head):
                if (i, c) == (0, 0):
                    pe.wait_ge(sbb.operands_ready, head * 2 * BLOCKS + 2 * (qb + 1))
                claim(sbb, item)
                width = BLK if c < qb else (i + 1) * P
                at = qb * BLK + i * P
                if c == qb:
                    pe.matmul(bank[:, i * P:(i + 1) * P], ident_r[:, :], later_keys[:, :], start=True, stop=True)
                pe.matmul(bank[:, 0:width], QH[hs][:, at:at + P], KH[hs][:, c * BLK:c * BLK + width],
                          start=(c < qb), stop=True, skip_group_check=True).then_inc(sbb.ring_put, 1)

            turn_x(8)
            ffn_out(0, 2)
            for b in range(BLOCKS):
                pe.wait_ge(xnt_ready, 2 * BLOCKS + b + 1)
                for j in (2 * b, 2 * b + 1):
                    project_b(0, j, RING[j % 2], j, 0)
                if b == 0:
                    ffn_out(0, 3)
                if b + 1 < BLOCKS:
                    turn_x(9 + b)
            for part in range(BLOCKS):
                n = 2 * BLOCKS + part
                values_b(0, part, RING[n % 2], n, 0)
            for i in range(BT):
                n = 3 * BLOCKS + i
                max_b(0, 0, i, 0, RING[n % 2], n, 0)
            rows(sbb, RING[(n + 1) % 2], n + 1, 0)
            for i, (qt, c) in enumerate(max_items_b(1)):
                n = LEAD_B - 2 - 2 * BT + i
                max_b(0, 1, qt, c, RING[n % 2], n, 0)
            rows(sbb, RING[(LEAD_B - 2) % 2], LEAD_B - 2, 1)

            def spread(slot, bank, item):
                claim(sbb, item)
                pe.wait_ge(sbb.ring_taken, item)
                pe.matmul(bank[:, :], ones_r[:, :], MROW[:, slot, :], start=True, stop=True
                          ).then_inc(sbb.ring_put, 1)

            spread(0, RING[(LEAD_B - 1) % 2], LEAD_B - 1)
            for i in range(2):
                ins = pe.matmul(SB[i][:, :], ones_r[:, :], MROW[:, 0, :], start=True, stop=True)
            ins.then_inc(sbb.primed, 1)
            pe.wait_ge(ones_set, 2)

            def pv_b(ul, step, g, half):
                qb = ul % BLOCKS
                if half == 0:
                    pe.wait_ge(sbb.exps, g + 1)
                for qt in range(max(2 * half, step - BT * qb), 2 * half + 2):
                    bank, at = (OB[ul % 2][0], qt * VB) if qt < 3 else (OB[ul % 2][1], 0)
                    ins = pe.matmul(bank[:, at:at + VB], PRB[:, step % 2, qt * P:(qt + 1) * P],
                                    VBS[:, ul // BLOCKS, step, :], start=(step == 0 and qt in (0, 3)),
                                    stop=(step == BT * qb + qt), skip_group_check=True)
                if half == 1:
                    ins.then_inc(sbb.pv, 1)

            def body_b(it, first=False, last=False):
                k = SKIP if first else 0
                g = it * G_B
                for ul in range(UNITS_B):
                    hs, qb = divmod(ul, BLOCKS)
                    u = it * UNITS_B + ul
                    head = it * 2 + hs
                    for step in range(steps_b(qb)):
                        pe.wait_ge(sbb.filled, g + 1)
                        keys = slice(step * P, (step + 1) * P)
                        c0 = max(0, step - BT * qb) * P
                        q = slice(qb * BLK + c0, (qb + 1) * BLK)
                        tile = SB[step % 2][:, c0:BLK]
                        diagonal = step >= BT * qb
                        if diagonal:
                            pe.matmul(SB[step % 2][:, c0:c0 + P], ident_r[:, :], later_keys_t[:, :],
                                      start=False, stop=False, skip_group_check=True)
                        pe.matmul(tile, KH[hs][:, keys], QH[hs][:, q], start=False, stop=False,
                                  skip_group_check=True)
                        pe.matmul(tile, KL[hs][:, keys], QH[hs][:, q], start=False, stop=False,
                                  skip_group_check=True)
                        pe.matmul(tile, KH[hs][:, keys], QL[hs][:, q], start=False, stop=True,
                                  skip_group_check=True).then_inc(sbb.scores, 1)
                        items = ring_items_b(ul, step, first, last)
                        place = 0

                        def ring_items(count):
                            nonlocal k, place
                            for item in items[place:place + count]:
                                n = LEAD_B - SKIP + it * RING_B + k
                                bank = RING[(LEAD_B - SKIP + k) % 2]
                                k += 1
                                if item[0] == "max":
                                    i, c = max_items_b(item[1])[item[2]]
                                    other = item[1] < qb
                                    max_b(1 - hs if other else hs, item[1], i, c, bank, n, head + other)
                                elif item[0] == "rows":
                                    rows(sbb, bank, n, it * UNITS_B + target_unit(ul, item[1]))
                                elif item[0] == "spread":
                                    spread(item[1] % 2, bank, n)
                                elif item[0] == "project":
                                    project_b(1 - hs, item[1], bank, n, head + 1)
                                elif item[0] == "values":
                                    values_b(1 - hs, item[1], bank, n, head + 1)
                                elif item[0] == "turned":
                                    turned(sbb, bank, n, AB, u)
                                else:
                                    phead = head if qb else head - 1
                                    output(sbb, bank, n, WAO[:, bass.ds(phead, 1), :].rearrange("p a c -> p (a c)"),
                                           item is items[0])
                            place += count

                        ring_items(1)
                        if not (first and ul == 0 and step == 0):
                            pul = ul if step else (ul - 1) % UNITS_B
                            pstep = step - 1 if step else steps_b(pul % BLOCKS) - 1
                            if step == 1:
                                wait(pe, sbb.o_taken, u - 1)
                            pv_b(pul, pstep, g - 1, 0)
                            ring_items(1)
                            pv_b(pul, pstep, g - 1, 1)
                        ring_items(len(items) - place)
                        g = g + 1
                return k

            body_b(0, first=True)
            with pe.Fori(1, ITER_B - 1) as it:
                body_b(it)
            k = body_b(ITER_B - 1, last=True)
            for half in range(2):
                pv_b(UNITS_B - 1, TILES - 1, ITER_B * G_B - 1, half)
            n = LEAD_B - SKIP + (ITER_B - 1) * RING_B + k
            turned(sbb, RING[n % 2], n, AB, ITER_B * UNITS_B)
            output(sbb, RING[(n + 1) % 2], n + 1, WAO[:, HB - 1, :])
            pe.wait_ge(sbb.ring_taken, n + 2)
            turn_x(12)
            turn_x(13)
            hidden(1, 0)
            turn_x(14)
            hidden(1, 1)
            ffn_out(1, 0)
            turn_x(15)
            hidden(1, 2)
            ffn_out(1, 1)
            hidden(1, 3)
            ffn_out(1, 2)
            ffn_out(1, 3)


def rope_tables():
    half = DB // 2
    freqs = np.power(np.float32(10000.0), -np.arange(half, dtype=np.float32) / np.float32(half)).astype(np.float32)
    radians = np.arange(T, dtype=np.float32)[None, :] * freqs[:, None]
    cos, sin = np.cos(radians), np.sin(radians)
    return (np.concatenate([cos, cos]).astype(np.float32), np.concatenate([-sin, sin]).astype(np.float32))


_INS = ['L0_attn_a_x', 'L0_attn_a_adaptive_scale', 'L0_attn_a_Wq', 'L0_attn_a_bq', 'L0_attn_a_Wk', 'L0_attn_a_bk',
        'L0_attn_a_Wv', 'L0_attn_a_bv', 'L0_attn_a_Wo', 'L0_attn_a_bo', 'L0_attn_a_gamma', 'L0_attn_a_beta',
        'L0_attn_b_w_aq', 'L0_attn_b_w_ak', 'L0_attn_b_w_av', 'L0_attn_b_w_ao', 'L0_ffn_W1', 'L0_ffn_b1',
        'L0_ffn_W2', 'L0_ffn_b2']


def kernel(**inputs):
    import concourse.bacc as bacc
    from concourse.bass_utils import run_bass_kernel_spmd

    nc = bacc.Bacc("TRN2", target_bir_lowering=False, num_devices=1)
    cos, sin = rope_tables()
    arrays, args = {}, []
    for name, a in [*((n, inputs[n]) for n in _INS), ("rope_cos", cos), ("rope_sin", sin)]:
        a = np.ascontiguousarray(a)
        arrays[f"in_{name}"] = a
        args.append(nc.dram_tensor(f"in_{name}", a.shape, mybir.dt.from_np(a.dtype), kind="ExternalInput").ap())
    args.append(nc.dram_tensor("out_0", (1, T, D), F32, kind="ExternalOutput").ap())
    build(nc, *args)
    r = run_bass_kernel_spmd(nc, [arrays], core_ids=[0])
    return r.results[0]["out_0"]
```
